# Optimizing a Trainium2 kernel written in Bass

```python
import numpy as np
import jax
import jax.numpy as jnp

def _softmax(x, axis=-1):
    return jax.nn.softmax(x, axis=axis)

def _gelu(x):
    return jax.nn.gelu(x, approximate=True)

def _silu(x):
    return jax.nn.silu(x)

def _sigmoid(x):
    return jax.nn.sigmoid(x)

def _layernorm(x, axis=-1, eps=1e-05):
    m = jnp.mean(x, axis=axis, keepdims=True)
    v = jnp.var(x, axis=axis, keepdims=True)
    return (x - m) / jnp.sqrt(v + eps)

def _scatter_add(tgt, idx, src, axis=0):
    return tgt.at[idx].add(src)

def _segment_sum(src, seg, n):
    return jax.ops.segment_sum(src, seg, n)
kernel_name = 'mk_adaln_d1_jaxref_r8_9987db'

def setup_inputs(seed: int=0):
    np.random.seed(seed)
    _w = jnp.asarray

    def _L0_attn_setup():
        import jax, jax.numpy as jnp
        import numpy as np
        B, S, D = (2, 256, 128)
        H, DH = (16, 64)
        DQL, DKVL = (64, 64)
        DR = 64
        TOPK = 64
        LN_EPS = 1e-05
        ROPE_BASE = 10000.0

        def _rope_tables(seq_len, dim):
            inv_freq = 1.0 / ROPE_BASE ** (np.arange(0, dim, 2, dtype=np.float32) / dim)
            t = np.arange(seq_len, dtype=np.float32)
            freqs = np.outer(t, inv_freq)
            cos = np.concatenate([np.cos(freqs), np.cos(freqs)], -1)[:, ::2]
            sin = np.concatenate([np.sin(freqs), np.sin(freqs)], -1)[:, ::2]
            return (jnp.asarray(cos), jnp.asarray(sin))

        def _apply_rope_subspace(x, d_rope):
            s = x.shape[-2]
            cos, sin = _rope_tables(s, d_rope)
            xr, xp = (x[..., :d_rope], x[..., d_rope:])
            e, o = (xr[..., 0::2], xr[..., 1::2])
            rot = jnp.stack([e * cos - o * sin, e * sin + o * cos], axis=-1).reshape(xr.shape)
            return jnp.concatenate([rot, xp], axis=-1)

        def _reference_tuple_inner(x, w_down_q, w_down_kv, w_up_q, w_up_k, w_up_v, w_out, ln_scale, ln_bias):
            b, s, d = x.shape
            residual = x
            mu = jnp.mean(x, axis=-1, keepdims=True)
            var = jnp.mean((x - mu) ** 2, axis=-1, keepdims=True)
            h = (x - mu) * jax.lax.rsqrt(var + LN_EPS) * ln_scale + ln_bias
            c_q = h @ w_down_q.T
            c_kv = h @ w_down_kv.T
            q = (c_q @ w_up_q.T).reshape(b, s, H, DH).transpose(0, 2, 1, 3)
            k = (c_kv @ w_up_k.T).reshape(b, s, H, DH).transpose(0, 2, 1, 3)
            v = (c_kv @ w_up_v.T).reshape(b, s, H, DH).transpose(0, 2, 1, 3)
            q = _apply_rope_subspace(q, DR)
            k = _apply_rope_subspace(k, DR)
            scale = 1.0 / np.sqrt(DH).astype(np.float32)
            scores = jnp.einsum('bhqd,bhkd->bhqk', q, k) * scale
            _, indices = jax.lax.top_k(scores, min(TOPK, s))
            attn = jax.nn.softmax(scores, axis=-1)
            out = jnp.einsum('bhqk,bhkd->bhqd', attn, v)
            out = out.transpose(0, 2, 1, 3).reshape(b, s, H * DH)
            out = out @ w_out.T + residual
            return (out, indices.astype(jnp.int64))
        key = jax.random.key(seed)
        ks = jax.random.split(key, 7)
        init = lambda k, shape: jax.random.normal(k, shape, jnp.float32) * 0.02
        return {'x': jax.random.normal(ks[0], (B, S, D), jnp.float32), 'w_down_q': init(ks[1], (DQL, D)), 'w_down_kv': init(ks[2], (DKVL, D)), 'w_up_q': init(ks[3], (H * DH, DQL)), 'w_up_k': init(ks[4], (H * DH, DKVL)), 'w_up_v': init(ks[5], (H * DH, DKVL)), 'w_out': init(ks[6], (D, H * DH)), 'ln_scale': jnp.ones((D,), jnp.float32), 'ln_bias': jnp.zeros((D,), jnp.float32)}
    _L0_attn_in = _L0_attn_setup()

    def _L0_ffn_setup():
        import jax, jax.numpy as jnp
        import numpy as np
        B, S, D, E, K = (4, 256, 128, 8, 2)
        H = 4 * D
        key = jax.random.key(seed)
        ks = jax.random.split(key, 4)
        sc = lambda n: 1.0 / np.sqrt(n)
        return {'x': jax.random.normal(ks[0], (B, S, D), jnp.float32), 'gate_w': jax.random.normal(ks[1], (D, E), jnp.float32) * sc(D), 'gate_b': jnp.zeros((E,), jnp.float32), 'w1': jax.random.normal(ks[2], (E, D, H), jnp.float32) * sc(D), 'b1': jnp.zeros((E, H), jnp.float32), 'w2': jax.random.normal(ks[3], (E, H, D), jnp.float32) * sc(H), 'b2': jnp.zeros((E, D), jnp.float32)}
    _L0_ffn_in = _L0_ffn_setup()
    _L0_c = _w((lambda *s: np.random.randn(*s).astype(np.float32) * 0.05)(2, 128))
    _L0_wmod = _w((lambda *s: np.random.randn(*s).astype(np.float32) * 0.05)(128, 6 * 128) * 128 ** (-0.5))
    _d = {'L0_attn_x': _L0_attn_in['x'], 'L0_attn_w_down_q': _L0_attn_in['w_down_q'], 'L0_attn_w_down_kv': _L0_attn_in['w_down_kv'], 'L0_attn_w_up_q': _L0_attn_in['w_up_q'], 'L0_attn_w_up_k': _L0_attn_in['w_up_k'], 'L0_attn_w_up_v': _L0_attn_in['w_up_v'], 'L0_attn_w_out': _L0_attn_in['w_out'], 'L0_attn_ln_scale': _L0_attn_in['ln_scale'], 'L0_attn_ln_bias': _L0_attn_in['ln_bias'], 'L0_ffn_gate_w': _L0_ffn_in['gate_w'], 'L0_ffn_gate_b': _L0_ffn_in['gate_b'], 'L0_ffn_w1': _L0_ffn_in['w1'], 'L0_ffn_b1': _L0_ffn_in['b1'], 'L0_ffn_w2': _L0_ffn_in['w2'], 'L0_ffn_b2': _L0_ffn_in['b2'], 'L0_c': _L0_c, 'L0_wmod': _L0_wmod}
    _x0 = _d['L0_attn_x']
    _d['L0_attn_x'] = jax.random.normal(jax.random.fold_in(jax.random.key(seed), 1), (2, 1024, 128), dtype=_x0.dtype)
    del _x0
    return _d

def reference(L0_attn_x, L0_attn_w_down_q, L0_attn_w_down_kv, L0_attn_w_up_q, L0_attn_w_up_k, L0_attn_w_up_v, L0_attn_w_out, L0_attn_ln_scale, L0_attn_ln_bias, L0_ffn_gate_w, L0_ffn_gate_b, L0_ffn_w1, L0_ffn_b1, L0_ffn_w2, L0_ffn_b2, L0_c, L0_wmod):

    def _L0_attn_ref(x, w_down_q, w_down_kv, w_up_q, w_up_k, w_up_v, w_out, ln_scale, ln_bias):
        import jax, jax.numpy as jnp
        import numpy as np
        B, S, D = (2, 256, 128)
        H, DH = (16, 64)
        DQL, DKVL = (64, 64)
        DR = 64
        TOPK = 64
        LN_EPS = 1e-05
        ROPE_BASE = 10000.0

        def _rope_tables(seq_len, dim):
            inv_freq = 1.0 / ROPE_BASE ** (np.arange(0, dim, 2, dtype=np.float32) / dim)
            t = np.arange(seq_len, dtype=np.float32)
            freqs = np.outer(t, inv_freq)
            cos = np.concatenate([np.cos(freqs), np.cos(freqs)], -1)[:, ::2]
            sin = np.concatenate([np.sin(freqs), np.sin(freqs)], -1)[:, ::2]
            return (jnp.asarray(cos), jnp.asarray(sin))

        def _apply_rope_subspace(x, d_rope):
            s = x.shape[-2]
            cos, sin = _rope_tables(s, d_rope)
            xr, xp = (x[..., :d_rope], x[..., d_rope:])
            e, o = (xr[..., 0::2], xr[..., 1::2])
            rot = jnp.stack([e * cos - o * sin, e * sin + o * cos], axis=-1).reshape(xr.shape)
            return jnp.concatenate([rot, xp], axis=-1)

        def _reference_tuple_inner(x, w_down_q, w_down_kv, w_up_q, w_up_k, w_up_v, w_out, ln_scale, ln_bias):
            b, s, d = x.shape
            residual = x
            mu = jnp.mean(x, axis=-1, keepdims=True)
            var = jnp.mean((x - mu) ** 2, axis=-1, keepdims=True)
            h = (x - mu) * jax.lax.rsqrt(var + LN_EPS) * ln_scale + ln_bias
            c_q = h @ w_down_q.T
            c_kv = h @ w_down_kv.T
            q = (c_q @ w_up_q.T).reshape(b, s, H, DH).transpose(0, 2, 1, 3)
            k = (c_kv @ w_up_k.T).reshape(b, s, H, DH).transpose(0, 2, 1, 3)
            v = (c_kv @ w_up_v.T).reshape(b, s, H, DH).transpose(0, 2, 1, 3)
            q = _apply_rope_subspace(q, DR)
            k = _apply_rope_subspace(k, DR)
            scale = 1.0 / np.sqrt(DH).astype(np.float32)
            scores = jnp.einsum('bhqd,bhkd->bhqk', q, k) * scale
            _, indices = jax.lax.top_k(scores, min(TOPK, s))
            attn = jax.nn.softmax(scores, axis=-1)
            out = jnp.einsum('bhqk,bhkd->bhqd', attn, v)
            out = out.transpose(0, 2, 1, 3).reshape(b, s, H * DH)
            out = out @ w_out.T + residual
            return (out, indices.astype(jnp.int64))
        return _reference_tuple_inner(x, w_down_q, w_down_kv, w_up_q, w_up_k, w_up_v, w_out, ln_scale, ln_bias)[0]

    def _L0_ffn_ref(x, gate_w, gate_b, w1, b1, w2, b2):
        import jax, jax.numpy as jnp
        import numpy as np
        B, S, D, E, K = (4, 256, 128, 8, 2)
        H = 4 * D
        Bx, Sx, Dx = x.shape
        n_exp = w1.shape[0]
        logits = jnp.einsum('bsd,de->bse', x, gate_w) + gate_b
        scores = jax.nn.softmax(logits, axis=-1)
        topk_s, topk_i = jax.lax.top_k(scores, K)
        onehot = jax.nn.one_hot(topk_i, n_exp, dtype=scores.dtype)
        dispatch = jnp.einsum('bske,bsk->bse', onehot, topk_s)
        xf = x.reshape(-1, Dx)
        wf = dispatch.reshape(-1, n_exp)
        out = jnp.zeros_like(xf)
        for i in range(n_exp):
            wi = wf[:, i:i + 1]
            h = jax.nn.relu(xf * wi @ w1[i] + b1[i])
            y = h @ w2[i] + b2[i]
            out = jnp.where(wi > 0, y, out)
        return out.reshape(Bx, Sx, Dx)
    x = L0_attn_x
    mod = (_silu(L0_c) @ L0_wmod).reshape(L0_c.shape[0], 6, 1, -1)
    sa, ca, ga, sb, cb, gb = (mod[:, 0], mod[:, 1], mod[:, 2], mod[:, 3], mod[:, 4], mod[:, 5])
    ga = (2 * (ga >= 0) - 1) * jnp.maximum(jnp.abs(ga), 0.25)
    gb = (2 * (gb >= 0) - 1) * jnp.maximum(jnp.abs(gb), 0.25)
    h = _layernorm(x, axis=-1) * (1 + ca) + sa
    x = x + ga * _L0_attn_ref(h, L0_attn_w_down_q, L0_attn_w_down_kv, L0_attn_w_up_q, L0_attn_w_up_k, L0_attn_w_up_v, L0_attn_w_out, L0_attn_ln_scale, L0_attn_ln_bias)
    h = _layernorm(x, axis=-1) * (1 + cb) + sb
    x = x + gb * _L0_ffn_ref(h, L0_ffn_gate_w, L0_ffn_gate_b, L0_ffn_w1, L0_ffn_b1, L0_ffn_w2, L0_ffn_b2)
    return x

_drawn_inputs = setup_inputs


def setup_inputs(seed=0):
    import zlib

    import numpy as np

    out = dict(_drawn_inputs(seed))
    spreads = {'L0_attn_ln_scale': (1.0, 0.6),
     'L0_attn_ln_bias': (0.0, 0.8),
     'L0_ffn_gate_b': (0.0, 1.357),
     'L0_ffn_b1': (0.0, 2.0),
     'L0_ffn_b2': (0.0, 1.468)}
    factors = {'L0_attn_w_down_q': 8.0,
     'L0_attn_w_down_kv': 8.0,
     'L0_attn_w_up_q': 8.0,
     'L0_attn_w_up_k': 8.0,
     'L0_attn_w_up_v': 8.0,
     'L0_attn_w_out': 8.0,
     'L0_ffn_w1': 4.825}
    for name, (base, spread) in spreads.items():
        noise = np.random.default_rng([zlib.crc32(name.encode()), seed]).standard_normal(out[name].shape)
        drawn = base * np.exp(spread * noise) if base else spread * noise
        out[name] = jnp.asarray(drawn.astype(out[name].dtype))
    for name, factor in factors.items():
        out[name] = (out[name] * factor).astype(out[name].dtype)
    return out
```

```python
from contextlib import ExitStack

import numpy as np

import concourse.bass as bass
from concourse import mybir

ALU = mybir.AluOpType
ACT = mybir.ActivationFunctionType
AX = mybir.AxisListType
F32 = mybir.dt.float32
F32R = mybir.dt.float32r
I32 = mybir.dt.int32

P = 128
B, S, D = 2, 1024, 128
H, DH, LAT = 16, 64, 64
NT = B * S // P
TB = S // P
HP = H // 2
NPAIR = B * HP
HALF = 512
NSTEP = 2 * TB
E, F = 8, 512
NSL = 24
EPS = 1e-5
SCALE = 0.125


def ge(eng, sem, value):
    if not (isinstance(value, int) and value <= 0):
        eng.wait_ge(sem, value)


def ge_all(eng, *waits):
    for _, v in waits:
        if not isinstance(v, int):
            eng.compute_val(v)
    for sem, v in waits:
        ge(eng, sem, v)


def build(nc, t, out, dbg=None):
    ctx = ExitStack()
    with ctx:
        def sb(name, shape, dt=F32):
            return ctx.enter_context(nc.sbuf_tensor(name, shape, dt))

        def pb(name, shape=(P, HALF), dt=F32):
            return ctx.enter_context(nc.psum_tensor(name, list(shape), dt))

        def sem(name):
            return ctx.enter_context(nc.semaphore(name))

        x_sb = sb("x_sb", [P, NT, D])
        h0 = sb("h0", [P, NT, D])
        hn = sb("hn", [P, NT, D])
        hT = sb("hT", [P, B * S])
        cT = sb("cT", [P, B * S])
        c_all = sb("c_all", [P, NT, LAT])
        ident = sb("ident", [P, P])
        ones = sb("ones", [P, 32])
        wmod_sb = sb("wmod_sb", [P, 6 * D])
        wd_sb = sb("wd_sb", [P, 2 * LAT])
        c_col = sb("c_col", [P, B])
        c_e = sb("c_e", [P, 3, B])
        c_rep = sb("c_rep", [P, B, P])
        mod = sb("mod", [P, B, 6, D])
        g_tmp = sb("g_tmp", [P, B, 2, D])
        g_abs = sb("g_abs", [P, B, 2, D])
        lns = sb("lns", [P, 2])
        bst = sb("bst", [P, NT, 6])
        mv = sb("mv", [P, NT, 2])
        sd = sb("sd", [P, 2, NT])
        g_all = sb("g_all", [P, HP, D])
        cos_sb = sb("cos_sb", [P, S])
        sin_sb = sb("sin_sb", [P, S])

        wqk = sb("wqk", [P, 2, P])
        us = sb("us", [P, 2, S])
        vs = sb("vs", [P, 2, S])
        xh = sb("xh", [P, 2, S], F32R)
        qq = sb("qq", [P, 2, 2, S], F32R)
        kk = sb("kk", [P, 2, 2, S], F32R)
        q2 = sb("q2", [P, 2, 2, S], F32R)
        k2 = sb("k2", [P, 2, 2, S], F32R)
        cv = sb("cv", [P, 2, TB, LAT])
        probs = sb("probs", [P, 4, 2, HALF])
        acc = sb("acc", [P, 2, 2, HALF])
        mx = sb("mx", [P, 2, 2, TB])
        nm = sb("nm", [P, 2, TB], F32R)
        den = sb("den", [64, HALF])
        denc = sb("denc", [P, 2, 2, 4])
        rc = sb("rc", [P, 2, 2, 4])
        rr = sb("rr", [P, 2, HALF])
        ou = sb("ou", [P, 2, HALF])

        rd_dram = nc.dram_tensor("rd_dram", [2, 2, HALF], F32, kind="Internal").ap()
        o_dram = nc.dram_tensor("o_dram", [NPAIR, P, S], F32, kind="Internal").ap()

        wuv_sb = us[0:64, 0, :].rearrange("p (h l) -> p h l", h=H)
        wo_sb = vs[0:64, :, :].rearrange("p a n -> p (a n)").rearrange("p (h d) -> p h d", h=H)
        on = [x[:].bitcast(F32).rearrange("p a h n -> p (a h n)").rearrange("p (j n) -> p j n", j=HP) for x in (qq, kk)]
        xs = q2[:].bitcast(F32).rearrange("p a h n -> p (a h n)")[:, 0:NSL * D].rearrange("p (t d) -> p t d", d=D)
        aT = cT[:, 0:2 * HALF].rearrange("p (a n) -> p a n", a=2)
        h2, h2T, xw = hn, hT, h0
        w1_sb = [probs[:, n, 0, :] for n in range(4)]
        w2_sb = [probs[:, n, 1, :] for n in range(4)]
        hid = [acc[:, n, 0, :] for n in range(2)]
        xT = [acc[:, n, 1, 0:D] for n in range(2)]
        ys = us[:, 0, 0:4 * D].rearrange("p (n d) -> p n d", n=4)
        b2_sb = us[:, 1, 0:4 * D].rearrange("p (n d) -> p n d", n=4)
        yg = vs[:].rearrange("p a n -> p (a n)").rearrange("p (t d) -> p t d", d=D)
        gw_sb = sb("gw_sb", [P, E])
        gb_sb = sb("gb_sb", [P, E])
        b1_sb = sb("b1_sb", [P, 4, 4])
        zero = sb("zero", [P, D])
        tri = sb("tri", [P, P])
        ones_sq = sb("ones_sq", [P, P])
        rev = sb("rev", [P, E])
        thr = sb("thr", [P, NT])
        tix = sb("tix", [P, NSL])
        lg = sb("lg", [P, NT, E])
        rt = vs[:].rearrange("p a n -> p (a n)")[:, 0:12 * NT * E].rearrange("p (a t e) -> p a t e", a=12, e=E)
        rs = sb("rs", [P, 12, NT])
        cn = sb("cn", [P, 12, E])
        cmp3 = sb("cmp3", [P, E, NSL])
        slot = sb("slot", [P, NT], I32)
        eid = sb("eid", [P, NSL], I32)
        wsel = rs[:, 10, :]
        tcount = sb("tcount", [P, NSL])

        xs_dram = nc.dram_tensor("xs_dram", [NSL * P, D], F32, kind="Internal").ap()
        ys_dram = nc.dram_tensor("ys_dram", [NSL * P, D], F32, kind="Internal").ap()

        ps_s = [pb(f"ps_s{n}") for n in range(4)]
        ps_m = [pb(f"ps_m{n}") for n in range(2)]
        ps_o = pb("ps_o")
        ps_x = pb("ps_x")

        names = ("init modps modsb silu crep bst mvr std rstd xn h0r hnx trp tre cps cev lps lev c "
                 "dve pool scores exp pv add maxps maxr nm u uev den denev rcp mul oev rope gps gev yps yev ytp ybk h2x h2tp h2te lgp lgx ex2 pre rtd cnt xwx sc ga xtp xte hps hev_a hev_d yo yoe fin"
                 ).split()
        s = {n: sem("s_" + n) for n in names}
        d_in, d_in2, d_in3 = sem("d_in"), sem("d_in2"), sem("d_in3")
        d_w = sem("d_w")
        d_cv = sem("d_cv")
        d_swap = [sem("d_swap0"), sem("d_swap1")]
        d_pq = [sem("d_pq0"), sem("d_pq1")]
        d_p2 = [sem("d_p20"), sem("d_p21")]
        d_m = [sem("d_m0"), sem("d_m1")]
        d_d1 = sem("d_d1")
        d_d2 = sem("d_d2")
        d_d3 = sem("d_d3")
        d_sp = [sem("d_sp0"), sem("d_sp1")]
        d_dbg = sem("d_dbg")
        d_vo, d_gw, d_zero, d_xs, d_yg, d_out = [sem(n) for n in ("d_vo", "d_gw", "d_zero", "d_xs", "d_yg", "d_out")]
        d_on = [sem(f"d_on{n}") for n in range(2)]
        d_sc = sem("d_sc")
        d_wp = [sem(f"d_wp{n}") for n in range(4)]
        d_ys = [sem(f"d_ys{n}") for n in range(4)]

        block = ctx.enter_context(nc.Block())

        def n_score(p, st, h):
            return 32 * p + 2 * st + h + 1

        def n_add(p, st, h):
            half, kt = divmod(st, TB)
            return 28 * p + 14 * half + 2 * (max(kt, 1) - 1) + h + 1

        def step_before(p, st, n):
            st -= n
            if st < 0:
                p, st = p - 1, st + NSTEP
            return None if isinstance(p, int) and p < 0 else (p, st)

        def pairs(eng, body):
            body(0, 0)
            with eng.Fori(1, NPAIR - 3, 2) as p:
                body(p, 1)
                body(p + 1, 0)
            for q in range(NPAIR - 3, NPAIR):
                body(q, q % 2)

        def last(p):
            return isinstance(p, int) and p >= NPAIR - 1

        def last2(p):
            return isinstance(p, int) and p >= NPAIR - 2

        MAXN = [0, 0, 0, 2, 3, 3, 3, 3, 3, 3, 3, 3, 3, 3, 0, 0]

        UP_STEPS = (6, 7, 8, 9)

        @block.tensor
        def _(pe):
            pe.wait_ge(s["crep"], 1)
            pe.wait_ge(d_in3, 80)
            for b in range(B):
                for n in range(2):
                    nc.tensor.matmul(ps_s[2 * b + n][:, 0:3 * D], c_rep[:, b, :], wmod_sb[:, n * 3 * D:(n + 1) * 3 * D],
                                     start=True, stop=True).then_inc(s["modps"], 1)
            pe.wait_ge(d_vo, 32)
            for n in range(2):
                for j in range(4):
                    for h in range(2):
                        head = 2 * (4 * n + j) + h
                        ins = nc.tensor.matmul(ps_m[n][64 * h:64 * h + 64, j * P:(j + 1) * P], wuv_sb[:, head, :],
                                               wo_sb[:, head, :], start=True, stop=True)
                ins.then_inc(s["gps"], 1)
            pe.wait_ge(s["init"], 1)
            for g in range(NT // 4):
                pe.wait_ge(s["hnx"], 4 * g + 4)
                if g < 4:
                    pe.wait_ge(s["modsb"], 4)
                for n in range(4):
                    ins = nc.tensor.transpose(ps_s[g % 4][:, n * P:(n + 1) * P], hn[:, 4 * g + n, :], ident[:])
                ins.then_inc(s["trp"], 1)
            for g in range(4):
                pe.wait_ge(s["tre"], g + 1)
                nc.tensor.matmul(ps_s[g][:], wd_sb[:], hT[:, g * HALF:(g + 1) * HALF],
                                 start=True, stop=True).then_inc(s["cps"], 1)
            pe.wait_ge(s["gev"], 2)
            for g in range(2):
                for n in range(8):
                    k = 8 * g + n
                    ins = nc.tensor.matmul(ps_m[g][:, n * LAT:(n + 1) * LAT], hT[:, k * P:(k + 1) * P],
                                           wd_sb[:, LAT:2 * LAT], start=True, stop=True)
                ins.then_inc(s["lps"], 1)

            def up(q, j):
                h, half = divmod(j, 2)
                if j == 0:
                    ge(pe, s["denev"], 2 * q - 4)
                ge(pe, s["uev"], 4 * q + j)
                if j == 0:
                    pe.wait_ge(d_w, 64 * (q + 1))
                nc.tensor.matmul(ps_x[:], wqk[:, h, :], cT[:, bass.ds((q // HP) * S + half * HALF, HALF)],
                                 start=True, stop=True).then_inc(s["u"], 1)

            def maxima(q, par, n):
                h, r = divmod(n, 16)
                qt, kh = divmod(r, 2)
                if r == 0:
                    pe.wait_ge(d_pq[h], 64 * (q + 1))
                ge(pe, s["maxr"], 32 * q + n - 1)
                qs = qq[:, par, h, :].rearrange("p (m t) -> p t m", t=TB)
                nc.tensor.matmul(ps_m[n % 2][:], qs[:, qt, :], kk[:, par, h, kh * HALF:(kh + 1) * HALF],
                                 start=True, stop=True).then_inc(s["maxps"], 1)

            def score(p, par, st, h):
                half, kt = divmod(st, TB)
                if st == 0:
                    pe.wait_ge(d_p2[h], 32 * (p + 1))
                before = step_before(p, st, 2)
                if before:
                    ge(pe, s["exp"], n_score(*before, h))
                bank = ps_s[2 * (st % 2) + h]
                nc.tensor.matmul(bank[:], kk[:, par, h, kt * P:(kt + 1) * P], qq[:, par, h, half * HALF:(half + 1) * HALF],
                                 start=True, stop=False)
                if st == 0:
                    pe.wait_ge(d_m[h], 16 * (p + 1))
                nc.tensor.matmul(bank[:], k2[0:65, par, h, kt * P:(kt + 1) * P], q2[0:65, par, h, half * HALF:(half + 1) * HALF],
                                 start=False, stop=True).then_inc(s["scores"], 1)

            def pv(p, par, st):
                half, kt = divmod(st, TB)
                if st == 0:
                    pe.wait_ge(d_cv, 16 * (p + 1))
                if kt == 0:
                    ge(pe, s["oev"], 2 * p + half)
                for h in range(2):
                    pe.wait_ge(s["exp"], n_score(p, st, h))
                    ins = nc.tensor.matmul(ps_o[64 * h:64 * h + 64, :], cv[:, par, kt, :], probs[:, st % 4, h, :],
                                           start=(kt == 0), stop=(kt == TB - 1))
                ins.then_inc(s["pv"], 1)

            def denominators(p, half):
                pe.wait_ge(s["add"], n_add(p, TB * half + TB - 1, 1))
                for h in range(2):
                    ins = nc.tensor.matmul(ps_x[32 * h:32 * h + 32, :], ones[:], acc[:, half, h, :], start=True, stop=True)
                ins.then_inc(s["den"], 1)

            for j in range(4):
                if j == 0:
                    pe.wait_ge(s["cev"], 4)
                up(0, j)
            for n in range(32):
                maxima(0, 0, n)
            for j in range(4):
                up(1, j)

            def pair(p, par):
                first = isinstance(p, int) and p == 0
                for st in range(NSTEP):
                    todo = [] if last(p) else list(range(sum(MAXN[:st]), sum(MAXN[:st + 1])))
                    score(p, par, st, 0)
                    for n in todo[:1]:
                        maxima(p + 1, 1 - par, n)
                    score(p, par, st, 1)
                    for n in todo[1:2]:
                        maxima(p + 1, 1 - par, n)
                    if st > 0:
                        pv(p, par, st - 1)
                    elif not first:
                        pv(p - 1, 1 - par, NSTEP - 1)
                    for n in todo[2:]:
                        maxima(p + 1, 1 - par, n)
                    if st == 2 and not first:
                        ge(pe, s["denev"], 2 * p - 1)
                        denominators(p - 1, 1)
                    if st in UP_STEPS and not last2(p):
                        up(p + 2, st - UP_STEPS[0])
                    if st == 10:
                        if last2(p):
                            pe.wait_ge(s["denev"], 2 * p)
                        else:
                            pe.wait_ge(s["uev"], 4 * (p + 3))
                        denominators(p, 0)

            pairs(pe, pair)
            pv(NPAIR - 1, 1, NSTEP - 1)
            pe.wait_ge(s["denev"], 2 * NPAIR - 1)
            denominators(NPAIR - 1, 1)

            def project(g):
                pe.wait_ge(d_on[g % 2], 16 * (g // 2 + 1))
                for j in range(HP):
                    ins = nc.tensor.matmul(ps_s[g % 2][:], g_all[:, j, :], on[g % 2][:, j, :],
                                           start=(j == 0), stop=(j == HP - 1))
                ins.then_inc(s["yps"], 1)

            def attn_back(g):
                pe.wait_ge(s["yev"], g + 1)
                if g >= 2:
                    pe.wait_ge(s["ybk"], g - 1)
                for n in range(4):
                    ins = nc.tensor.transpose(ps_s[2 + g % 2][:, n * P:(n + 1) * P], aT[:, g % 2, n * P:(n + 1) * P], ident[:])
                ins.then_inc(s["ytp"], 1)

            def logits(g):
                pe.wait_ge(s["h2x"], g + 1)
                if g >= 2:
                    pe.wait_ge(s["h2te"], g - 1)
                for n in range(4):
                    ins = nc.tensor.transpose(ps_m[g % 2][:, n * P:(n + 1) * P], h2[:, 4 * g + n, :], ident[:])
                ins.then_inc(s["h2tp"], 1)
                pe.wait_ge(s["h2te"], g + 1)
                for n in range(4):
                    k = 4 * g + n
                    ins = nc.tensor.matmul(ps_o[:, k * E:(k + 1) * E], h2T[:, k * P:(k + 1) * P], gw_sb[:],
                                           start=True, stop=True)
                ins.then_inc(s["lgp"], 1)

            pe.wait_ge(s["oev"], 2 * NPAIR)
            for g in range(5):
                if g < 4:
                    project(g)
                    attn_back(g)
                if g >= 1:
                    logits(g - 1)

            pe.wait_ge(s["cnt"], 1)
            nc.tensor.matmul(ps_x[:, 0:E], tri[:], cn[:, 0, :], start=True, stop=True)
            nc.tensor.matmul(ps_x[:, E:2 * E], ones_sq[:], cn[:, 0, :], start=True, stop=True).then_inc(s["pre"], 1)

            def slots_T(k, n):
                ge(pe, s["xte"], k - 1)
                nc.tensor.transpose(ps_m[n % 2][:, 0:P], xs[:, k, :], ident[:]).then_inc(s["xtp"], 1)

            pe.wait_ge(d_xs, 16)

            def up_e(k, n):
                pe.wait_ge(s["xte"], k + 1)
                pe.wait_ge(d_wp[n], 12 * (k - n) + 48)
                ge(pe, s["hev_a"], k - 1)
                ge(pe, s["hev_d"], k - 1)
                for c in range(4):
                    ins = nc.tensor.matmul(ps_s[n % 2 + (c & 2)][:, c * P:(c + 1) * P], w1_sb[n][:, c * P:(c + 1) * P], xT[n % 2],
                                           start=True, stop=True)
                ins.then_inc(s["hps"], 1)

            def down_e(k, n):
                pe.wait_ge(s["hev_a"], k + 1)
                pe.wait_ge(s["hev_d"], k + 1)
                ge(pe, s["yoe"], k - 1)
                for c in range(4):
                    ins = nc.tensor.matmul((ps_o, ps_x)[n % 2][:, 0:D], hid[n % 2][:, c * P:(c + 1) * P],
                                           w2_sb[n][:, c * P:(c + 1) * P], start=(c == 0), stop=(c == 3))
                ins.then_inc(s["yo"], 1)

            for k in range(NSL + 1):
                if k < NSL:
                    slots_T(k, k % 4)
                    up_e(k, k % 4)
                if k:
                    down_e(k - 1, (k - 1) % 4)

        @block.scalar
        def _(act):
            act.wait_ge(d_in, 16)
            nc.scalar.activation(c_e[:, 0, :], c_col[:], ACT.Exp, scale=-1.0).then_inc(s["silu"], 1)
            for n in range(4):
                act.wait_ge(s["modps"], n + 1)
                dst = mod[:, n // 2, 3 * (n % 2):3 * (n % 2) + 3, :].rearrange("p a d -> p (a d)")
                nc.scalar.copy(dst, ps_s[n][:, 0:3 * D]).then_inc(s["modsb"], 1)
            for n in range(2):
                act.wait_ge(s["gps"], n + 1)
                nc.scalar.copy(g_all[:, 4 * n:4 * n + 4, :].rearrange("p j d -> p (j d)"), ps_m[n][:]).then_inc(s["gev"], 1)
            for r in range(2):
                act.wait_ge(s["std"], r + 1)
                nc.scalar.activation(sd[:, 1, :], sd[:, 0, :], ACT.Sqrt).then_inc(s["rstd"], 1)
            act.wait_ge(d_in3, 80)
            for g in range(4):
                act.wait_ge(s["trp"], g + 1)
                nc.scalar.activation(hT[:, g * HALF:(g + 1) * HALF], ps_s[g % 4][:], ACT.Identity,
                                     bias=lns[:, 1:2], scale=lns[:, 0:1]).then_inc(s["tre"], 1)
            for g in range(4):
                act.wait_ge(s["cps"], g + 1)
                nc.scalar.copy(cT[:, g * HALF:(g + 1) * HALF], ps_s[g][:]).then_inc(s["cev"], 1)

            def up_out(q, j):
                h, half = divmod(j, 2)
                act.wait_ge(s["u"], 4 * q + j + 1)
                if half == 0:
                    ge(act, d_swap[h], 64 * q)
                    ge(act, s["rope"], 10 * (2 * q - 2 + h) + 10)
                nc.scalar.copy(us[:, h, half * HALF:(half + 1) * HALF], ps_x[:]).then_inc(s["uev"], 1)

            def expo(p, st, h):
                act.wait_ge(s["scores"], n_score(p, st, h))
                before = step_before(p, st, 4)
                if before:
                    bp, bst_ = before
                    if h == 0:
                        act.wait_ge(s["pv"], 16 * bp + bst_ + 1)
                    act.wait_ge(s["add"], n_add(bp, bst_, h))
                nc.scalar.activation(probs[:, st % 4, h, :], ps_s[2 * (st % 2) + h][:], ACT.Exp,
                                     scale=SCALE).then_inc(s["exp"], 1)

            def o_out(p, half):
                act.wait_ge(s["pv"], 16 * p + 8 * half + 8)
                ge(act, d_sp[half], 16 * p)
                nc.scalar.copy(ou[:, half, :], ps_o[:]).then_inc(s["oev"], 1)

            act.wait_ge(s["gps"], 2)
            for q in range(2):
                for j in range(4):
                    up_out(q, j)

            def pair(p, par):
                for st in range(NSTEP):
                    expo(p, st, 0)
                    expo(p, st, 1)
                    if st == 0 and not (isinstance(p, int) and p == 0):
                        o_out(p - 1, 1)
                    if st == 8:
                        o_out(p, 0)
                    if st in UP_STEPS and not last2(p):
                        up_out(p + 2, st - UP_STEPS[0])

            pairs(act, pair)
            o_out(NPAIR - 1, 1)

            for g in range(-1, 4):
                if g < 3:
                    n = g + 1
                    act.wait_ge(s["yps"], n + 1)
                    if n >= 2:
                        act.wait_ge(s["ytp"], n - 1)
                    nc.scalar.copy(aT[:, n % 2, :], ps_s[n % 2][:]).then_inc(s["yev"], 1)
                if g >= 0:
                    act.wait_ge(s["std"], 3 + g)
                    nc.scalar.activation(sd[:, 1, 4 * g:4 * g + 4], sd[:, 0, 4 * g:4 * g + 4], ACT.Sqrt).then_inc(s["rstd"], 1)
                    act.wait_ge(s["h2tp"], g + 1)
                    nc.scalar.copy(h2T[:, g * HALF:(g + 1) * HALF], ps_m[g % 2][:]).then_inc(s["h2te"], 1)
            act.wait_ge(s["lgx"], 1)
            nc.scalar.activation(rt[:, 1, :, :], rt[:, 0, :, :], ACT.Exp).then_inc(s["ex2"], 1)

            for k in range(NSL):
                n = k % 4
                act.wait_ge(s["xtp"], k + 1)
                ge(act, s["hps"], k - 1)
                nc.scalar.copy(xT[n % 2], ps_m[n % 2][:, 0:P]).then_inc(s["xte"], 1)
                act.wait_ge(s["hps"], k + 1)
                ge(act, s["yo"], k - 1)
                for c in range(2):
                    ins = nc.scalar.activation(hid[n % 2][:, c * P:(c + 1) * P], ps_s[n % 2][:, c * P:(c + 1) * P], ACT.Relu,
                                               bias=b1_sb[:, n, c:c + 1])
                ins.then_inc(s["hev_a"], 1)

        @block.gpsimd
        def _(pool):
            nc.gpsimd.memset(ident[:], 0.0).then_inc(s["pool"], 1)
            pool.wait_ge(s["pool"], 1)
            nc.gpsimd.affine_select(out=ident[:], in_=ident[:], compare_op=ALU.not_equal, fill=1.0, base=0,
                                    pattern=[[-1, P]], channel_multiplier=1).then_inc(s["init"], 1)
            nc.gpsimd.memset(ones_sq[:], 1.0)
            nc.gpsimd.memset(zero[:], 0.0).then_inc(s["pool"], 1)
            pool.wait_ge(s["pool"], 2)
            nc.gpsimd.affine_select(out=tri[:], in_=ones_sq[:], compare_op=ALU.is_gt, fill=0.0, base=0,
                                    pattern=[[1, P]], channel_multiplier=-1)
            nc.gpsimd.iota(rev[:], [[-1, E]], base=E, channel_multiplier=0, allow_small_or_imprecise_dtypes=True)
            nc.gpsimd.iota(thr[:], [[P, NT]], base=0, channel_multiplier=0, allow_small_or_imprecise_dtypes=True)
            nc.gpsimd.iota(tix[:], [[1, NSL]], base=0, channel_multiplier=0,
                           allow_small_or_imprecise_dtypes=True).then_inc(s["init"], 1)

            def add(p, st, h):
                half, kt = divmod(st, TB)
                pool.wait_ge(s["exp"], n_score(p, st, h))
                if kt == 1:
                    first = probs[:, (st - 1) % 4, h, :]
                    ge(pool, s["den"], 2 * p + half - 1)
                else:
                    first = acc[:, half, h, :]
                    pool.wait_ge(s["add"], n_add(p, st, h) - 2)
                nc.gpsimd.tensor_tensor(acc[:, half, h, :], first, probs[:, st % 4, h, :], ALU.add).then_inc(s["add"], 1)

            def pair(p, par):
                for st in range(NSTEP):
                    if st % TB:
                        add(p, st, 0)
                        add(p, st, 1)

            pairs(pool, pair)

            pool.wait_ge(s["xwx"], 1)
            pool.wait_ge(s["sc"], 1)
            pool.wait_ge(d_zero, 16 * NSL)
            for k in range(NT):
                nc.gpsimd.indirect_dma_start(out=xs_dram, out_offset=bass.IndirectOffsetOnAxis(ap=slot[:, k:k + 1], axis=0),
                                             in_=xw[:, k, :], in_offset=None).then_inc(d_sc, 16)
            for n in range(4):
                pool.wait_ge(d_ys[n], 16 * (NSL // 4))
            for k in range(NT):
                nc.gpsimd.indirect_dma_start(out=yg[:, k, :], out_offset=None, in_=ys_dram,
                                             in_offset=bass.IndirectOffsetOnAxis(ap=slot[:, k:k + 1], axis=0)).then_inc(d_yg, 16)

        @block.vector
        def _(dve):
            seq = [0]

            def then(ins):
                seq[0] += 1
                ins.then_inc(s["dve"], 1)
                dve.wait_ge(s["dve"], seq[0])

            nc.vector.memset(ones[:], 1.0)
            nc.vector.memset(wqk[0:64, :, 64:128], 0.0)
            nc.vector.memset(wqk[64:128, :, 0:64], 0.0)
            nc.vector.memset(k2[64:65, :, :, :].bitcast(F32), 1.0).then_inc(s["c"], 1)
            dve.wait_ge(s["silu"], 1)
            dve.wait_ge(d_in, 16)
            then(nc.vector.tensor_scalar_add(c_e[:, 1, :], c_e[:, 0, :], 1.0))
            then(nc.vector.reciprocal(c_e[:, 2, :], c_e[:, 1, :]))
            then(nc.vector.tensor_tensor(c_e[:, 0, :], c_e[:, 2, :], c_col[:], ALU.mult))
            for b in range(B):
                ins = nc.vector.tensor_copy(c_rep[:, b, :], c_e[:, 0, b:b + 1].to_broadcast([P, P]))
            ins.then_inc(s["crep"], 1)

            def normalise(dst, src, arrived):
                for k in range(NT):
                    arrived(k)
                    ins = nc.vector.bn_stats(bst[:, k, :], src[:, k, :])
                then(ins)
                for k in range(NT):
                    ins = nc.vector.bn_aggr(mv[:, k, :], bst[:, k, :])
                then(ins)
                nc.vector.tensor_scalar_add(sd[:, 0, :], mv[:, :, 1], EPS).then_inc(s["std"], 1)
                rounds[0] += 1
                dve.wait_ge(s["rstd"], rounds[0])
                then(nc.vector.reciprocal(sd[:, 0, :], sd[:, 1, :]))
                for k in range(NT):
                    ins = nc.vector.tensor_scalar(dst[:, k, :], src[:, k, :], mv[:, k, 0:1], sd[:, 0, k:k + 1],
                                                  ALU.subtract, ALU.mult)
                    if dst is hn:
                        ins.then_inc(s["hnx"], 1)
                return ins

            rounds = [0]

            def x_here(k):
                if k == 0:
                    dve.wait_ge(d_in2, 64)
            then(normalise(h0, x_sb, x_here))
            dve.wait_ge(s["modsb"], 4)
            then(nc.vector.tensor_scalar_add(mod[:, :, 1:5:3, :], mod[:, :, 1:5:3, :], 1.0))
            for b in range(B):
                tb = slice(b * TB, (b + 1) * TB)
                then(nc.vector.tensor_tensor(h0[:, tb, :], h0[:, tb, :], mod[:, b, 1:2, :].to_broadcast([P, TB, D]), ALU.mult))
                then(nc.vector.tensor_tensor(h0[:, tb, :], h0[:, tb, :], mod[:, b, 0:1, :].to_broadcast([P, TB, D]), ALU.add))
            normalise(hn, h0, lambda k: None)
            for b in range(B):
                gates = mod[:, b, 2:6:3, :]
                then(nc.vector.tensor_scalar(g_tmp[:, b, :, :], gates, 0.0, 2.0, ALU.is_ge, ALU.mult))
                then(nc.vector.tensor_scalar(g_abs[:, b, :, :], gates, -1.0, 0.25, ALU.mult, ALU.max))
                then(nc.vector.tensor_tensor(gates, gates, g_abs[:, b, :, :], ALU.max))
                then(nc.vector.scalar_tensor_tensor(out=gates, in0=g_tmp[:, b, :, :], scalar=-1.0, in1=gates,
                                                    op0=ALU.add, op1=ALU.mult))
            for g in range(2):
                dve.wait_ge(s["lps"], g + 1)
                nc.vector.tensor_copy(c_all[:, 8 * g:8 * g + 8, :].rearrange("p a l -> p (a l)"),
                                      ps_m[g][:]).then_inc(s["lev"], 1)

            def rope(q, h, half, step):
                n = 10 * (2 * q + h) + 5 * half
                c = slice(half * HALF, (half + 1) * HALF)
                if half == 0:
                    dve.wait_ge(s["uev"], 4 * q + 2 * h + 2)
                    dve.wait_ge(d_swap[h], 64 * (q + 1))
                    ge(dve, d_pq[h], 64 * q)
                    ge(dve, d_p2[h], 32 * q)
                if step == 0:
                    nc.vector.tensor_tensor(us[:, h, c], us[:, h, c], cos_sb[:, c], ALU.mult).then_inc(s["rope"], 1)
                if step == 1:
                    nc.vector.tensor_tensor(vs[:, h, c], vs[:, h, c], sin_sb[:, c], ALU.mult).then_inc(s["rope"], 1)
                if step == 2:
                    dve.wait_ge(s["rope"], n + 2)
                    nc.vector.tensor_tensor(us[:, h, c], us[:, h, c], vs[:, h, c], ALU.add).then_inc(s["rope"], 1)
                if step == 3:
                    dve.wait_ge(s["rope"], n + 3)
                    nc.vector.tensor_copy(xh[:, h, c], us[:, h, c]).then_inc(s["rope"], 1)
                if step == 4:
                    dve.wait_ge(s["rope"], n + 4)
                    nc.vector.tensor_tensor(vs[:, h, c], us[:, h, c], xh[:, h, c].bitcast(F32),
                                            ALU.subtract).then_inc(s["rope"], 1)

            def reduce_max(q, n):
                h, r = divmod(n, 16)
                qt, kh = divmod(r, 2)
                dve.wait_ge(s["maxps"], 32 * q + n + 1)
                if r == 0:
                    ge(dve, s["nm"], 2 * q + h - 1)
                nc.vector.reduce_max(mx[:, h, kh, qt:qt + 1], ps_m[n % 2][:], AX.X).then_inc(s["maxr"], 1)

            def neg_max(q, h):
                dve.wait_ge(s["maxr"], 32 * q + 16 * (h + 1))
                ge(dve, d_m[h], 16 * q)
                nc.vector.tensor_reduce(nm[:, h, :], mx[:, h, :, :].rearrange("p k t -> p t k"), AX.X, ALU.max,
                                        negate=True).then_inc(s["nm"], 1)

            def den_out(p, half):
                dve.wait_ge(s["den"], 2 * p + half + 1)
                ge(dve, d_d1, 32 * (2 * p + half))
                nc.vector.tensor_copy(den[:], ps_x[0:64, :]).then_inc(s["denev"], 1)

            def recip(p, half):
                dve.wait_ge(d_d1, 32 * (2 * p + half + 1))
                nc.vector.reciprocal(rc[:, half, :, :], denc[:, half, :, :]).then_inc(s["rcp"], 1)

            def divide(p, half):
                dve.wait_ge(d_d3, 32 * (2 * p + half + 1))
                dve.wait_ge(s["oev"], 2 * p + half + 1)
                nc.vector.tensor_tensor(ou[:, half, :], ou[:, half, :], rr[:, half, :], ALU.mult).then_inc(s["mul"], 1)

            dve.wait_ge(d_in3, 80)
            ROPE = [(h, half, step) for h in range(2) for half in range(2) for step in range(5)]
            for piece in ROPE:
                rope(0, *piece)
            for n in range(32):
                reduce_max(0, n)
                if n % 16 == 15:
                    neg_max(0, n // 16)
            for piece in ROPE:
                rope(1, *piece)

            def pair(p, par):
                first = isinstance(p, int) and p == 0
                rest = list(ROPE)

                def rope_on(n):
                    for _ in range(n if not last2(p) else 0):
                        if rest:
                            rope(p + 2, *rest.pop(0))

                for st in range(NSTEP):
                    if st == 1 and not first:
                        divide(p - 1, 0)
                    if st == 2 and not first:
                        den_out(p - 1, 1)
                    if st == 11:
                        den_out(p, 0)
                    if not last(p):
                        for n in range(sum(MAXN[:st]), sum(MAXN[:st + 1])):
                            reduce_max(p + 1, n)
                            if n % 16 == 15:
                                neg_max(p + 1, n // 16)
                            if st >= 10:
                                rope_on(1)
                    if st == 5 and not first:
                        recip(p - 1, 1)
                    if st == 9 and not first:
                        divide(p - 1, 1)
                    if st == 13:
                        recip(p, 0)
                rope_on(20)

            pairs(dve, pair)
            divide(NPAIR - 1, 0)
            den_out(NPAIR - 1, 1)
            recip(NPAIR - 1, 1)
            divide(NPAIR - 1, 1)

            def block_out(g):
                b = g // 2
                ts = slice(4 * g, 4 * g + 4)
                wide = lambda m: mod[:, b, m:m + 1, :].to_broadcast([P, 4, D])
                dve.wait_ge(s["ytp"], g + 1)
                a_ps = ps_s[2 + g % 2][:].rearrange("p (t d) -> p t d", d=D)
                ins = nc.vector.tensor_tensor(h0[:, ts, :], a_ps, h0[:, ts, :], ALU.add)
                ins.then_inc(s["ybk"], 1)
                dve.wait_ge(s["ybk"], g + 1)
                then(nc.vector.tensor_tensor(h0[:, ts, :], h0[:, ts, :], wide(2), ALU.mult))
                then(nc.vector.tensor_tensor(x_sb[:, ts, :], x_sb[:, ts, :], h0[:, ts, :], ALU.add))
                for k in range(4 * g, 4 * g + 4):
                    ins = nc.vector.bn_stats(bst[:, k, :], x_sb[:, k, :])
                then(ins)
                for k in range(4 * g, 4 * g + 4):
                    ins = nc.vector.bn_aggr(mv[:, k, :], bst[:, k, :])
                then(ins)
                nc.vector.tensor_scalar_add(sd[:, 0, ts], mv[:, ts, 1], EPS).then_inc(s["std"], 1)
                dve.wait_ge(s["rstd"], 3 + g)
                then(nc.vector.reciprocal(sd[:, 0, ts], sd[:, 1, ts]))
                for k in range(4 * g, 4 * g + 4):
                    ins = nc.vector.tensor_scalar(h2[:, k, :], x_sb[:, k, :], mv[:, k, 0:1], sd[:, 0, k:k + 1],
                                                  ALU.subtract, ALU.mult)
                then(ins)
                then(nc.vector.tensor_tensor(h2[:, ts, :], h2[:, ts, :], wide(4), ALU.mult))
                nc.vector.tensor_tensor(h2[:, ts, :], h2[:, ts, :], wide(3), ALU.add).then_inc(s["h2x"], 1)

            for g in range(4):
                block_out(g)

            dve.wait_ge(s["lgp"], 4)
            dve.wait_ge(d_gw, 32)
            dve.wait_ge(s["init"], 2)
            tok = lambda a: rs[:, a, :].unsqueeze(2).to_broadcast([P, NT, E])
            row = lambda a: a.unsqueeze(1).to_broadcast([P, NT, E])
            V = nc.vector
            then(V.tensor_tensor(lg[:], ps_o[:, 0:NT * E].rearrange("p (t e) -> p t e", e=E), row(gb_sb[:]), ALU.add))
            then(V.reduce_max(rs[:, 0, :], lg[:], AX.X))
            V.tensor_tensor(rt[:, 0], lg[:], tok(0), ALU.subtract).then_inc(s["lgx"], 1)
            dve.wait_ge(s["ex2"], 1)
            then(V.reduce_sum(rs[:, 1, :], rt[:, 1], AX.X))
            then(V.reciprocal(rs[:, 2, :], rs[:, 1, :]))
            then(V.tensor_tensor(lg[:], rt[:, 1], tok(2), ALU.mult))
            then(V.reduce_max(rs[:, 3, :], lg[:], AX.X))
            then(V.tensor_tensor(rt[:, 2], lg[:], tok(3), ALU.is_equal))
            then(V.tensor_tensor(rt[:, 3], rt[:, 2], row(rev[:]), ALU.mult))
            then(V.reduce_max(rs[:, 4, :], rt[:, 3], AX.X))
            then(V.tensor_tensor(rt[:, 4], rt[:, 3], tok(4), ALU.is_equal))
            then(V.scalar_tensor_tensor(out=rt[:, 5], in0=rt[:, 4], scalar=-2.0, in1=lg[:], op0=ALU.mult, op1=ALU.add))
            then(V.reduce_max(rs[:, 5, :], rt[:, 5], AX.X))
            then(V.tensor_tensor(rt[:, 6], rt[:, 5], tok(5), ALU.is_equal))
            then(V.tensor_tensor(rt[:, 7], rt[:, 6], row(rev[:]), ALU.mult))
            then(V.reduce_max(rs[:, 6, :], rt[:, 7], AX.X))
            then(V.tensor_tensor(rs[:, 7, :], rs[:, 6, :], rs[:, 4, :], ALU.is_lt))
            then(V.scalar_tensor_tensor(out=rs[:, 7, :], in0=rs[:, 5, :], scalar=0.0, in1=rs[:, 7, :],
                                        op0=ALU.is_gt, op1=ALU.mult))
            then(V.tensor_scalar(rs[:, 8, :], rs[:, 7, :], -1.0, 1.0, ALU.mult, ALU.add))
            then(V.tensor_tensor(rs[:, 9, :], rs[:, 3, :], rs[:, 8, :], ALU.mult))
            then(V.tensor_tensor(rs[:, 5, :], rs[:, 5, :], rs[:, 7, :], ALU.mult))
            then(V.tensor_tensor(wsel, rs[:, 9, :], rs[:, 5, :], ALU.add))
            then(V.tensor_tensor(rs[:, 4, :], rs[:, 4, :], rs[:, 8, :], ALU.mult))
            then(V.tensor_tensor(rs[:, 6, :], rs[:, 6, :], rs[:, 7, :], ALU.mult))
            then(V.tensor_tensor(rs[:, 11, :], rs[:, 4, :], rs[:, 6, :], ALU.add))
            then(V.tensor_tensor(rt[:, 8], row(rev[:]), tok(11), ALU.is_equal))
            V.reduce_sum(cn[:, 0, :], rt[:, 8].rearrange("p t e -> p e t"), AX.X).then_inc(s["cnt"], 1)
            src = 8
            for n, sh in enumerate((1, 2, 4, 8)):
                dst = 9 + n % 2
                V.tensor_copy(rt[:, dst, 0:sh, :], rt[:, src, 0:sh, :])
                then(V.tensor_tensor(rt[:, dst, sh:, :], rt[:, src, sh:, :], rt[:, src, 0:NT - sh, :], ALU.add))
                src = dst
            then(V.tensor_tensor(rt[:, 11], rt[:, src], rt[:, 8], ALU.subtract))
            for k in range(NT):
                ins = V.tensor_scalar(xw[:, k, :], h2[:, k, :], wsel[:, k:k + 1], None, ALU.mult)
            ins.then_inc(s["xwx"], 1)
            dve.wait_ge(s["pre"], 1)
            then(V.tensor_copy(cn[:, 1:3, :].rearrange("p a e -> p (a e)"), ps_x[:, 0:2 * E]))
            then(V.tensor_tensor(cmp3[:, :, 0:NT], cn[:, 2, :].unsqueeze(2).to_broadcast([P, E, NT]),
                                 thr[:].unsqueeze(1).to_broadcast([P, E, NT]), ALU.is_gt))
            then(V.reduce_sum(cn[:, 3, :], cmp3[:, :, 0:NT], AX.X))
            src = 3
            for n, sh in enumerate((1, 2, 4)):
                dst = 4 + n
                V.tensor_copy(cn[:, dst, 0:sh], cn[:, src, 0:sh])
                then(V.tensor_tensor(cn[:, dst, sh:], cn[:, src, sh:], cn[:, src, 0:E - sh], ALU.add))
                src = dst
            then(V.tensor_tensor(cn[:, 7, :], cn[:, src, :], cn[:, 3, :], ALU.subtract))
            then(V.scalar_tensor_tensor(out=cn[:, 8, :], in0=cn[:, 7, :], scalar=float(P), in1=cn[:, 1, :],
                                        op0=ALU.mult, op1=ALU.add))
            then(V.tensor_tensor(rt[:, 9], rt[:, 11], row(cn[:, 8, :]), ALU.add))
            then(V.tensor_tensor(rt[:, 10], rt[:, 9], rt[:, 8], ALU.mult))
            then(V.reduce_sum(rs[:, 0, :], rt[:, 10], AX.X))
            V.tensor_copy(slot[:], rs[:, 0, :]).then_inc(s["sc"], 1)
            then(V.tensor_tensor(cmp3[:], cn[:, src, :].unsqueeze(2).to_broadcast([P, E, NSL]),
                                 tix[:].unsqueeze(1).to_broadcast([P, E, NSL]), ALU.is_le))
            then(V.reduce_sum(tcount[:], cmp3[:].rearrange("p e t -> p t e"), AX.X))
            V.tensor_scalar(eid[:], tcount[:], float(E - 1), None, ALU.min).then_inc(s["sc"], 1)

            for k in range(NSL):
                n = k % 4
                dve.wait_ge(s["hps"], k + 1)
                ge(dve, s["yo"], k - 1)
                for c in range(2, 4):
                    ins = V.tensor_scalar(hid[n % 2][:, c * P:(c + 1) * P], ps_s[2 + n % 2][:, c * P:(c + 1) * P],
                                          b1_sb[:, n, c:c + 1], 0.0, ALU.add, ALU.max)
                ins.then_inc(s["hev_d"], 1)
                dve.wait_ge(s["yo"], k + 1)
                ge(dve, d_ys[n], 16 * (k // 4))
                V.tensor_tensor(ys[:, n, :], (ps_o, ps_x)[n % 2][:, 0:D], b2_sb[:, n, :], ALU.add).then_inc(s["yoe"], 1)

            dve.wait_ge(d_yg, 16 * NT)
            for g in range(4):
                b = g // 2
                ts = slice(4 * g, 4 * g + 4)
                then(V.tensor_tensor(yg[:, ts, :], yg[:, ts, :], mod[:, b, 5:6, :].to_broadcast([P, 4, D]), ALU.mult))
                V.tensor_tensor(x_sb[:, ts, :], x_sb[:, ts, :], yg[:, ts, :], ALU.add).then_inc(s["fin"], 1)

        @block.sync
        def _(sp):
            sp.dma_start(c_col[:], t["c_t"]).then_inc(d_in, 16)
            sp.dma_start(wmod_sb[:], t["wmod"]).then_inc(d_in3, 16)
            for g in range(4):
                sp.dma_start(x_sb[:, 4 * g:4 * g + 4, :],
                             t["x"][4 * g * P:4 * (g + 1) * P, :].rearrange("(t p) d -> p t d", p=P)).then_inc(d_in2, 16)
            sp.dma_start(lns[:], t["lns"]).then_inc(d_in3, 16)
            sp.dma_start(wd_sb[:], t["wd"]).then_inc(d_in3, 16)
            sp.dma_start(cos_sb[:], t["cos"]).then_inc(d_in3, 16)
            sp.dma_start(sin_sb[:], t["sin"]).then_inc(d_in3, 16)
            sp.dma_start(wuv_sb, t["wuv"]).then_inc(d_vo, 16)
            sp.dma_start(wo_sb, t["wo"]).then_inc(d_vo, 16)
            sp.dma_start(gw_sb[:], t["gate_w"]).then_inc(d_gw, 16)
            sp.dma_start(gb_sb[:], t["gate_b"].to_broadcast([P, E])).then_inc(d_gw, 16)

            def weights(q):
                ge_all(sp,
                       (s["u"], 4 * q),
                       (s["c"], 1))
                j = q % HP
                for h in range(2):
                    sp.dma_start(wqk[0:64, h, 0:64], t["wq"][j, h]).then_inc(d_w, 16)
                    sp.dma_start(wqk[64:128, h, 64:128], t["wk"][j, h]).then_inc(d_w, 16)

            def values(q, par):
                ge_all(sp,
                       (s["pv"], 16 * (q - 1)),
                       (s["lev"], 2))
                b = q // HP
                sp.dma_start(cv[:, par, :, :], c_all[:, bass.ds(b * TB, TB), :]).then_inc(d_cv, 16)

            def swap(q, h):
                ge_all(sp,
                       (s["uev"], 4 * q + 2 * h + 2),
                       (d_p2[h], 32 * q),
                       (d_pq[h], 64 * q))
                for a in range(4):
                    c = a ^ 1
                    sp.dma_start(vs[32 * a:32 * a + 32, h, :], us[32 * c:32 * c + 32, h, :]).then_inc(d_swap[h], 16)

            def place(q, par, h):
                ge_all(sp,
                       (s["rope"], 10 * (2 * q + h) + 10),
                       (s["scores"], 32 * (q - 1)))
                xf = xh[:, h, :].bitcast(F32)
                lo = vs[:, h, :]
                sp.dma_start(qq[0:64, par, h, :].bitcast(F32), xf[0:64, :]).then_inc(d_pq[h], 16)
                sp.dma_start(qq[64:128, par, h, :].bitcast(F32), xf[0:64, :]).then_inc(d_pq[h], 16)
                sp.dma_start(kk[0:64, par, h, :].bitcast(F32), xf[64:128, :]).then_inc(d_pq[h], 16)
                sp.dma_start(kk[64:128, par, h, :].bitcast(F32), lo[64:128, :]).then_inc(d_pq[h], 16)
                sp.dma_start(q2[0:64, par, h, :].bitcast(F32), lo[0:64, :]).then_inc(d_p2[h], 16)
                sp.dma_start(k2[0:64, par, h, :].bitcast(F32), xf[64:128, :]).then_inc(d_p2[h], 16)

            def max_row(q, par, h):
                ge_all(sp,
                       (s["nm"], 2 * q + h + 1),
                       (s["scores"], 32 * (q - 1)))
                sp.dma_start(q2[64:65, par, h, :].bitcast(F32), nm[:, h, :].bitcast(F32)).then_inc(d_m[h], 16)

            def den_cols(p, half):
                sp.wait_ge(s["denev"], 2 * p + half + 1)
                for h in range(2):
                    sp.dma_start(denc[:, half, h, :], den[32 * h:32 * h + 1, :]).then_inc(d_d1, 16)

            def inv_rows(p, half):
                sp.wait_ge(s["rcp"], 2 * p + half + 1)
                sp.dma_start(rd_dram[half].rearrange("h (p f) -> p h f", f=4), rc[:, half, :, :]).then_inc(d_d2, 16)

            def inv_spread(p, half):
                sp.wait_ge(d_d2, 16 * (2 * p + half + 1))
                for h in range(2):
                    sp.dma_start(rr[64 * h:64 * h + 64, half, :],
                                 rd_dram[half, h:h + 1, :].to_broadcast([64, HALF])).then_inc(d_d3, 16)

            def spill(p, half):
                ge_all(sp,
                       (s["mul"], 2 * p + half + 1),
                       (s["mul"], 1))
                sp.dma_start(o_dram[p, :, half * HALF:(half + 1) * HALF], ou[:, half, :]).then_inc(d_sp[half], 16)

            sp.wait_ge(s["c"], 1)
            weights(0)
            weights(1)
            sp.wait_ge(s["lev"], 2)
            values(0, 0)
            for h in range(2):
                swap(0, h)
            for h in range(2):
                place(0, 0, h)
            swap(1, 0)
            swap(1, 1)
            for h in range(2):
                max_row(0, 0, h)

            def pair(p, par):
                first = isinstance(p, int) and p == 0
                if not last(p):
                    place(p + 1, 1 - par, 0)
                    place(p + 1, 1 - par, 1)
                if not first:
                    spill(p - 1, 0)
                if not last2(p):
                    weights(p + 2)
                if not last(p):
                    values(p + 1, 1 - par)
                if not first:
                    den_cols(p - 1, 1)
                    inv_rows(p - 1, 1)
                    inv_spread(p - 1, 1)
                if not last2(p):
                    swap(p + 2, 0)
                if not last(p):
                    max_row(p + 1, 1 - par, 0)
                if not first:
                    spill(p - 1, 1)
                if not last2(p):
                    swap(p + 2, 1)
                den_cols(p, 0)
                inv_rows(p, 0)
                if not last(p):
                    max_row(p + 1, 1 - par, 1)
                inv_spread(p, 0)

            pairs(sp, pair)
            spill(NPAIR - 1, 0)
            p = NPAIR - 1
            den_cols(p, 1)
            inv_rows(p, 1)
            inv_spread(p, 1)
            spill(p, 1)
            sp.wait_ge(s["init"], 2)
            for k in range(NSL):
                sp.dma_start(xs_dram[k * P:(k + 1) * P, :], zero[:]).then_inc(d_zero, 16)
            ge_all(sp,
                   (d_sp[0], 16 * NPAIR),
                   (d_sp[1], 16 * NPAIR))
            for g in range(4):
                b, half = divmod(g, 2)
                if g >= 2:
                    sp.wait_ge(s["yps"], g - 1)
                sp.dma_start(on[g % 2], o_dram[b * HP:(b + 1) * HP, :, half * HALF:(half + 1) * HALF].rearrange("j p n -> p j n")
                             ).then_inc(d_on[g % 2], 16)
            sp.wait_ge(s["sc"], 2)
            for k in range(NSL):
                n = k % 4
                if k == 4:
                    sp.wait_ge(d_sc, 16 * NT)
                    sp.dma_start(xs, xs_dram.rearrange("(t p) d -> p t d", p=P)).then_inc(d_xs, 16)
                if k >= 4:
                    sp.wait_ge(s["yoe"], k - 3)
                e = sp.value_load(eid[0:1, k:k + 1], min_val=0, max_val=E - 1)
                sp.dma_start(probs[:, n, :, :], t["w12"][e]).then_inc(d_wp[n], 16)
                sp.dma_start(b1_sb[:, n, :], t["b1"][e]).then_inc(d_wp[n], 16)
                sp.dma_start(b2_sb[:, n, :], t["b2"][bass.ds(e, 1), :].to_broadcast([P, D])).then_inc(d_wp[n], 16)
                if k >= 4:
                    j = k - 4
                    sp.dma_start(ys_dram[j * P:(j + 1) * P, :], ys[:, j % 4, :]).then_inc(d_ys[j % 4], 16)
            for j in range(NSL - 4, NSL):
                sp.wait_ge(s["yoe"], j + 1)
                sp.dma_start(ys_dram[j * P:(j + 1) * P, :], ys[:, j % 4, :]).then_inc(d_ys[j % 4], 16)
            if out is not None:
                for g in range(4):
                    sp.wait_ge(s["fin"], g + 1)
                    sp.dma_start(out[4 * g * P:4 * (g + 1) * P, :].rearrange("(t p) d -> p t d", p=P),
                                 x_sb[:, 4 * g:4 * g + 4, :]).then_inc(d_out, 16)
                sp.wait_ge(d_out, 64)
            if dbg:
                n = 0
                for name, src in (("o", o_dram), ("h0", h0), ("mod", mod), ("cT", cT), ("qq",qq),("kk",kk),("q2",q2),("k2",k2)):
                    if name in dbg:
                        a = src[:] if name != "o" else src
                        if name in ("qq","kk","q2","k2"): a = src[0:64].bitcast(F32)
                        sp.dma_start(dbg[name], a).then_inc(d_dbg, 16)
                        n += 16
                sp.wait_ge(d_dbg, n)


def tables():
    inv_freq = 1.0 / 10000.0 ** (np.arange(0, DH, 2, dtype=np.float32) / DH)
    freqs = np.outer(np.arange(S, dtype=np.float32), inv_freq)
    cos = np.concatenate([np.cos(freqs), np.cos(freqs)], -1)[:, ::2].T
    sin = np.concatenate([np.sin(freqs), np.sin(freqs)], -1)[:, ::2].T
    return (np.ascontiguousarray(np.concatenate([cos] * 4), dtype=np.float32),
            np.ascontiguousarray(np.concatenate([-sin, sin] * 2), dtype=np.float32))


def layout(i):
    def up(w):
        w = np.asarray(w).reshape(HP, 2, DH // 2, 2, LAT).transpose(0, 1, 4, 3, 2)
        return np.ascontiguousarray(w.reshape(HP, 2, LAT, DH))
    cos, sin = tables()
    f = lambda a: np.ascontiguousarray(np.asarray(a))
    return {
        "x": f(i["L0_attn_x"]).reshape(B * S, D),
        "c_t": f(np.asarray(i["L0_c"]).T),
        "wmod": f(i["L0_wmod"]),
        "wd": f(np.concatenate([np.asarray(i["L0_attn_w_down_q"]), np.asarray(i["L0_attn_w_down_kv"])]).T),
        "lns": f(np.stack([np.asarray(i["L0_attn_ln_scale"]), np.asarray(i["L0_attn_ln_bias"])], 1)),
        "wq": up(i["L0_attn_w_up_q"]), "wk": up(i["L0_attn_w_up_k"]),
        "cos": cos, "sin": sin,
        "wuv": f(np.asarray(i["L0_attn_w_up_v"]).reshape(H, DH, LAT).transpose(1, 0, 2)),
        "wo": f(np.asarray(i["L0_attn_w_out"]).T.reshape(H, DH, D).transpose(1, 0, 2)),
        "gate_w": f(i["L0_ffn_gate_w"]), "gate_b": f(i["L0_ffn_gate_b"]).reshape(1, E),
        "w12": f(np.stack([np.asarray(i["L0_ffn_w1"]),
                           np.asarray(i["L0_ffn_w2"]).reshape(E, 4, P, D).transpose(0, 2, 1, 3).reshape(E, P, 4 * D)], 2)),
        "b1": f(np.asarray(i["L0_ffn_b1"]).reshape(E, 4, P).transpose(0, 2, 1)),
        "b2": f(i["L0_ffn_b2"]),
    }


def kernel(**inputs):
    import concourse.bacc as bacc
    from concourse.bass_utils import run_bass_kernel_spmd

    nc = bacc.Bacc("TRN2", target_bir_lowering=False, num_devices=1)
    arrays = layout(inputs)
    aps = {n: nc.dram_tensor(f"in_{n}", a.shape, mybir.dt.from_np(a.dtype), kind="ExternalInput").ap()
           for n, a in arrays.items()}
    out = nc.dram_tensor("out_dram", [B * S, D], F32, kind="ExternalOutput").ap()
    build(nc, aps, out)
    r = run_bass_kernel_spmd(nc, [{f"in_{n}": a for n, a in arrays.items()}], core_ids=[0])
    return r.results[0]["out_dram"].reshape(B, S, D)
```

```python
from contextlib import ExitStack

import numpy as np

import concourse.bass as bass
from concourse import mybir

ALU = mybir.AluOpType
ACT = mybir.ActivationFunctionType
AX = mybir.AxisListType
F32 = mybir.dt.float32
F32R = mybir.dt.float32r
I32 = mybir.dt.int32

P = 128
B, S, D = 2, 1024, 128
H, DH, LAT = 16, 64, 64
NT = B * S // P
TB = S // P
HP = H // 2
NPAIR = B * HP
HALF = 512
NSTEP = 2 * TB
E, F = 8, 512
NSL = TB + E - 1
GS = 3
NG = B * NSL // GS
NA = NG // B
WROW = 2 * F + F // P + D
EPS = 1e-5
SCALE = 0.125


def ge(eng, sem, value):
    if not (isinstance(value, int) and value <= 0):
        eng.wait_ge(sem, value)


def ge_all(eng, *waits):
    for _, v in waits:
        if not isinstance(v, int):
            eng.compute_val(v)
    for sem, v in waits:
        ge(eng, sem, v)


def build(nc, t, out, dbg=None):
    ctx = ExitStack()
    with ctx:
        def sb(name, shape, dt=F32):
            return ctx.enter_context(nc.sbuf_tensor(name, shape, dt))

        def pb(name, shape=(P, HALF), dt=F32):
            return ctx.enter_context(nc.psum_tensor(name, list(shape), dt))

        def sem(name):
            return ctx.enter_context(nc.semaphore(name))

        x_sb = sb("x_sb", [P, NT, D])
        h0 = sb("h0", [P, NT, D])
        hn = sb("hn", [P, NT, D])
        hT = sb("hT", [P, B * S])
        cq = sb("cq", [P, B * S], F32R)
        ck = sb("ck", [P, B * S], F32R)
        c_all = sb("c_all", [P, NT, LAT])
        ident = sb("ident", [P, P])
        ones = sb("ones", [P, 64])
        wmod_sb = sb("wmod_sb", [P, 6 * D])
        wd_sb = sb("wd_sb", [P, 2, 2 * LAT])
        c_col = sb("c_col", [P, B])
        c_e = sb("c_e", [P, 3, B])
        c_rep = sb("c_rep", [P, B, P])
        mod = sb("mod", [P, B, 6, D])
        lns = sb("lns", [P, 2])
        bst = sb("bst", [P, NT, 6])
        mv = sb("mv", [P, NT, 2])
        sd = sb("sd", [P, 2, NT])
        rot = sb("rot", [P, 2, S])
        cos_sb, sin_sb = rot[:, 0, :], rot[:, 1, :]

        wu = sb("wu", [P, 2, P])
        wh = sb("wh", [P, 2, P], F32R)
        wl = sb("wl", [P, 2, P], F32R)
        us = sb("us", [P, 2, S])
        vs = sb("vs", [P, 2, S])
        xh = sb("xh", [P, 2, S], F32R)
        qq = sb("qq", [P, 2, 2, S], F32R)
        kk = sb("kk", [P, 2, 2, S], F32R)
        q2 = sb("q2", [P, 2, 2, S], F32R)
        k2 = sb("k2", [P, 2, 2, S], F32R)
        cv = sb("cv", [P, 2, TB, LAT])
        probs = sb("probs", [P, 4, 2, HALF])
        acc = sb("acc", [P, 2, 2, HALF])
        mx = sb("mx", [P, 2, 2, TB])
        nm = sb("nm", [P, 2, TB], F32R)
        den = sb("den", [64, HALF])
        denc = sb("denc", [P, 2, 2, 4])
        rc = sb("rc", [P, 2, 2, 4])
        rr = sb("rr", [P, 2, HALF])
        ou = sb("ou", [P, 2, HALF])

        rd_dram = nc.dram_tensor("rd_dram", [2, 2, HALF], F32, kind="Internal").ap()
        xs_dram = [nc.dram_tensor(f"xs_dram{b}", [NSL * P, D], F32, kind="Internal").ap() for b in range(B)]
        ys_dram = [nc.dram_tensor(f"ys_dram{b}", [NSL * P, D], F32, kind="Internal").ap() for b in range(B)]

        flat = lambda a: a.rearrange("p a n -> p (a n)")
        wuv_sb = us[0:64, 0, :].rearrange("p (h l) -> p h l", h=H)
        wo_sb = flat(vs[0:64, :, :]).rearrange("p (h d) -> p h d", h=H)
        g_tmp, g_abs = [probs[:, n, 0, :].rearrange("p (b m d) -> p b m d", b=B, m=2) for n in range(2)]
        g_raw = acc[:].rearrange("p a h n -> p (a h n)")[:, 0:HP * D]
        g_all = hT[:].rearrange("p (b j d) -> p b j d", b=B, d=D)
        h2, xw, yg = hn, h0, hn
        h2T = c_all[:].rearrange("p t l -> p (t l)")
        p_flat = probs[:].rearrange("p s h n -> p (s h n)")
        wb = ([flat(us[:])[:, 0:WROW], flat(rot[:])[:, 0:WROW]] + [p_flat[:, n * WROW:(n + 1) * WROW] for n in range(3)]
              + [hT[:, 0:WROW]])
        w1_sb = [x[:, 0:F] for x in wb]
        w2_sb = [x[:, F:2 * F] for x in wb]
        b1_sb = [x[:, 2 * F:2 * F + F // P] for x in wb]
        b2_sb = [x[:, WROW - D:WROW] for x in wb]
        xs = flat(xh[:].bitcast(F32))[:, 0:2 * GS * D].rearrange("p (g t d) -> p g t d", g=2, d=D)
        ys = flat(vs[:])[:, 0:2 * GS * D].rearrange("p (g t d) -> p g t d", g=2, d=D)
        hid = [acc[:, 0, n, :] for n in range(2)]
        xT = [flat(vs[:])[:, (2 * GS + n) * D:(2 * GS + n + 1) * D] for n in range(2)]
        rt = [x.rearrange("p (a n) -> p a n", a=12) for x in (flat(vs[:])[:, 2 * S - 12 * TB * E:2 * S], wmod_sb[:])]

        gw_sb = sb("gw_sb", [P, E])
        gb_sb = sb("gb_sb", [P, E])
        zero = sb("zero", [P, D])
        tri = sb("tri", [P, P])
        ones_sq = sb("ones_sq", [P, P])
        half_neg = sb("half_neg", [P, TB])
        rev = sb("rev", [P, E])
        thr = sb("thr", [P, TB])
        tix = sb("tix", [P, NSL])
        again = sb("again", [P, E * TB])
        rs = sb("rs", [P, 12, TB])
        cn = sb("cn", [P, 6, E])
        cmp3 = sb("cmp3", [P, E, NSL])
        tcount = sb("tcount", [P, NSL])
        slot = sb("slot", [P, NT], I32)
        eid = sb("eid", [P, B * NSL], I32)

        ps_s = [pb(f"ps_s{n}") for n in range(4)]
        ps_m = [pb(f"ps_m{n}") for n in range(2)]
        ps_o = pb("ps_o")
        ps_x = pb("ps_x")

        names = ("lnq lnr tout nxt0 mod1 init modps modsb silu crep nrm nxt hmod trp tre cps cev csub lps lev c gate gx gfold wsp "
                 "dve pool hev yev scores exp pv add adx maxps maxr nm xps xev rcp mul oev rope xhc rq rs gps gev h2x h2tp h2te lgp lgx ex2 pre cnt xwx sc xtp xte hps hev_a hev_d yo yoe fin"
                 ).split()
        s = {n: sem("s_" + n) for n in names}
        d_in, d_mod, d_lns, d_wd, d_rope = [sem(n) for n in ("d_in", "d_mod", "d_lns", "d_wd", "d_rope")]
        d_w = sem("d_w")
        d_cv = sem("d_cv")
        d_swap = [sem("d_swap0"), sem("d_swap1")]
        d_pq = [sem("d_pq0"), sem("d_pq1")]
        d_ql = [sem("d_ql0"), sem("d_ql1")]
        d_kh = [sem("d_kh0"), sem("d_kh1")]
        d_m = [sem("d_m0"), sem("d_m1")]
        d_d1 = sem("d_d1")
        d_d2 = sem("d_d2")
        d_d3 = sem("d_d3")
        d_x = [sem(f"d_x{b}") for b in range(B)]
        d_vo, d_gw, d_zero, d_out = [sem(n) for n in ("d_vo", "d_gw", "d_zero", "d_out")]
        d_yg = [sem(f"d_yg{g}") for g in range(4)]
        d_sc = sem("d_sc")
        d_xs = [sem("d_xs0"), sem("d_xs1")]
        d_wp = [sem(f"d_wp{n}") for n in range(2 * GS)]
        d_ys = [sem("d_ys0"), sem("d_ys1")]

        block = ctx.enter_context(nc.Block())

        def n_score(p, st, h):
            return 32 * p + 2 * st + h + 1

        def n_add(p, st, h):
            half, kt = divmod(st, TB)
            if last(p):
                return (0 if h else 28 * p) + 7 * half + max(kt, 1)
            return 28 * p + 14 * half + 2 * (max(kt, 1) - 1) + h + 1

        def wait_adds(eng, p, st, heads):
            for h in heads:
                if last(p) and h == 1:
                    eng.wait_ge(s["adx"], n_add(p, st, h))
                elif last(p) or h == heads[-1]:
                    eng.wait_ge(s["add"], n_add(p, st, h))

        def x_use(what, p, k):
            place = {("up", 0): 0, ("up", 1): 1, ("up", 2): 2, ("up", 3): 3, ("den", 1): 4,
                     ("out", 0): 5, ("den", 0): 6, ("out", 1): 7}[what, k]
            at = p - 2 if what == "up" else p if (what, k) == ("den", 0) else p + 1
            if isinstance(at, int):
                if at < 0:
                    return 4 * p + k
                if at == 0:
                    return 4 * 2 + (k if what == "up" else 4)
                if at == NPAIR:
                    return 8 * (NPAIR - 2) + 5 + 8 + {4: 0, 5: 1, 7: 2}[place]
                if at >= NPAIR - 2:
                    return 8 * (NPAIR - 2) + 5 + 4 * (at - NPAIR + 2) + place - 4
            return 8 * at + 5 + place

        def step_before(p, st, n):
            st -= n
            if st < 0:
                p, st = p - 1, st + NSTEP
            return None if isinstance(p, int) and p < 0 else (p, st)

        def pairs(eng, body):
            body(0, 0)
            with eng.Fori(1, NPAIR - 3, 2) as p:
                body(p, 1)
                body(p + 1, 0)
            for q in range(NPAIR - 3, NPAIR):
                body(q, q % 2)

        def is_first(p):
            return isinstance(p, int) and p == 0

        def last(p, n=1):
            return isinstance(p, int) and p >= NPAIR - n

        MAXN = [0, 0, 0] + [3] * 10 + [2] + [0] * 2
        UP_STEPS = (1, 2, 3, 4)
        DEN1, OUT0, DEN0, OUT1 = 5, 8, 10, 14

        NACT = 4
        ROPE = []
        for n in range(4):
            ROPE += [(n, 0), (n, 1), (n, 2)]
            if n >= NACT:
                ROPE.append((n, 3))
            if n:
                ROPE.append((n - 1, 4))
        ROPE.append((3, 4))
        NROPE = len(ROPE)
        ROPE_STEPS = {5: 1, 6: 1, 7: 1, 8: 1, 9: 1, 10: 1, 11: 1, 12: 1, 13: 2, 14: 3, 15: 3}
        ACT_ROPE = {8: 0, 11: 1, 14: 2, 15: 3}

        LAST_ADD = 10
        T_H2, T_CN = 6, 9

        T_BANK = [ps_s[0], ps_s[1], ps_m[1], ps_o]
        C_BANK = [ps_s[2], ps_s[3], ps_s[0], ps_s[1]]

        def rope(eng, q, n, step):
            V = nc.vector if eng.engine == nc.vector.engine else nc.gpsimd
            w, half = divmod(n, 2)
            c = slice(half * HALF, (half + 1) * HALF)
            before = lambda i: eng.wait_ge(s["rope"], NROPE * q + ROPE.index((n, i)) + 1)
            if step == 0:
                if half == 0:
                    eng.wait_ge(d_swap[w], 64 * (q + 1))
                ins = V.tensor_tensor(us[:, w, c], us[:, w, c], cos_sb[:, c], ALU.mult)
            if step == 1:
                ins = V.tensor_tensor(vs[:, w, c], vs[:, w, c], sin_sb[:, c], ALU.mult)
            if step == 2:
                before(1)
                ins = V.tensor_tensor(us[:, w, c], us[:, w, c], vs[:, w, c], ALU.add)
            if step == 3:
                before(2)
                ins = V.tensor_copy(xh[:, w, c], us[:, w, c])
            if step == 4:
                if n < NACT:
                    eng.wait_ge(s["xhc"], NACT * q + n + 1)
                else:
                    before(3)
                ins = V.tensor_tensor(vs[:, w, c], us[:, w, c], xh[:, w, c].bitcast(F32), ALU.subtract)
            ins.then_inc(s["rope"], 1)

        def up_bank(q, j):
            return (ps_x, ps_s[2], ps_s[3], ps_s[0])[j] if is_first(q) else ps_x

        def max_bank(q, n):
            return (ps_m[0], ps_m[1], ps_s[0], ps_s[1])[n % 4] if is_first(q) else ps_m[n % 2]

        @block.tensor
        def _(pe):
            pe.wait_ge(s["crep"], 1)
            pe.wait_ge(d_mod, 16)
            for b in range(B):
                for n in range(2):
                    nc.tensor.matmul(ps_s[2 * b + n][:, 0:3 * D], c_rep[:, b, :], wmod_sb[:, n * 3 * D:(n + 1) * 3 * D],
                                     start=True, stop=True).then_inc(s["modps"], 1)
            pe.wait_ge(d_vo, 32)
            for n, bank in enumerate((ps_m[1], ps_o)):
                for j in range(4):
                    for h in range(2):
                        head = 2 * (4 * n + j) + h
                        ins = nc.tensor.matmul(bank[64 * h:64 * h + 64, j * P:(j + 1) * P], wuv_sb[:, head, :],
                                               wo_sb[:, head, :], start=True, stop=True)
                ins.then_inc(s["gps"], 1)

            def latents(b):
                for g in (2 * b, 2 * b + 1):
                    if g == 2:
                        pe.wait_ge(s["gev"], 2)
                    for n in range(4):
                        pe.wait_ge(s["nxt"], 4 * g + n + 1)
                        ins = nc.tensor.transpose(T_BANK[g][:, n * P:(n + 1) * P], hn[:, 4 * g + n, :], ident[:])
                    ins.then_inc(s["trp"], 1)
                if b == 1:
                    pe.wait_ge(s["xev"], 4)
                for n in range(4 * b, 4 * b + 4):
                    half, w = divmod(n % 4, 2)
                    pe.wait_ge(s["tre"], 2 * b + half + 1)
                    ge(pe, s["csub"], n - 3)
                    nc.tensor.matmul(C_BANK[n % 4][:], wd_sb[:, w, :], hT[:, b * S + half * HALF:b * S + (half + 1) * HALF],
                                     start=True, stop=True).then_inc(s["cps"], 1)
                ge(pe, s["lev"], b)
                for n in range(TB):
                    k = b * TB + n
                    ins = nc.tensor.matmul(ps_m[0][:, n * LAT:(n + 1) * LAT], hT[:, k * P:(k + 1) * P],
                                           wd_sb[:, 1, 0:LAT], start=True, stop=True)
                ins.then_inc(s["lps"], 1)

            def up(q, j):
                w, half = divmod(j, 2)
                if not is_first(q):
                    ge(pe, s["xev"], x_use("up", q, j))
                if j == 0:
                    pe.wait_ge(s["wsp"], 2 * (q + 1))
                c = (cq, ck)[w][:, bass.ds((q // HP) * S + half * HALF, HALF)]
                nc.tensor.matmul(up_bank(q, j)[:], wh[:, w, :], c, start=True, stop=False)
                nc.tensor.matmul(up_bank(q, j)[:], wl[:, w, :], c, start=False, stop=True).then_inc(s["xps"], 1)

            def maxima(q, par, n):
                h, r = divmod(n, 16)
                qt, kh = divmod(r, 2)
                if r == 0:
                    pe.wait_ge(d_pq[h], 64 * (q + 1))
                ge(pe, s["maxr"], n - 3 if is_first(q) else 32 * q + n - 1)
                qs = qq[:, par, h, :].rearrange("p (m t) -> p t m", t=TB)
                nc.tensor.matmul(max_bank(q, n)[:], qs[:, qt, :], kk[:, par, h, kh * HALF:(kh + 1) * HALF],
                                 start=True, stop=True).then_inc(s["maxps"], 1)

            def score(p, par, st, h):
                half, kt = divmod(st, TB)
                if st == 0:
                    pe.wait_ge(d_ql[h], 16 * (p + 1))
                    pe.wait_ge(d_kh[h], 16 * (p + 1))
                before = step_before(p, st, 2)
                if before:
                    ge(pe, s["exp"], n_score(*before, h))
                bank = ps_s[2 * (st % 2) + h]
                nc.tensor.matmul(bank[:], kk[:, par, h, kt * P:(kt + 1) * P], qq[:, par, h, half * HALF:(half + 1) * HALF],
                                 start=True, stop=False)
                if st == 0:
                    pe.wait_ge(d_m[h], 16 * (p + 1))
                nc.tensor.matmul(bank[:], k2[0:65, par, h, kt * P:(kt + 1) * P], q2[0:65, par, h, half * HALF:(half + 1) * HALF],
                                 start=False, stop=True).then_inc(s["scores"], 1)

            def pv(p, par, st):
                half, kt = divmod(st, TB)
                if st == 0:
                    pe.wait_ge(d_cv, 16 * (p + 1))
                if kt == 0:
                    ge(pe, s["oev"], 2 * p + half)
                for h in range(2):
                    pe.wait_ge(s["exp"], n_score(p, st, h))
                    ins = nc.tensor.matmul(ps_o[64 * h:64 * h + 64, :], cv[:, par, kt, :], probs[:, st % 4, h, :],
                                           start=(kt == 0), stop=(kt == TB - 1))
                ins.then_inc(s["pv"], 1)

            def denominators(p, half):
                ge(pe, s["xev"], x_use("den", p, half))
                wait_adds(pe, p, TB * half + TB - 1, (0, 1))
                for h in range(2):
                    ins = nc.tensor.matmul(ps_x[32 * h:32 * h + 32, :], ones[:, 0:32], acc[:, half, h, :], start=True, stop=True)
                ins.then_inc(s["xps"], 1)

            def outputs(p, half):
                ge(pe, s["xev"], x_use("out", p, half))
                pe.wait_ge(s["mul"], 2 * p + half + 1)
                for n in range(4):
                    ins = nc.tensor.matmul(ps_x[:, n * P:(n + 1) * P], ou[:, half, n * P:(n + 1) * P],
                                           g_all[:, p // HP, p % HP, :], start=True, stop=True)
                ins.then_inc(s["xps"], 1)

            pe.wait_ge(s["init"], 1)
            pe.wait_ge(d_wd, 16)
            latents(0)
            pe.wait_ge(s["csub"], 4)
            for j in range(4):
                up(0, j)
            latents(1)
            for j in range(4):
                up(1, j)
            pe.wait_ge(s["lev"], 2)
            pe.wait_ge(s["csub"], 8)
            for n in range(32):
                maxima(0, 0, n)
            pe.wait_ge(s["maxr"], 32)
            pe.wait_ge(s["gfold"], 2)

            def h2_features(b):
                pe.wait_ge(s["h2x"], b + 1)
                for g in range(2):
                    for n in range(4):
                        ins = nc.tensor.transpose(ps_m[g][:, n * P:(n + 1) * P], h2[:, TB * b + 4 * g + n, :], ident[:])
                    ins.then_inc(s["h2tp"], 1)

            def logits(b):
                pe.wait_ge(s["h2te"], 2 * b + 2)
                for n in range(TB):
                    ins = nc.tensor.matmul(ps_m[0][:, n * E:(n + 1) * E], h2T[:, n * P:(n + 1) * P], gw_sb[:],
                                           start=True, stop=True)
                ins.then_inc(s["lgp"], 1)

            def counts_before(b):
                pe.wait_ge(s["cnt"], b + 1)
                last_tile = rt[b][:, 9, :].rearrange("p (e t) -> p e t", e=E)[:, :, TB - 1]
                nc.tensor.matmul(ps_m[1][:, 0:E], tri[:], last_tile, start=True, stop=True)
                nc.tensor.matmul(ps_m[1][:, E:2 * E], ones_sq[:], last_tile, start=True, stop=True).then_inc(s["pre"], 1)

            def pair(p, par):
                for st in range(NSTEP):
                    if last(p):
                        if st == 0:
                            pe.wait_ge(s["maxr"], 32 * NPAIR)
                            h2_features(0)
                        if st == 2:
                            logits(0)
                        if st == 8:
                            counts_before(0)
                    todo = [] if last(p) else list(range(sum(MAXN[:st]), sum(MAXN[:st + 1])))
                    score(p, par, st, 0)
                    for n in todo[:1]:
                        maxima(p + 1, 1 - par, n)
                    score(p, par, st, 1)
                    for n in todo[1:2]:
                        maxima(p + 1, 1 - par, n)
                    if st > 0:
                        pv(p, par, st - 1)
                    elif not is_first(p):
                        pv(p - 1, 1 - par, NSTEP - 1)
                    for n in todo[2:]:
                        maxima(p + 1, 1 - par, n)
                    if st in UP_STEPS and not last(p, 2):
                        up(p + 2, st - UP_STEPS[0])
                    if not is_first(p):
                        if st == DEN1:
                            denominators(p - 1, 1)
                        if st == OUT0:
                            outputs(p - 1, 0)
                        if st == OUT1:
                            outputs(p - 1, 1)
                    if st == DEN0:
                        denominators(p, 0)

            pairs(pe, pair)
            pv(NPAIR - 1, 1, NSTEP - 1)
            ge(pe, s["xev"], x_use("den", NPAIR - 1, 1))
            wait_adds(pe, NPAIR - 1, NSTEP - 1, (0, 1))
            for h in range(2):
                ins = nc.tensor.matmul(ps_x[64 * h:64 * h + 64, :], ones[:], acc[:, 1, h, :], start=True, stop=True)
            ins.then_inc(s["xps"], 1)

            def slots_T(i, k):
                g = i // GS
                if i % GS == 0:
                    pe.wait_ge(d_xs[g % 2], 16 * (k // (2 * GS) + 1))
                ge(pe, s["xte"], k)
                nc.tensor.transpose(ps_s[2][:, 0:P], xs[:, g % 2, i % GS, :], ident[:]).then_inc(s["xtp"], 1)

            def up_e(i, k):
                pe.wait_ge(s["xte"], k + 1)
                pe.wait_ge(d_wp[i], 16 * (k // (2 * GS) + 1))
                ge(pe, s["hev"], k - 1)
                for c in range(4):
                    ins = nc.tensor.matmul(ps_s[i % 2][:, c * P:(c + 1) * P], w1_sb[i][:, c * P:(c + 1) * P], xT[i % 2],
                                           start=True, stop=True)
                ins.then_inc(s["hps"], 1)

            def down_e(i, k):
                pe.wait_ge(s["hev"], k + 1)
                ge(pe, s["yev"], k)
                for c in range(4):
                    ins = nc.tensor.matmul(ps_s[3][:, 0:D], hid[i % 2][:, c * P:(c + 1) * P],
                                           w2_sb[i][:, c * P:(c + 1) * P], start=(c == 0), stop=(c == 3))
                ins.then_inc(s["yo"], 1)

            def tiles(k0, lead=True, follow=True, between={}):
                if lead:
                    slots_T(0, k0)
                for i in range(2 * GS):
                    up_e(i, k0 + i)
                    if i < 2 * GS - 1 or follow:
                        slots_T((i + 1) % (2 * GS), k0 + i + 1)
                    if i or not isinstance(k0, int) or k0:
                        down_e((i - 1) % (2 * GS), k0 + i - 1)
                    if i in between:
                        between[i]()

            pe.wait_ge(s["exp"], 32 * NPAIR)
            outputs(NPAIR - 1, 0)
            tiles(0, between={0: lambda: outputs(NPAIR - 1, 1)})
            tiles(2 * GS, lead=False, between={T_H2 - 2 * GS: lambda: (h2_features(1), logits(1)),
                                               T_CN - 2 * GS: lambda: counts_before(1)})
            tiles(4 * GS, lead=False, follow=False)
            with pe.Fori(3, NG // 2) as g2:
                tiles(g2 * (2 * GS), follow=False)
            down_e(2 * GS - 1, NG * GS - 1)

        @block.scalar
        def _(act):
            act.wait_ge(d_in, 16)
            nc.scalar.activation(c_e[:, 0, :], c_col[:], ACT.Exp, scale=-1.0).then_inc(s["silu"], 1)

            def root(n):
                b = n // 2
                act.wait_ge(s["rq"], n + 1)
                nc.scalar.activation(sd[:, 1, b * TB:(b + 1) * TB], sd[:, 0, b * TB:(b + 1) * TB], ACT.Sqrt).then_inc(s["rs"], 1)

            root(0)
            for n in range(4):
                act.wait_ge(s["modps"], n + 1)
                dst = mod[:, n // 2, 3 * (n % 2):3 * (n % 2) + 3, :].rearrange("p a d -> p (a d)")
                nc.scalar.copy(dst, ps_s[n][:, 0:3 * D]).then_inc(s["modsb"], 1)
            root(1)
            for n, bank in enumerate((ps_m[1], ps_o)):
                act.wait_ge(s["gps"], n + 1)
                nc.scalar.copy(g_raw[:, n * HALF:(n + 1) * HALF], bank[:]).then_inc(s["gev"], 1)

            def features(g):
                if g == 0:
                    act.wait_ge(d_lns, 16)
                act.wait_ge(s["trp"], g + 1)
                nc.scalar.activation(hT[:, g * HALF:(g + 1) * HALF], T_BANK[g][:], ACT.Identity,
                                     bias=lns[:, 1:2], scale=lns[:, 0:1]).then_inc(s["tre"], 1)

            def upper(n):
                half, w = divmod(n % 4, 2)
                c = (n // 4) * S + half * HALF
                act.wait_ge(s["cps"], n + 1)
                nc.scalar.copy((cq, ck)[w][:, c:c + HALF], C_BANK[n % 4][:]).then_inc(s["cev"], 1)

            def values_out(b):
                act.wait_ge(s["lps"], b + 1)
                nc.scalar.copy(c_all[:, TB * b:TB * b + TB, :].rearrange("p a l -> p (a l)"), ps_m[0][:]).then_inc(s["lev"], 1)

            def up_out(q, j):
                w, half = divmod(j, 2)
                act.wait_ge(s["xps"], x_use("up", q, j) + 1)
                if j == 0:
                    ge(act, s["rope"], NROPE * q)
                nc.scalar.copy(us[:, w, half * HALF:(half + 1) * HALF], up_bank(q, j)[:]).then_inc(s["xev"], 1)

            def upper_rot(q, n):
                w, half = divmod(n, 2)
                if n == 0:
                    ge(act, d_pq[0], 64 * q)
                    ge(act, d_pq[1], 64 * q)
                act.wait_ge(s["rope"], NROPE * q + ROPE.index((n, 2)) + 1)
                c = slice(half * HALF, (half + 1) * HALF)
                nc.scalar.copy(xh[:, w, c], us[:, w, c]).then_inc(s["xhc"], 1)

            def expo(p, st, h):
                act.wait_ge(s["scores"], n_score(p, st, h))
                before = step_before(p, st, 4)
                if before:
                    bp, bst_ = before
                    if h == 0:
                        act.wait_ge(s["pv"], 16 * bp + bst_ + 1)
                    wait_adds(act, bp, bst_, (h,))
                nc.scalar.activation(probs[:, st % 4, h, :], ps_s[2 * (st % 2) + h][:], ACT.Exp,
                                     scale=SCALE).then_inc(s["exp"], 1)

            def o_out(p, half):
                act.wait_ge(s["pv"], 16 * p + 8 * half + 8)
                if not is_first(p):
                    act.wait_ge(s["xps"], x_use("out", p - 1, half) + 1)
                nc.scalar.copy(ou[:, half, :], ps_o[:]).then_inc(s["oev"], 1)

            def den_out(p, half):
                act.wait_ge(s["xps"], x_use("den", p, half) + 1)
                ge(act, d_d1, 32 * (2 * p + half))
                nc.scalar.copy(den[:], ps_x[0:64, :]).then_inc(s["xev"], 1)

            features(0)
            features(1)
            root(2)
            for n in range(4):
                upper(n)
            values_out(0)
            act.wait_ge(s["gps"], 2)
            for j in range(4):
                up_out(0, j)
            root(3)
            features(2)
            features(3)
            for n in range(NACT):
                upper_rot(0, n)
            for n in range(4, 8):
                upper(n)
            values_out(1)
            for j in range(4):
                up_out(1, j)
            for n in range(NACT):
                upper_rot(1, n)

            def h2T_out(b):
                for g in range(2):
                    act.wait_ge(s["h2tp"], 2 * b + g + 1)
                    nc.scalar.copy(h2T[:, g * HALF:(g + 1) * HALF], ps_m[g][:]).then_inc(s["h2te"], 1)

            def exp_logits(b):
                act.wait_ge(s["lgx"], b + 1)
                nc.scalar.activation(rt[b][:, 1, :], rt[b][:, 0, :], ACT.Exp).then_inc(s["ex2"], 1)

            def pair(p, par):
                for st in range(NSTEP):
                    expo(p, st, 0)
                    expo(p, st, 1)
                    if last(p):
                        if st == 0:
                            h2T_out(0)
                        if st == 3:
                            exp_logits(0)
                    if st == 0 and not is_first(p):
                        o_out(p - 1, 1)
                    if st == 8:
                        o_out(p, 0)
                    if st in UP_STEPS and not last(p, 2):
                        up_out(p + 2, st - UP_STEPS[0])
                    if st == DEN1 and not is_first(p):
                        den_out(p - 1, 1)
                    if st == DEN0:
                        den_out(p, 0)
                    if st in ACT_ROPE and not last(p, 2):
                        upper_rot(p + 2, ACT_ROPE[st])

            pairs(act, pair)

            def hidden(i, k):
                act.wait_ge(s["hps"], k + 1)
                ge(act, s["yo"], k - 1)
                for c in range(4):
                    ins = nc.scalar.activation(hid[i % 2][:, c * P:(c + 1) * P], ps_s[i % 2][:, c * P:(c + 1) * P], ACT.Relu,
                                               bias=b1_sb[i][:, c:c + 1])
                ins.then_inc(s["hev"], 1)

            def slots_out(i, k):
                act.wait_ge(s["xtp"], k + 1)
                ge(act, s["hps"], k - 1)
                nc.scalar.copy(xT[i % 2], ps_s[2][:, 0:P]).then_inc(s["xte"], 1)

            def y_out(i, k):
                act.wait_ge(s["yo"], k + 1)
                ge(act, d_ys[i // GS], 16 * (k // (2 * GS)))
                nc.scalar.copy(ys[:, i // GS, i % GS, :], ps_s[3][:, 0:D]).then_inc(s["yev"], 1)

            slots_out(0, 0)
            for k in range(NA * GS):
                if k + 1 < NA * GS:
                    slots_out((k + 1) % (2 * GS), k + 1)
                hidden(k % (2 * GS), k)
                if k:
                    y_out((k - 1) % (2 * GS), k - 1)
                if k == T_H2:
                    h2T_out(1)
                    exp_logits(1)
            for k in range(NA * GS, 6 * GS):
                hidden(k % (2 * GS), k)
                if k == NA * GS:
                    y_out((k - 1) % (2 * GS), k - 1)
            with act.Fori(3, NG // 2) as g2:
                for i in range(2 * GS):
                    hidden(i, g2 * (2 * GS) + i)

        @block.gpsimd
        def _(pool):
            V = nc.gpsimd
            V.memset(ident[:], 0.0).then_inc(s["pool"], 1)
            pool.wait_ge(s["pool"], 1)
            V.affine_select(out=ident[:], in_=ident[:], compare_op=ALU.not_equal, fill=1.0, base=0,
                            pattern=[[-1, P]], channel_multiplier=1).then_inc(s["init"], 1)
            V.memset(ones_sq[:], 1.0)
            V.memset(half_neg[:], -0.5)
            V.memset(again[:], 1.0).then_inc(s["pool"], 1)
            V.memset(zero[:], 0.0).then_inc(s["pool"], 1)
            pool.wait_ge(s["pool"], 3)
            V.memset(again[:].rearrange("p (e t) -> p e t", e=E)[:, :, 0:1], 0.0)
            V.affine_select(out=tri[:], in_=ones_sq[:], compare_op=ALU.is_gt, fill=0.0, base=0,
                            pattern=[[1, P]], channel_multiplier=-1)
            V.iota(rev[:], [[-1, E]], base=E, channel_multiplier=0, allow_small_or_imprecise_dtypes=True)
            V.iota(thr[:], [[P, TB]], base=0, channel_multiplier=0, allow_small_or_imprecise_dtypes=True)
            V.iota(tix[:], [[1, NSL]], base=0, channel_multiplier=0,
                   allow_small_or_imprecise_dtypes=True).then_inc(s["init"], 1)

            def split(q):
                pool.wait_ge(d_w, 16 * (q + 1))
                if not is_first(q):
                    pool.wait_ge(s["xps"], x_use("up", q - 1, 3) + 1)
                V.tensor_tensor(wh[:], wu[:], ones_sq[:].unsqueeze(1).to_broadcast([P, 2, P]),
                                ALU.mult).then_inc(s["wsp"], 1)
                pool.wait_ge(s["wsp"], 2 * q + 1)
                V.tensor_tensor(wl[:], wu[:], wh[:].bitcast(F32), ALU.subtract).then_inc(s["wsp"], 1)

            split(0)
            pool.wait_ge(s["nxt0"], 1)
            pool.wait_ge(s["mod1"], 1)
            hb = h0[:, TB:NT, :]
            V.tensor_tensor(hb, hb, mod[:, 1, 1:2, :].to_broadcast([P, TB, D]), ALU.mult).then_inc(s["hmod"], 1)
            pool.wait_ge(s["hmod"], 1)
            V.tensor_tensor(hb, hb, mod[:, 1, 0:1, :].to_broadcast([P, TB, D]), ALU.add).then_inc(s["hmod"], 1)
            split(1)
            pool.wait_ge(s["gev"], 2)
            pool.wait_ge(s["gate"], 1)
            pool.wait_ge(s["lps"], 2)
            for b in range(B):
                V.tensor_tensor(g_all[:, b, :, :], g_raw.rearrange("p (j d) -> p j d", d=D),
                                mod[:, b, 2:3, :].to_broadcast([P, HP, D]), ALU.mult).then_inc(s["gfold"], 1)
            split(2)
            for piece in ROPE:
                rope(pool, 1, *piece)

            def add(p, st, h):
                half, kt = divmod(st, TB)
                pool.wait_ge(s["exp"], n_score(p, st, h))
                if kt == 1:
                    first = probs[:, (st - 1) % 4, h, :]
                    if not is_first(p):
                        pool.wait_ge(s["xps"], x_use("den", p - 1, half) + 1)
                else:
                    first = acc[:, half, h, :]
                    pool.wait_ge(s["add"], n_add(p, st, h) - (1 if last(p) else 2))
                V.tensor_tensor(acc[:, half, h, :], first, probs[:, st % 4, h, :], ALU.add).then_inc(s["add"], 1)

            def inverse_root(b):
                v = sd[:, 0, b * TB:(b + 1) * TB]
                pool.wait_ge(s["lnq"], b + 1)
                V.tensor_tensor(v, v, half_neg[:], ALU.pow).then_inc(s["lnr"], 1)

            def scatter(b):
                pool.wait_ge(d_zero, 16 * B)
                pool.wait_ge(s["sc"], 2 * b + 1)
                pool.wait_ge(s["xwx"], b + 1)
                for k in range(b * TB, (b + 1) * TB):
                    nc.gpsimd.indirect_dma_start(out=xs_dram[b], out_offset=bass.IndirectOffsetOnAxis(ap=slot[:, k:k + 1], axis=0),
                                                 in_=xw[:, k, :], in_offset=None).then_inc(d_sc, 16)

            pool.wait_ge(s["gfold"], 2)

            def pair(p, par):
                for st in range(NSTEP):
                    if st % TB and not (last(p) and st > LAST_ADD):
                        add(p, st, 0)
                        if not last(p):
                            add(p, st, 1)
                    if last(p, 2) and not last(p) and st == 9:
                        inverse_root(0)
                    if st == TB and not last(p, 3):
                        split(p + 3)

            pairs(pool, pair)

            def add_b2(k):
                i = k % (2 * GS)
                pool.wait_ge(s["yev"], k + 1)
                y = ys[:, i // GS, i % GS, :]
                V.tensor_tensor(y, y, b2_sb[i], ALU.add).then_inc(s["yoe"], 1)

            scatter(0)
            for k in range(NA * GS):
                add_b2(k)
                if k == 1:
                    inverse_root(1)
                if k == T_CN:
                    scatter(1)
            for b in range(B):
                groups = NG // B * (b + 1)
                for n in range(2):
                    pool.wait_ge(d_ys[n], 16 * ((groups + 1 - n) // 2))
                for k in range(b * TB, (b + 1) * TB):
                    nc.gpsimd.indirect_dma_start(out=yg[:, k, :], out_offset=None, in_=ys_dram[b],
                                                 in_offset=bass.IndirectOffsetOnAxis(ap=slot[:, k:k + 1], axis=0)
                                                 ).then_inc(d_yg[k // 4], 16)

        @block.vector
        def _(dve):
            seq = [0]
            V = nc.vector

            def then(ins):
                seq[0] += 1
                ins.then_inc(s["dve"], 1)
                dve.wait_ge(s["dve"], seq[0])

            V.memset(ones[:], 1.0)
            V.memset(k2[64:65, :, :, :].bitcast(F32), 1.0).then_inc(s["c"], 1)

            def statistics(src, tiles):
                for k in tiles:
                    ins = V.bn_stats(bst[:, k, :], src[:, k, :])
                then(ins)
                for k in tiles:
                    ins = V.bn_aggr(mv[:, k, :], bst[:, k, :])
                then(ins)
                ts = slice(tiles[0], tiles[-1] + 1)
                V.tensor_scalar_add(sd[:, 0, ts], mv[:, ts, 1], EPS).then_inc(s["rq"], 1)

            def inverse(tiles, n):
                ts = slice(tiles[0], tiles[-1] + 1)
                dve.wait_ge(s["rs"], n)
                then(V.reciprocal(sd[:, 0, ts], sd[:, 1, ts]))

            def normalise(dst, src, tiles):
                for k in tiles:
                    ins = V.tensor_scalar(dst[:, k, :], src[:, k, :], mv[:, k, 0:1], sd[:, 0, k:k + 1],
                                          ALU.subtract, ALU.mult)
                    if dst is hn:
                        ins.then_inc(s["nxt"], 1)
                return ins

            T0, T1 = range(0, TB), range(TB, NT)
            dve.wait_ge(s["silu"], 1)
            dve.wait_ge(d_in, 16)
            then(V.tensor_scalar_add(c_e[:, 1, :], c_e[:, 0, :], 1.0))
            then(V.reciprocal(c_e[:, 2, :], c_e[:, 1, :]))
            then(V.tensor_tensor(c_e[:, 0, :], c_e[:, 2, :], c_col[:], ALU.mult))
            for b in range(B):
                ins = V.tensor_copy(c_rep[:, b, :], c_e[:, 0, b:b + 1].to_broadcast([P, P]))
            ins.then_inc(s["crep"], 1)
            dve.wait_ge(d_x[0], 32)
            statistics(x_sb, T0)
            inverse(T0, 1)
            then(normalise(h0, x_sb, T0))
            dve.wait_ge(s["modsb"], 4)
            V.tensor_scalar_add(mod[:, :, 1:5:3, :], mod[:, :, 1:5:3, :], 1.0).then_inc(s["mod1"], 1)
            dve.wait_ge(s["mod1"], 1)
            hb = h0[:, 0:TB, :]
            then(V.tensor_tensor(hb, hb, mod[:, 0, 1:2, :].to_broadcast([P, TB, D]), ALU.mult))
            then(V.tensor_tensor(hb, hb, mod[:, 0, 0:1, :].to_broadcast([P, TB, D]), ALU.add))
            statistics(h0, T0)
            inverse(T0, 2)
            normalise(hn, h0, T0)
            def lower(n):
                half, w = divmod(n % 4, 2)
                c = slice((n // 4) * S + half * HALF, (n // 4) * S + (half + 1) * HALF)
                dst = (cq, ck)[w][64:128, c]
                dve.wait_ge(s["cev"], n + 1)
                V.tensor_tensor(dst, C_BANK[n % 4][64:128, :], dst.bitcast(F32), ALU.subtract).then_inc(s["csub"], 1)

            dve.wait_ge(d_x[1], 32)
            statistics(x_sb, T1)
            lower(0)
            inverse(T1, 3)
            normalise(h0, x_sb, T1).then_inc(s["nxt0"], 1)
            for n in range(1, 4):
                lower(n)
            for b in range(B):
                gates = mod[:, b, 2:6:3, :]
                then(V.tensor_scalar(g_tmp[:, b, :, :], gates, 0.0, 2.0, ALU.is_ge, ALU.mult))
                then(V.tensor_scalar(g_abs[:, b, :, :], gates, -1.0, 0.25, ALU.mult, ALU.max))
                then(V.tensor_tensor(gates, gates, g_abs[:, b, :, :], ALU.max))
                ins = V.scalar_tensor_tensor(out=gates, in0=g_tmp[:, b, :, :], scalar=-1.0, in1=gates,
                                             op0=ALU.add, op1=ALU.mult)
            ins.then_inc(s["gate"], 1)

            dve.wait_ge(s["hmod"], 2)
            statistics(h0, T1)
            inverse(T1, 4)
            normalise(hn, h0, T1)
            def reduce_max(q, n):
                h, r = divmod(n, 16)
                qt, kh = divmod(r, 2)
                dve.wait_ge(s["maxps"], 32 * q + n + 1)
                if r == 0:
                    ge(dve, s["nm"], 2 * q + h - 1)
                V.reduce_max(mx[:, h, kh, qt:qt + 1], max_bank(q, n)[:], AX.X).then_inc(s["maxr"], 1)

            def neg_max(q, h):
                dve.wait_ge(s["maxr"], 32 * q + 16 * (h + 1))
                ge(dve, d_m[h], 16 * q)
                V.tensor_reduce(nm[:, h, :], mx[:, h, :, :].rearrange("p k t -> p t k"), AX.X, ALU.max,
                                negate=True).then_inc(s["nm"], 1)

            def recip(p, half):
                dve.wait_ge(d_d1, 32 * (2 * p + half + 1))
                V.reciprocal(rc[:, half, :, :], denc[:, half, :, :]).then_inc(s["rcp"], 1)

            def divide(p, half):
                dve.wait_ge(d_d3, 32 * (2 * p + half + 1))
                dve.wait_ge(s["oev"], 2 * p + half + 1)
                V.tensor_tensor(ou[:, half, :], ou[:, half, :], rr[:, half, :], ALU.mult).then_inc(s["mul"], 1)

            def out_add(p, half):
                dve.wait_ge(s["xps"], x_use("out", p, half) + 1)
                xt = x_sb[:, bass.ds((p // HP) * TB + 4 * half, 4), :]
                V.tensor_tensor(xt, xt, ps_x[:].rearrange("p (t d) -> p t d", d=D), ALU.add).then_inc(s["xev"], 1)

            dve.wait_ge(d_rope, 32)
            for piece in ROPE:
                rope(dve, 0, *piece)
            for n in range(4, 8):
                lower(n)
            dve.wait_ge(s["gate"], 1)
            for b in range(B):
                tb = slice(b * TB, (b + 1) * TB)
                dve.wait_ge(s["nxt"], TB * (b + 1))
                then(V.tensor_tensor(h0[:, tb, :], h0[:, tb, :], mod[:, b, 2:3, :].to_broadcast([P, TB, D]), ALU.mult))
                then(V.tensor_tensor(x_sb[:, tb, :], x_sb[:, tb, :], h0[:, tb, :], ALU.add))
            dve.wait_ge(s["lev"], 2)
            for n in range(16):
                reduce_max(0, n)
            neg_max(0, 0)
            for n in range(16, 32):
                reduce_max(0, n)
            neg_max(0, 1)
            def add_sums(st, h):
                half, kt = divmod(st, TB)
                sums = s["adx" if h else "add"]
                dve.wait_ge(s["exp"], n_score(NPAIR - 1, st, h))
                if kt == 1:
                    first = probs[:, (st - 1) % 4, h, :]
                    dve.wait_ge(s["xps"], x_use("den", NPAIR - 2, half) + 1)
                else:
                    first = acc[:, half, h, :]
                    dve.wait_ge(sums, n_add(NPAIR - 1, st, h) - 1)
                V.tensor_tensor(acc[:, half, h, :], first, probs[:, st % 4, h, :], ALU.add).then_inc(sums, 1)

            def block_stats(tiles):
                for k in tiles:
                    ins = V.bn_stats(bst[:, k, :], x_sb[:, k, :])
                then(ins)

            def block_norm(b):
                tiles, ts = range(b * TB, (b + 1) * TB), slice(b * TB, (b + 1) * TB)
                for k in tiles:
                    ins = V.bn_aggr(mv[:, k, :], bst[:, k, :])
                then(ins)
                V.tensor_scalar_add(sd[:, 0, ts], mv[:, ts, 1], EPS).then_inc(s["lnq"], 1)

            def block_out(b):
                ts = slice(b * TB, (b + 1) * TB)
                wide = lambda m: mod[:, b, m:m + 1, :].to_broadcast([P, TB, D])
                dve.wait_ge(s["lnr"], b + 1)
                for k in range(b * TB, (b + 1) * TB):
                    ins = V.tensor_scalar(h2[:, k, :], x_sb[:, k, :], mv[:, k, 0:1], sd[:, 0, k:k + 1],
                                          ALU.subtract, ALU.mult)
                then(ins)
                then(V.tensor_tensor(h2[:, ts, :], h2[:, ts, :], wide(4), ALU.mult))
                V.tensor_tensor(h2[:, ts, :], h2[:, ts, :], wide(3), ALU.add).then_inc(s["h2x"], 1)
                dve.wait_ge(s["h2x"], b + 1)

            tok = lambda a: a.unsqueeze(2).to_broadcast([P, TB, E])
            row = lambda a: a.unsqueeze(1).to_broadcast([P, TB, E])
            by_tok = lambda a: a.rearrange("p (t e) -> p t e", e=E)
            by_exp = lambda a: a.rearrange("p (e t) -> p e t", e=E)

            def judge(b):
                r = [by_tok(rt[b][:, n, :]) for n in range(8)]
                dve.wait_ge(s["lgp"], b + 1)
                if b == 0:
                    dve.wait_ge(d_gw, 32)
                    dve.wait_ge(s["init"], 2)
                then(V.tensor_tensor(r[2], by_tok(ps_m[0][:, 0:TB * E]), row(gb_sb[:]), ALU.add))
                then(V.reduce_max(rs[:, 0, :], r[2], AX.X))
                V.tensor_tensor(r[0], r[2], tok(rs[:, 0, :]), ALU.subtract).then_inc(s["lgx"], 1)

            def choose(b):
                r = [by_tok(rt[b][:, n, :]) for n in range(8)]
                dve.wait_ge(s["ex2"], b + 1)
                then(V.reduce_sum(rs[:, 1, :], r[1], AX.X))
                then(V.reciprocal(rs[:, 2, :], rs[:, 1, :]))
                then(V.tensor_tensor(r[3], r[1], tok(rs[:, 2, :]), ALU.mult))
                then(V.reduce_max(rs[:, 3, :], r[3], AX.X))
                then(V.tensor_tensor(r[4], r[3], tok(rs[:, 3, :]), ALU.is_equal))
                then(V.tensor_tensor(r[4], r[4], row(rev[:]), ALU.mult))
                then(V.reduce_max(rs[:, 4, :], r[4], AX.X))
                then(V.tensor_tensor(r[5], r[4], tok(rs[:, 4, :]), ALU.is_equal))
                then(V.scalar_tensor_tensor(out=r[6], in0=r[5], scalar=-2.0, in1=r[3], op0=ALU.mult, op1=ALU.add))
                then(V.reduce_max(rs[:, 5, :], r[6], AX.X))
                then(V.tensor_tensor(r[7], r[6], tok(rs[:, 5, :]), ALU.is_equal))
                then(V.tensor_tensor(r[7], r[7], row(rev[:]), ALU.mult))
                then(V.reduce_max(rs[:, 6, :], r[7], AX.X))
                then(V.tensor_tensor(rs[:, 7, :], rs[:, 6, :], rs[:, 4, :], ALU.is_lt))
                then(V.scalar_tensor_tensor(out=rs[:, 7, :], in0=rs[:, 5, :], scalar=0.0, in1=rs[:, 7, :],
                                            op0=ALU.is_gt, op1=ALU.mult))
                V.tensor_tensor(rs[:, 5, :], rs[:, 5, :], rs[:, 7, :], ALU.mult)
                V.tensor_tensor(rs[:, 6, :], rs[:, 6, :], rs[:, 7, :], ALU.mult)
                then(V.tensor_scalar(rs[:, 8, :], rs[:, 7, :], -1.0, 1.0, ALU.mult, ALU.add))
                V.tensor_tensor(rs[:, 9, :], rs[:, 3, :], rs[:, 8, :], ALU.mult)
                then(V.tensor_tensor(rs[:, 4, :], rs[:, 4, :], rs[:, 8, :], ALU.mult))
                V.tensor_tensor(rs[:, 10, :], rs[:, 9, :], rs[:, 5, :], ALU.add)
                then(V.tensor_tensor(rs[:, 11, :], rs[:, 4, :], rs[:, 6, :], ALU.add))
                one_hot, count = rt[b][:, 8, :], rt[b][:, 9, :]
                then(V.tensor_tensor(by_exp(one_hot), rev[:].unsqueeze(2).to_broadcast([P, E, TB]),
                                     rs[:, 11, :].unsqueeze(1).to_broadcast([P, E, TB]), ALU.is_equal))
                V.tensor_tensor_scan(count, again[:], one_hot, 0.0, ALU.mult, ALU.add).then_inc(s["cnt"], 1)
                dve.wait_ge(s["cnt"], b + 1)

            def scaled(b):
                for k in range(b * TB, (b + 1) * TB):
                    ins = V.tensor_scalar(xw[:, k, :], h2[:, k, :], rs[:, 10, k - b * TB:k - b * TB + 1], None, ALU.mult)
                ins.then_inc(s["xwx"], 1)

            def find_slots(b):
                one_hot, count, at = rt[b][:, 8, :], rt[b][:, 9, :], rt[b][:, 10, :]
                dve.wait_ge(s["pre"], b + 1)
                then(V.tensor_copy(cn[:, 0:2, :].rearrange("p a e -> p (a e)"), ps_m[1][:, 0:2 * E]))
                then(V.tensor_tensor(cmp3[:, :, 0:TB], cn[:, 1, :].unsqueeze(2).to_broadcast([P, E, TB]),
                                     thr[:].unsqueeze(1).to_broadcast([P, E, TB]), ALU.is_gt))
                then(V.reduce_sum(cn[:, 2, :], cmp3[:, :, 0:TB], AX.X))
                then(V.tensor_tensor_scan(cn[:, 3, :], ones_sq[:, 0:E], cn[:, 2, :], 0.0, ALU.mult, ALU.add))
                then(V.tensor_tensor(cn[:, 4, :], cn[:, 3, :], cn[:, 2, :], ALU.subtract))
                then(V.scalar_tensor_tensor(out=cn[:, 5, :], in0=cn[:, 4, :], scalar=float(P), in1=cn[:, 0, :],
                                            op0=ALU.mult, op1=ALU.add))
                then(V.tensor_tensor(by_exp(at), by_exp(count), cn[:, 5, :].unsqueeze(2).to_broadcast([P, E, TB]), ALU.add))
                then(V.tensor_tensor(at, at, one_hot, ALU.mult))
                then(V.reduce_sum(rs[:, 0, :], at.rearrange("p (e t) -> p t e", e=E), AX.X))
                V.tensor_scalar_add(slot[:, b * TB:(b + 1) * TB], rs[:, 0, :], -1.0).then_inc(s["sc"], 1)
                then(V.tensor_tensor(cmp3[:], cn[:, 3, :].unsqueeze(2).to_broadcast([P, E, NSL]),
                                     tix[:].unsqueeze(1).to_broadcast([P, E, NSL]), ALU.is_le))
                then(V.reduce_sum(tcount[:], cmp3[:].rearrange("p e t -> p t e"), AX.X))
                V.tensor_scalar(eid[:, b * NSL:(b + 1) * NSL], tcount[:], float(E - 1), None, ALU.min).then_inc(s["sc"], 1)
                dve.wait_ge(s["sc"], 2 * b + 2)

            def pair(p, par):
                rest = [] if last(p, 2) else list(ROPE)

                for st in range(NSTEP):
                    pieces = ROPE_STEPS.get(st, 0)
                    if last(p) and st % TB:
                        add_sums(st, 1)
                        if st > LAST_ADD:
                            add_sums(st, 0)
                    if last(p, 2) and not last(p):
                        if st == 7:
                            block_stats(T0)
                            block_norm(0)
                        if st == 14:
                            block_out(0)
                    if last(p):
                        if st == 3:
                            judge(0)
                        if st == 5:
                            choose(0)
                        if st == 7:
                            scaled(0)
                        if st == 9:
                            find_slots(0)
                    if not is_first(p):
                        if st == 1:
                            divide(p - 1, 0)
                        if st == 8:
                            recip(p - 1, 1)
                        if st == 11:
                            divide(p - 1, 1)
                    if not last(p):
                        for n in range(sum(MAXN[:st]), sum(MAXN[:st + 1])):
                            reduce_max(p + 1, n)
                            if n % 16 == 15:
                                neg_max(p + 1, n // 16)
                            if rest and pieces:
                                rope(dve, p + 2, *rest.pop(0))
                                pieces -= 1
                    for _ in range(pieces):
                        if rest:
                            rope(dve, p + 2, *rest.pop(0))
                    if not is_first(p):
                        if st == OUT0:
                            out_add(p - 1, 0)
                        if st == OUT1:
                            out_add(p - 1, 1)
                    if st == 13:
                        recip(p, 0)
                while rest:
                    rope(dve, p + 2, *rest.pop(0))

            pairs(dve, pair)
            p = NPAIR - 1
            divide(p, 0)
            dve.wait_ge(s["xps"], x_use("den", p, 1) + 1)
            V.reciprocal(rr[:, 1, :], ps_x[:]).then_inc(s["xev"], 1)
            dve.wait_ge(s["xev"], x_use("den", p, 1) + 1)
            dve.wait_ge(s["pv"], 16 * NPAIR)
            V.tensor_tensor(ou[:, 1, :], ps_o[:], rr[:, 1, :], ALU.mult).then_inc(s["mul"], 1)
            for half in range(2):
                out_add(p, half)
                dve.wait_ge(s["xev"], x_use("out", p, half) + 1)
                block_stats(T1[4 * half:4 * half + 4])
            block_norm(1)
            block_out(1)
            judge(1)
            choose(1)
            scaled(1)
            find_slots(1)

            def slots_out(i, k):
                dve.wait_ge(s["xtp"], k + 1)
                dve.wait_ge(s["hps"], k - 1)
                V.tensor_copy(xT[i % 2], ps_s[2][:, 0:P]).then_inc(s["xte"], 1)

            def y_out(i, k):
                dve.wait_ge(s["yo"], k + 1)
                dve.wait_ge(d_ys[i // GS], 16 * (k // (2 * GS)))
                V.tensor_tensor(ys[:, i // GS, i % GS, :], ps_s[3][:, 0:D], b2_sb[i], ALU.add).then_inc(s["yev"], 1)

            def tiles(k0, first, i0=0):
                slots_out(i0, k0 + i0)
                for i in range(i0, 2 * GS):
                    if i < 2 * GS - 1:
                        slots_out(i + 1, k0 + i + 1)
                    if i > i0 or not first:
                        y_out((i - 1) % (2 * GS), k0 + i - 1)

            tiles(4 * GS, True, GS)
            with dve.Fori(3, NG // 2) as g2:
                tiles(g2 * (2 * GS), False)
            y_out(2 * GS - 1, NG * GS - 1)

            for g in range(4):
                b = g // 2
                ts = slice(4 * g, 4 * g + 4)
                dve.wait_ge(d_yg[g], 16 * 4)
                then(V.tensor_tensor(yg[:, ts, :], yg[:, ts, :], mod[:, b, 5:6, :].to_broadcast([P, 4, D]), ALU.mult))
                V.tensor_tensor(x_sb[:, ts, :], x_sb[:, ts, :], yg[:, ts, :], ALU.add).then_inc(s["fin"], 1)

        @block.sync
        def _(sp):
            sp.dma_start(c_col[:], t["c_t"]).then_inc(d_in, 16)
            for g in range(4):
                sp.dma_start(x_sb[:, 4 * g:4 * g + 4, :],
                             t["x"][4 * g * P:4 * (g + 1) * P, :].rearrange("(t p) d -> p t d", p=P)).then_inc(d_x[g // 2], 16)
                if g == 1:
                    sp.dma_start(wmod_sb[:], t["wmod"]).then_inc(d_mod, 16)
            sp.dma_start(wuv_sb, t["wuv"]).then_inc(d_vo, 16)
            sp.dma_start(wo_sb, t["wo"]).then_inc(d_vo, 16)
            sp.dma_start(lns[:], t["lns"]).then_inc(d_lns, 16)
            sp.dma_start(wd_sb[:], t["wd"]).then_inc(d_wd, 16)

            def weights(q):
                if isinstance(q, int):
                    ge(sp, s["wsp"], 2 * q)
                    sp.dma_start(wu[:], t["wqk"][q % HP]).then_inc(d_w, 16)
                    return
                ge_all(sp,
                       (s["wsp"], 2 * q),
                       (s["c"], 1))
                sp.dma_start(wu[:], t["wqk"][q % HP]).then_inc(d_w, 16)

            def values(q, par):
                ge_all(sp,
                       (s["pv"], 16 * (q - 1)),
                       (s["lev"], 2))
                b = q // HP
                sp.dma_start(cv[:, par, :, :], c_all[:, bass.ds(b * TB, TB), :]).then_inc(d_cv, 16)

            def swap(q, w):
                gone = [(d_ql[h], 16 * q) for h in range(2)]
                if w == 1:
                    gone = [(d_pq[h], 64 * q) for h in range(2)] + [(d_kh[h], 16 * q) for h in range(2)]
                ge_all(sp,
                       (s["xev"], x_use("up", q, 2 * w + 1) + 1),
                       *gone)
                for a in range(4):
                    c = a ^ 1
                    sp.dma_start(vs[32 * a:32 * a + 32, w, :], us[32 * c:32 * c + 32, w, :]).then_inc(d_swap[w], 16)

            def place(q, par):
                ge_all(sp,
                       (s["rope"], NROPE * q + ROPE.index((1, 4)) + 1),
                       (s["scores"], 32 * (q - 1)))
                for h in range(2):
                    r = slice(64 * h, 64 * h + 64)
                    q_hi, k_hi = [xh[r, w, :].bitcast(F32) for w in range(2)]
                    for n, (dst, src) in enumerate(((qq[0:64], q_hi), (qq[64:128], q_hi), (kk[0:64], k_hi), (kk[64:128], vs[r, 1, :]))):
                        if h == 0 and n == 2:
                            sp.wait_ge(s["rope"], NROPE * (q + 1))
                        sp.dma_start(dst[:, par, h, :].bitcast(F32), src).then_inc(d_pq[h], 16)
                    if h == 0:
                        for i in range(2):
                            sp.dma_start(q2[0:64, par, i, :].bitcast(F32), vs[64 * i:64 * i + 64, 0, :]).then_inc(d_ql[i], 16)

            def place_k(q, par):
                for h in range(2):
                    sp.dma_start(k2[0:64, par, h, :].bitcast(F32), xh[64 * h:64 * h + 64, 1, :].bitcast(F32)).then_inc(d_kh[h], 16)

            def max_row(q, par, h):
                ge_all(sp,
                       (s["nm"], 2 * q + h + 1),
                       (s["scores"], 32 * (q - 1)))
                sp.dma_start(q2[64:65, par, h, :].bitcast(F32), nm[:, h, :].bitcast(F32)).then_inc(d_m[h], 16)

            def den_cols(p, half):
                sp.wait_ge(s["xev"], x_use("den", p, half) + 1)
                for h in range(2):
                    sp.dma_start(denc[:, half, h, :], den[32 * h:32 * h + 1, :]).then_inc(d_d1, 16)

            def inv_rows(p, half):
                sp.wait_ge(s["rcp"], 2 * p + half + 1)
                sp.dma_start(rd_dram[half].rearrange("h (p f) -> p h f", f=4), rc[:, half, :, :]).then_inc(d_d2, 16)

            def inv_spread(p, half):
                sp.wait_ge(d_d2, 16 * (2 * p + half + 1))
                for h in range(2):
                    sp.dma_start(rr[64 * h:64 * h + 64, half, :],
                                 rd_dram[half, h:h + 1, :].to_broadcast([64, HALF])).then_inc(d_d3, 16)

            weights(0)
            weights(1)
            sp.dma_start(cos_sb, t["cos"]).then_inc(d_rope, 16)
            sp.dma_start(sin_sb, t["sin"]).then_inc(d_rope, 16)
            sp.dma_start(gw_sb[:], t["gate_w"]).then_inc(d_gw, 16)
            sp.dma_start(gb_sb[:], t["gate_b"].to_broadcast([P, E])).then_inc(d_gw, 16)
            sp.wait_ge(s["init"], 2)
            for b in range(B):
                sp.dma_start(xs_dram[b].rearrange("(t p) d -> p t d", p=P),
                             zero[:].unsqueeze(1).to_broadcast([P, NSL, D])).then_inc(d_zero, 16)
            swap(0, 0)
            swap(0, 1)
            place(0, 0)
            place_k(0, 0)
            weights(2)
            values(0, 0)
            swap(1, 0)
            swap(1, 1)
            for h in range(2):
                max_row(0, 0, h)

            def pair(p, par):
                if not last(p):
                    place(p + 1, 1 - par)
                if not last(p, 2):
                    swap(p + 2, 0)
                if not last(p):
                    place_k(p + 1, 1 - par)
                if not last(p, 2):
                    swap(p + 2, 1)
                if not last(p):
                    values(p + 1, 1 - par)
                if not last(p, 3):
                    weights(p + 3)
                if not is_first(p):
                    den_cols(p - 1, 1)
                if not last(p):
                    max_row(p + 1, 1 - par, 0)
                if not is_first(p):
                    inv_rows(p - 1, 1)
                    inv_spread(p - 1, 1)
                den_cols(p, 0)
                if not last(p):
                    max_row(p + 1, 1 - par, 1)
                inv_rows(p, 0)
                inv_spread(p, 0)

            pairs(sp, pair)

            def expert_data(g, par, i):
                k = g * GS + i
                by_pool = isinstance(g, int) and g - 2 < NA
                if isinstance(g, int):
                    if k == 2:
                        sp.wait_ge(s["pv"], 16 * NPAIR)
                        wait_adds(sp, NPAIR - 1, NSTEP - 1, (0, 1))
                    if k == 5:
                        sp.wait_ge(s["xps"], x_use("out", NPAIR - 1, 1) + 1)
                ge_all(sp,
                       (s["yoe" if by_pool else "yev"], k - 2 * GS + 1),
                       (s["sc"], 2))
                e = sp.value_load(eid[0:1, bass.ds(k, 1)], min_val=0, max_val=E - 1)
                sp.dma_start(wb[par * GS + i], t["experts"][e]).then_inc(d_wp[par * GS + i], 16)

            def rows(dram, g):
                b = 0 if isinstance(g, int) and g < NG // B else 1
                return dram[b][bass.ds((g - b * (NG // B)) * (GS * P), GS * P), :].rearrange("(t p) d -> p t d", p=P)

            def slots_in(g, par):
                ge_all(sp,
                       (s["xtp"], GS * (g - 1)),
                       (d_sc, 16 * TB * (g // (NG // B) + 1)),
                       (s["sc"], 2))
                sp.dma_start(xs[:, par, :, :], rows(xs_dram, g)).then_inc(d_xs[par], 16)

            def store(g, par):
                if isinstance(g, int) and g < NA:
                    sp.wait_ge(s["yoe"], GS * (g + 1))
                else:
                    ge_all(sp, (s["yev"], GS * (g + 1)), (s["sc"], 4))
                sp.dma_start(rows(ys_dram, g), ys[:, par, :, :]).then_inc(d_ys[par], 16)

            def group(g, par, first=False):
                expert_data(g, par, 0)
                slots_in(g, par)
                expert_data(g, par, 1)
                expert_data(g, par, 2)
                if not first:
                    store(g - 2, par)

            sp.wait_ge(s["sc"], 2)
            for g in range(NG):
                if g == NG // B:
                    sp.wait_ge(s["sc"], 4)
                group(g, g % 2, g < 2)
            store(NG - 2, 0)
            store(NG - 1, 1)
            for g in range(4):
                sp.wait_ge(s["fin"], g + 1)
                sp.dma_start(out[4 * g * P:4 * (g + 1) * P, :].rearrange("(t p) d -> p t d", p=P),
                             x_sb[:, 4 * g:4 * g + 4, :]).then_inc(d_out, 16)
            sp.wait_ge(d_out, 64)


def tables():
    inv_freq = 1.0 / 10000.0 ** (np.arange(0, DH, 2, dtype=np.float32) / DH)
    freqs = np.outer(np.arange(S, dtype=np.float32), inv_freq)
    cos = np.concatenate([np.cos(freqs), np.cos(freqs)], -1)[:, ::2].T
    sin = np.concatenate([np.sin(freqs), np.sin(freqs)], -1)[:, ::2].T
    return (np.ascontiguousarray(np.concatenate([cos] * 4), dtype=np.float32),
            np.ascontiguousarray(np.concatenate([-sin, sin] * 2), dtype=np.float32))


def layout(i):
    def up(w):
        w = np.asarray(w).reshape(HP, 2, DH // 2, 2, LAT).transpose(0, 4, 1, 3, 2).reshape(HP, LAT, 2 * DH)
        return np.concatenate([w, w], 1)
    cos, sin = tables()
    f = lambda a: np.ascontiguousarray(np.asarray(a))
    return {
        "x": f(i["L0_attn_x"]).reshape(B * S, D),
        "c_t": f(np.asarray(i["L0_c"]).T),
        "wmod": f(i["L0_wmod"]),
        "wd": f(np.stack([np.concatenate([np.asarray(w)] * 2) for w in (i["L0_attn_w_down_q"], i["L0_attn_w_down_kv"])]
                         ).transpose(2, 0, 1)),
        "lns": f(np.stack([np.asarray(i["L0_attn_ln_scale"]), np.asarray(i["L0_attn_ln_bias"])], 1)),
        "wqk": f(np.stack([up(i["L0_attn_w_up_q"]), up(i["L0_attn_w_up_k"])], 2)),
        "cos": cos, "sin": sin,
        "wuv": f(np.asarray(i["L0_attn_w_up_v"]).reshape(H, DH, LAT).transpose(1, 0, 2)),
        "wo": f(np.asarray(i["L0_attn_w_out"]).T.reshape(H, DH, D).transpose(1, 0, 2)),
        "gate_w": f(i["L0_ffn_gate_w"]), "gate_b": f(i["L0_ffn_gate_b"]).reshape(1, E),
        "experts": f(np.concatenate([np.asarray(i["L0_ffn_w1"]),
                                     np.asarray(i["L0_ffn_w2"]).reshape(E, 4, P, D).transpose(0, 2, 1, 3).reshape(E, P, 4 * D),
                                     np.asarray(i["L0_ffn_b1"]).reshape(E, 4, P).transpose(0, 2, 1),
                                     np.broadcast_to(np.asarray(i["L0_ffn_b2"])[:, None, :], (E, P, D))], 2)),
    }


def kernel(**inputs):
    import concourse.bacc as bacc
    from concourse.bass_utils import run_bass_kernel_spmd

    nc = bacc.Bacc("TRN2", target_bir_lowering=False, num_devices=1)
    arrays = layout(inputs)
    aps = {n: nc.dram_tensor(f"in_{n}", a.shape, mybir.dt.from_np(a.dtype), kind="ExternalInput").ap()
           for n, a in arrays.items()}
    out = nc.dram_tensor("out_dram", [B * S, D], F32, kind="ExternalOutput").ap()
    build(nc, aps, out)
    r = run_bass_kernel_spmd(nc, [{f"in_{n}": a for n, a in arrays.items()}], core_ids=[0])
    return r.results[0]["out_dram"].reshape(B, S, D)
```

```python
from contextlib import ExitStack

import numpy as np

import concourse.bass as bass
from concourse import mybir

ALU = mybir.AluOpType
ACT = mybir.ActivationFunctionType
AX = mybir.AxisListType
F32 = mybir.dt.float32
F32R = mybir.dt.float32r
I32 = mybir.dt.int32

P = 128
B, S, D = 2, 1024, 128
H, DH, LAT = 16, 64, 64
NT = B * S // P
TB = S // P
HP = H // 2
NPAIR = B * HP
HALF = 512
NSTEP = 2 * TB
E, F = 8, 512
NSL = TB + E - 1
GS = 3
NG = B * NSL // GS
NA = NG // B
WROW = 2 * F + F // P + D
PARTS = [(0, 4), (4, 8), (8, 12), (12, 15), (15, 16)]
EPS = 1e-5
SCALE = 0.125


def ge(eng, sem, value):
    if not (isinstance(value, int) and value <= 0):
        eng.wait_ge(sem, value)


def ge_all(eng, *waits):
    for _, v in waits:
        if not isinstance(v, int):
            eng.compute_val(v)
    for sem, v in waits:
        ge(eng, sem, v)


def build(nc, t, out):
    ctx = ExitStack()
    with ctx:
        def sb(name, shape, dt=F32):
            return ctx.enter_context(nc.sbuf_tensor(name, shape, dt))

        def pb(name, shape=(P, HALF), dt=F32):
            return ctx.enter_context(nc.psum_tensor(name, list(shape), dt))

        def sem(name):
            return ctx.enter_context(nc.semaphore(name))

        x_sb = sb("x_sb", [P, NT, D])
        h0 = sb("h0", [P, NT, D])
        hn = sb("hn", [P, NT, D])
        hT = sb("hT", [P, B * S])
        cq = sb("cq", [P, B * S], F32R)
        ck = sb("ck", [P, B * S], F32R)
        c_all = sb("c_all", [P, NT, LAT])
        ident = sb("ident", [P, P])
        ones = sb("ones", [P, 64])
        wmod_sb = sb("wmod_sb", [P, 6 * D])
        wd_sb = sb("wd_sb", [P, 2, 2 * LAT])
        c_col = sb("c_col", [P, B])
        c_e = sb("c_e", [P, 3, B])
        c_rep = sb("c_rep", [P, B, P])
        mod = sb("mod", [P, B, 6, D])
        lns = sb("lns", [P, 2])
        bst = sb("bst", [P, NT, 6])
        mv = sb("mv", [P, NT, 2])
        sd = sb("sd", [P, 2, NT])
        rot = sb("rot", [P, 2, S])
        cos_sb, sin_sb = rot[:, 0, :], rot[:, 1, :]

        wu = sb("wu", [P, 2, P])
        wh = sb("wh", [P, 2, P], F32R)
        wl = sb("wl", [P, 2, P], F32R)
        us = sb("us", [P, 2, S])
        vs = sb("vs", [P, 2, S])
        xh = sb("xh", [P, 2, S], F32R)
        qq = sb("qq", [P, 2, 2, S], F32R)
        kk = sb("kk", [P, 2, 2, S], F32R)
        q2 = sb("q2", [P, 2, 2, S], F32R)
        k2 = sb("k2", [P, 2, 2, S], F32R)
        cv = sb("cv", [P, 2, TB, LAT])
        probs = sb("probs", [P, 4, 2, HALF])
        acc = sb("acc", [P, 2, 2, HALF])
        mx = sb("mx", [P, 2, 2, TB])
        nm = sb("nm", [P, 2, TB], F32R)
        den = sb("den", [64, HALF])
        denc = sb("denc", [P, 2, 2, 4])
        rc = sb("rc", [P, 2, 2, 4])
        rr = sb("rr", [P, 2, HALF])
        ou = sb("ou", [P, 2, HALF])

        rd_dram = nc.dram_tensor("rd_dram", [2, 2, HALF], F32, kind="Internal").ap()
        xs_dram = [nc.dram_tensor(f"xs_dram{b}", [NSL * P, D], F32, kind="Internal").ap() for b in range(B)]
        ys_dram = [nc.dram_tensor(f"ys_dram{b}", [NSL * P, D], F32, kind="Internal").ap() for b in range(B)]

        flat = lambda a: a.rearrange("p a n -> p (a n)")
        wuv_sb = us[0:64, 0, :].rearrange("p (h l) -> p h l", h=H)
        wo_sb = flat(vs[0:64, :, :]).rearrange("p (h d) -> p h d", h=H)
        g_tmp, g_abs = [probs[:, n, 0, :].rearrange("p (b m d) -> p b m d", b=B, m=2) for n in range(2)]
        g_raw = acc[:].rearrange("p a h n -> p (a h n)")[:, 0:HP * D]
        g_all = hT[:].rearrange("p (b j d) -> p b j d", b=B, d=D)
        h2, xw, yg = hn, h0, hn
        h2T = c_all[:].rearrange("p t l -> p (t l)")
        p_flat = probs[:].rearrange("p s h n -> p (s h n)")
        wb = ([flat(us[:])[:, 0:WROW], flat(rot[:])[:, 0:WROW]] + [p_flat[:, n * WROW:(n + 1) * WROW] for n in range(3)]
              + [hT[:, 0:WROW]])
        w1_sb = [x[:, 0:F] for x in wb]
        w2_sb = [x[:, F:2 * F] for x in wb]
        b1_sb = [x[:, 2 * F:2 * F + F // P] for x in wb]
        b2_sb = [x[:, WROW - D:WROW] for x in wb]
        xs = flat(xh[:].bitcast(F32))[:, 0:2 * GS * D].rearrange("p (g t d) -> p g t d", g=2, d=D)
        ys = flat(vs[:])[:, 0:2 * GS * D].rearrange("p (g t d) -> p g t d", g=2, d=D)
        hid = [acc[:, 0, n, :] for n in range(2)]
        xT = [flat(vs[:])[:, (2 * GS + n) * D:(2 * GS + n + 1) * D] for n in range(2)]
        rt = [x.rearrange("p (a n) -> p a n", a=12) for x in (flat(vs[:])[:, 2 * S - 12 * TB * E:2 * S], wmod_sb[:])]

        gw_sb = sb("gw_sb", [P, E])
        gb_sb = sb("gb_sb", [P, E])
        zero = sb("zero", [P, D])
        tri = sb("tri", [P, P])
        ones_sq = sb("ones_sq", [P, P])
        half_neg = sb("half_neg", [P, TB])
        rev = sb("rev", [P, E])
        thr = sb("thr", [P, TB])
        tix = sb("tix", [P, NSL])
        again = sb("again", [P, E * TB])
        rs = sb("rs", [P, 12, TB])
        cn = sb("cn", [P, 6, E])
        cmp3 = sb("cmp3", [P, E, NSL])
        tcount = sb("tcount", [P, NSL])
        slot = sb("slot", [P, NT], I32)
        eid = sb("eid", [P, B * NSL], I32)

        ps_s = [pb(f"ps_s{n}") for n in range(4)]
        ps_m = [pb(f"ps_m{n}") for n in range(2)]
        ps_o = pb("ps_o")
        ps_x = pb("ps_x")

        signals = {
            "cond_exp": "exp(-c) is there (scalar)",
            "cond_wide": "silu(c) as equal columns (vector)",
            "mod_product": "a part of the modulations is in PSUM (tensor)",
            "mod_copied": "and in SBUF (scalar)",
            "mod_scales": "1 is added to the scales (vector)",
            "gates": "the gates are kept away from zero (vector)",
            "g_product": "half of the folded output weights is in PSUM (tensor)",
            "g_copied": "and in SBUF (scalar)",
            "g_gated": "one batch's, times its gate (gpsimd)",
            "var_ready": "variances of a batch's tokens, before the attention (vector)",
            "dev_ready": "their roots (scalar)",
            "norm1": "batch 1's x is normalised (vector)",
            "modulated": "a step of batch 1's modulation (gpsimd)",
            "tile_norm": "a tile's second normalisation (vector)",
            "features_T": "four tiles transposed (tensor)",
            "features": "and scaled and biased in SBUF (scalar)",
            "latent_product": "a part of the latents (tensor)",
            "latent_hi": "its upper bits (scalar)",
            "latent_lo": "its lower bits (vector)",
            "value_product": "a batch's latents with tokens on partitions (tensor)",
            "values": "and in SBUF (scalar)",
            "constants": "vector's constants",
            "tables": "gpsimd's constants",
            "pool_step": "gpsimd's steps that read each other",
            "vector_step": "vector's steps that read each other",
            "weights_split": "a step of the split of a pair's up projections (gpsimd)",
            "x_product": "a use of ps_x: its products are done (tensor)",
            "x_free": "and it is read (scalar or vector)",
            "rotated": "a step of a pair's rotation (vector; gpsimd for pair 1)",
            "rotated_hi": "upper bits of a part of the rotated q and k (scalar)",
            "max_product": "a tile of scores for the maxima (tensor)",
            "max_reduced": "its rows' maxima (vector)",
            "max_row": "a head's maxima, negated (vector)",
            "scores": "a tile of scores less the maximum (tensor)",
            "probs": "its probabilities (scalar)",
            "sums": "values times a step's probabilities, both heads (tensor)",
            "added": "a tile is in the sums of probabilities (gpsimd)",
            "added_last": "the same for the last pair's head 1 (vector)",
            "inverses": "denominators inverted (vector)",
            "sums_copied": "latent sums of half a pair are in SBUF (scalar)",
            "divided": "and divided (vector)",
            "var2_ready": "variances after the attention (vector)",
            "inv2_ready": "their inverse roots (gpsimd)",
            "norm2": "a batch's second block input (vector)",
            "norm2_T": "half of it transposed (tensor)",
            "norm2_features": "and in SBUF (scalar)",
            "logit_product": "a batch's logits (tensor)",
            "logits": "biased, less their maximum (vector)",
            "logit_exp": "their exponentials (scalar)",
            "counts": "running counts of the experts' tokens (vector)",
            "counts_before": "summed over partitions (tensor)",
            "weighted": "a batch's tokens times their score (vector)",
            "slots": "first a batch's slots, then its tiles' experts (vector)",
            "slots_T": "a tile of slots transposed (tensor)",
            "slots_in": "and in SBUF (scalar, then vector)",
            "hidden_product": "a tile's hidden layer (tensor)",
            "hidden": "with bias and relu (scalar)",
            "y_product": "a tile's outputs (tensor)",
            "y_copied": "and in SBUF (scalar, then vector with b2)",
            "y_biased": "b2 added to them (gpsimd)",
            "done": "a part of the result (vector)",
        }
        s = {n: sem("s_" + n) for n in signals}
        c_in, wmod_in, lns_in, down_in, rot_in, vo_in, gatew_in = [
            sem(n) for n in ("c_in", "wmod_in", "lns_in", "down_in", "rot_in", "vo_in", "gatew_in")]
        x_in = [sem(f"x_in{b}") for b in range(B)]
        up_in = sem("up_in")
        cv_in = sem("cv_in")
        swapped = [sem(f"swapped{w}") for w in range(2)]
        qk_placed = [sem(f"qk_placed{h}") for h in range(2)]
        qlo_placed = [sem(f"qlo_placed{h}") for h in range(2)]
        khi_placed = [sem(f"khi_placed{h}") for h in range(2)]
        row_placed = [sem(f"row_placed{h}") for h in range(2)]
        den_cols_in, inv_out, inv_in = sem("den_cols_in"), sem("inv_out"), sem("inv_in")
        zeros_out, scattered = sem("zeros_out"), sem("scattered")
        group_in = [sem(f"group_in{n}") for n in range(2)]
        expert_in = [sem(f"expert_in{n}") for n in range(2 * GS)]
        group_out = [sem(f"group_out{n}") for n in range(2)]
        gathered = [sem(f"gathered{g}") for g in range(len(PARTS))]
        result_out = sem("result_out")

        block = ctx.enter_context(nc.Block())

        def n_score(p, st, h):
            return 32 * p + 2 * st + h + 1

        def n_add(p, st, h):
            half, kt = divmod(st, TB)
            if last(p):
                return (0 if h else 28 * p) + 7 * half + max(kt, 1)
            return 28 * p + 14 * half + 2 * (max(kt, 1) - 1) + h + 1

        def wait_adds(eng, p, st, heads):
            for h in heads:
                if last(p) and h == 1:
                    eng.wait_ge(s["added_last"], n_add(p, st, h))
                elif last(p) or h == heads[-1]:
                    eng.wait_ge(s["added"], n_add(p, st, h))

        def x_use(what, p, k):
            place = {("up", 0): 0, ("up", 1): 1, ("up", 2): 2, ("up", 3): 3, ("den", 1): 4,
                     ("out", 0): 5, ("den", 0): 6, ("out", 1): 7}[what, k]
            at = p - 2 if what == "up" else p if (what, k) == ("den", 0) else p + 1
            if isinstance(at, int):
                if at < 0:
                    return 4 * p + k
                if at == 0:
                    return 4 * 2 + (k if what == "up" else 4)
                if at == NPAIR:
                    return 8 * (NPAIR - 2) + 5 + 8 + {4: 0, 5: 1, 7: 2}[place]
                if at >= NPAIR - 2:
                    return 8 * (NPAIR - 2) + 5 + 4 * (at - NPAIR + 2) + place - 4
            return 8 * at + 5 + place

        def step_before(p, st, n):
            st -= n
            if st < 0:
                p, st = p - 1, st + NSTEP
            return None if isinstance(p, int) and p < 0 else (p, st)

        def pairs(eng, body):
            body(0, 0)
            with eng.Fori(1, NPAIR - 3, 2) as p:
                body(p, 1)
                body(p + 1, 0)
            for q in range(NPAIR - 3, NPAIR):
                body(q, q % 2)

        def is_first(p):
            return isinstance(p, int) and p == 0

        def last(p, n=1):
            return isinstance(p, int) and p >= NPAIR - n

        MAXN = [0, 0, 0] + [3] * 10 + [2] + [0] * 2
        UP_STEPS = (1, 2, 3, 4)
        DEN1, OUT0, DEN0, OUT1 = 5, 8, 10, 14

        ROPE = []
        for n in range(4):
            ROPE += [(n, 0), (n, 1), (n, 2)]
            if n:
                ROPE.append((n - 1, 3))
        ROPE.append((3, 3))
        NROPE = len(ROPE)
        ROPE_STEPS = {5: 1, 6: 1, 7: 1, 8: 1, 9: 1, 10: 1, 11: 1, 12: 1, 13: 2, 14: 3, 15: 3}
        ACT_ROPE = {8: 0, 11: 1, 14: 2, 15: 3}

        LAST_ADD = 10
        T_H2, T_CN = 6, 9

        T_BANK = [ps_s[0], ps_s[1], ps_m[1], ps_o]
        C_BANK = [ps_s[2], ps_s[3], ps_s[0], ps_s[1]]

        def rope(eng, q, n, step):
            V = nc.vector if eng.engine == nc.vector.engine else nc.gpsimd
            w, half = divmod(n, 2)
            c = slice(half * HALF, (half + 1) * HALF)
            before = lambda i: eng.wait_ge(s["rotated"], NROPE * q + ROPE.index((n, i)) + 1)
            if step == 0:
                if half == 0:
                    eng.wait_ge(swapped[w], 64 * (q + 1))
                ins = V.tensor_tensor(us[:, w, c], us[:, w, c], cos_sb[:, c], ALU.mult)
            if step == 1:
                ins = V.tensor_tensor(vs[:, w, c], vs[:, w, c], sin_sb[:, c], ALU.mult)
            if step == 2:
                before(1)
                ins = V.tensor_tensor(us[:, w, c], us[:, w, c], vs[:, w, c], ALU.add)
            if step == 3:
                eng.wait_ge(s["rotated_hi"], 4 * q + n + 1)
                ins = V.tensor_tensor(vs[:, w, c], us[:, w, c], xh[:, w, c].bitcast(F32), ALU.subtract)
            ins.then_inc(s["rotated"], 1)

        def up_bank(q, j):
            return (ps_x, ps_s[2], ps_s[3], ps_s[0])[j] if is_first(q) else ps_x

        def max_bank(q, n):
            return (ps_m[0], ps_m[1], ps_s[0], ps_s[1])[n % 4] if is_first(q) else ps_m[n % 2]

        @block.tensor
        def _(pe):
            pe.wait_ge(s["cond_wide"], 1)
            pe.wait_ge(wmod_in, 16)
            for b in range(B):
                for n in range(2):
                    nc.tensor.matmul(ps_s[2 * b + n][:, 0:3 * D], c_rep[:, b, :], wmod_sb[:, n * 3 * D:(n + 1) * 3 * D],
                                     start=True, stop=True).then_inc(s["mod_product"], 1)
            pe.wait_ge(vo_in, 32)
            for n, bank in enumerate((ps_m[1], ps_o)):
                for j in range(4):
                    for h in range(2):
                        head = 2 * (4 * n + j) + h
                        ins = nc.tensor.matmul(bank[64 * h:64 * h + 64, j * P:(j + 1) * P], wuv_sb[:, head, :],
                                               wo_sb[:, head, :], start=True, stop=True)
                ins.then_inc(s["g_product"], 1)

            def latents(b):
                for g in (2 * b, 2 * b + 1):
                    if g == 2:
                        pe.wait_ge(s["g_copied"], 2)
                    for n in range(4):
                        pe.wait_ge(s["tile_norm"], 4 * g + n + 1)
                        ins = nc.tensor.transpose(T_BANK[g][:, n * P:(n + 1) * P], hn[:, 4 * g + n, :], ident[:])
                    ins.then_inc(s["features_T"], 1)
                if b == 1:
                    pe.wait_ge(s["x_free"], 4)
                for n in range(4 * b, 4 * b + 4):
                    half, w = divmod(n % 4, 2)
                    pe.wait_ge(s["features"], 2 * b + half + 1)
                    ge(pe, s["latent_lo"], n - 3)
                    nc.tensor.matmul(C_BANK[n % 4][:], wd_sb[:, w, :], hT[:, b * S + half * HALF:b * S + (half + 1) * HALF],
                                     start=True, stop=True).then_inc(s["latent_product"], 1)
                ge(pe, s["values"], b)
                for n in range(TB):
                    k = b * TB + n
                    ins = nc.tensor.matmul(ps_m[0][:, n * LAT:(n + 1) * LAT], hT[:, k * P:(k + 1) * P],
                                           wd_sb[:, 1, 0:LAT], start=True, stop=True)
                ins.then_inc(s["value_product"], 1)

            def up(q, j):
                w, half = divmod(j, 2)
                if not is_first(q):
                    ge(pe, s["x_free"], x_use("up", q, j))
                if j == 0:
                    pe.wait_ge(s["weights_split"], 2 * (q + 1))
                c = (cq, ck)[w][:, bass.ds((q // HP) * S + half * HALF, HALF)]
                nc.tensor.matmul(up_bank(q, j)[:], wh[:, w, :], c, start=True, stop=False)
                nc.tensor.matmul(up_bank(q, j)[:], wl[:, w, :], c, start=False, stop=True).then_inc(s["x_product"], 1)

            def maxima(q, par, n):
                h, r = divmod(n, 16)
                qt, kh = divmod(r, 2)
                if r == 0:
                    pe.wait_ge(qk_placed[h], 64 * (q + 1))
                ge(pe, s["max_reduced"], n - 3 if is_first(q) else 32 * q + n - 1)
                qs = qq[:, par, h, :].rearrange("p (m t) -> p t m", t=TB)
                nc.tensor.matmul(max_bank(q, n)[:], qs[:, qt, :], kk[:, par, h, kh * HALF:(kh + 1) * HALF],
                                 start=True, stop=True).then_inc(s["max_product"], 1)

            def score(p, par, st, h):
                half, kt = divmod(st, TB)
                if st == 0:
                    pe.wait_ge(qlo_placed[h], 16 * (p + 1))
                    pe.wait_ge(khi_placed[h], 16 * (p + 1))
                before = step_before(p, st, 2)
                if before:
                    ge(pe, s["probs"], n_score(*before, h))
                bank = ps_s[2 * (st % 2) + h]
                nc.tensor.matmul(bank[:], kk[:, par, h, kt * P:(kt + 1) * P], qq[:, par, h, half * HALF:(half + 1) * HALF],
                                 start=True, stop=False)
                if st == 0:
                    pe.wait_ge(row_placed[h], 16 * (p + 1))
                nc.tensor.matmul(bank[:], k2[0:65, par, h, kt * P:(kt + 1) * P], q2[0:65, par, h, half * HALF:(half + 1) * HALF],
                                 start=False, stop=True).then_inc(s["scores"], 1)

            def pv(p, par, st):
                half, kt = divmod(st, TB)
                if st == 0:
                    pe.wait_ge(cv_in, 16 * (p + 1))
                if kt == 0:
                    ge(pe, s["sums_copied"], 2 * p + half)
                for h in range(2):
                    pe.wait_ge(s["probs"], n_score(p, st, h))
                    ins = nc.tensor.matmul(ps_o[64 * h:64 * h + 64, :], cv[:, par, kt, :], probs[:, st % 4, h, :],
                                           start=(kt == 0), stop=(kt == TB - 1))
                ins.then_inc(s["sums"], 1)

            def denominators(p, half):
                ge(pe, s["x_free"], x_use("den", p, half))
                wait_adds(pe, p, TB * half + TB - 1, (0, 1))
                for h in range(2):
                    ins = nc.tensor.matmul(ps_x[32 * h:32 * h + 32, :], ones[:, 0:32], acc[:, half, h, :], start=True, stop=True)
                ins.then_inc(s["x_product"], 1)

            def outputs(p, half):
                ge(pe, s["x_free"], x_use("out", p, half))
                pe.wait_ge(s["divided"], 2 * p + half + 1)
                for n in range(4):
                    ins = nc.tensor.matmul(ps_x[:, n * P:(n + 1) * P], ou[:, half, n * P:(n + 1) * P],
                                           g_all[:, p // HP, p % HP, :], start=True, stop=True)
                ins.then_inc(s["x_product"], 1)

            pe.wait_ge(s["tables"], 1)
            pe.wait_ge(down_in, 16)
            latents(0)
            pe.wait_ge(s["latent_lo"], 4)
            for j in range(4):
                up(0, j)
            latents(1)
            for j in range(4):
                up(1, j)
            pe.wait_ge(s["values"], 2)
            pe.wait_ge(s["latent_lo"], 8)
            for n in range(32):
                maxima(0, 0, n)
            pe.wait_ge(s["max_reduced"], 32)
            pe.wait_ge(s["g_gated"], 2)

            def h2_features(b):
                pe.wait_ge(s["norm2"], b + 1)
                for g in range(2):
                    for n in range(4):
                        ins = nc.tensor.transpose(ps_m[g][:, n * P:(n + 1) * P], h2[:, TB * b + 4 * g + n, :], ident[:])
                    ins.then_inc(s["norm2_T"], 1)

            def logits(b):
                pe.wait_ge(s["norm2_features"], 2 * b + 2)
                for n in range(TB):
                    ins = nc.tensor.matmul(ps_m[0][:, n * E:(n + 1) * E], h2T[:, n * P:(n + 1) * P], gw_sb[:],
                                           start=True, stop=True)
                ins.then_inc(s["logit_product"], 1)

            def counts_before(b):
                pe.wait_ge(s["counts"], b + 1)
                last_tile = rt[b][:, 9, :].rearrange("p (e t) -> p e t", e=E)[:, :, TB - 1]
                nc.tensor.matmul(ps_m[1][:, 0:E], tri[:], last_tile, start=True, stop=True)
                nc.tensor.matmul(ps_m[1][:, E:2 * E], ones_sq[:], last_tile, start=True, stop=True).then_inc(s["counts_before"], 1)

            def pair(p, par):
                for st in range(NSTEP):
                    if last(p):
                        if st == 0:
                            pe.wait_ge(s["max_reduced"], 32 * NPAIR)
                            h2_features(0)
                        if st == 2:
                            logits(0)
                        if st == 8:
                            counts_before(0)
                    todo = [] if last(p) else list(range(sum(MAXN[:st]), sum(MAXN[:st + 1])))
                    score(p, par, st, 0)
                    for n in todo[:1]:
                        maxima(p + 1, 1 - par, n)
                    score(p, par, st, 1)
                    for n in todo[1:2]:
                        maxima(p + 1, 1 - par, n)
                    if st > 0:
                        pv(p, par, st - 1)
                    elif not is_first(p):
                        pv(p - 1, 1 - par, NSTEP - 1)
                    for n in todo[2:]:
                        maxima(p + 1, 1 - par, n)
                    if st in UP_STEPS and not last(p, 2):
                        up(p + 2, st - UP_STEPS[0])
                    if not is_first(p):
                        if st == DEN1:
                            denominators(p - 1, 1)
                        if st == OUT0:
                            outputs(p - 1, 0)
                        if st == OUT1:
                            outputs(p - 1, 1)
                    if st == DEN0:
                        denominators(p, 0)

            pairs(pe, pair)
            pv(NPAIR - 1, 1, NSTEP - 1)
            ge(pe, s["x_free"], x_use("den", NPAIR - 1, 1))
            wait_adds(pe, NPAIR - 1, NSTEP - 1, (0, 1))
            for h in range(2):
                ins = nc.tensor.matmul(ps_x[64 * h:64 * h + 64, :], ones[:], acc[:, 1, h, :], start=True, stop=True)
            ins.then_inc(s["x_product"], 1)

            def slots_T(i, k):
                g = i // GS
                if i % GS == 0:
                    pe.wait_ge(group_in[g % 2], 16 * (k // (2 * GS) + 1))
                ge(pe, s["slots_in"], k)
                nc.tensor.transpose(ps_s[2][:, 0:P], xs[:, g % 2, i % GS, :], ident[:]).then_inc(s["slots_T"], 1)

            def up_e(i, k):
                pe.wait_ge(s["slots_in"], k + 1)
                pe.wait_ge(expert_in[i], 16 * (k // (2 * GS) + 1))
                ge(pe, s["hidden"], k - 1)
                for c in range(4):
                    ins = nc.tensor.matmul(ps_s[i % 2][:, c * P:(c + 1) * P], w1_sb[i][:, c * P:(c + 1) * P], xT[i % 2],
                                           start=True, stop=True)
                ins.then_inc(s["hidden_product"], 1)

            def down_e(i, k):
                pe.wait_ge(s["hidden"], k + 1)
                ge(pe, s["y_copied"], k)
                for c in range(4):
                    ins = nc.tensor.matmul(ps_s[3][:, 0:D], hid[i % 2][:, c * P:(c + 1) * P],
                                           w2_sb[i][:, c * P:(c + 1) * P], start=(c == 0), stop=(c == 3))
                ins.then_inc(s["y_product"], 1)

            def tiles(k0, lead=True, follow=True, between={}):
                if lead:
                    slots_T(0, k0)
                for i in range(2 * GS):
                    up_e(i, k0 + i)
                    if i < 2 * GS - 1 or follow:
                        slots_T((i + 1) % (2 * GS), k0 + i + 1)
                    if i or not isinstance(k0, int) or k0:
                        down_e((i - 1) % (2 * GS), k0 + i - 1)
                    if i in between:
                        between[i]()

            pe.wait_ge(s["probs"], 32 * NPAIR)
            outputs(NPAIR - 1, 0)
            tiles(0, between={0: lambda: outputs(NPAIR - 1, 1)})
            tiles(2 * GS, lead=False, between={T_H2 - 2 * GS: lambda: (h2_features(1), logits(1)),
                                               T_CN - 2 * GS: lambda: counts_before(1)})
            tiles(4 * GS, lead=False, follow=False)
            with pe.Fori(3, NG // 2) as g2:
                tiles(g2 * (2 * GS), follow=False)
            down_e(2 * GS - 1, NG * GS - 1)

        @block.scalar
        def _(act):
            act.wait_ge(c_in, 16)
            nc.scalar.activation(c_e[:, 0, :], c_col[:], ACT.Exp, scale=-1.0).then_inc(s["cond_exp"], 1)

            def root(n):
                b = n // 2
                act.wait_ge(s["var_ready"], n + 1)
                nc.scalar.activation(sd[:, 1, b * TB:(b + 1) * TB], sd[:, 0, b * TB:(b + 1) * TB], ACT.Sqrt).then_inc(s["dev_ready"], 1)

            root(0)
            for n in range(4):
                act.wait_ge(s["mod_product"], n + 1)
                dst = mod[:, n // 2, 3 * (n % 2):3 * (n % 2) + 3, :].rearrange("p a d -> p (a d)")
                nc.scalar.copy(dst, ps_s[n][:, 0:3 * D]).then_inc(s["mod_copied"], 1)
            root(1)
            for n, bank in enumerate((ps_m[1], ps_o)):
                act.wait_ge(s["g_product"], n + 1)
                nc.scalar.copy(g_raw[:, n * HALF:(n + 1) * HALF], bank[:]).then_inc(s["g_copied"], 1)

            def features(g):
                if g == 0:
                    act.wait_ge(lns_in, 16)
                act.wait_ge(s["features_T"], g + 1)
                nc.scalar.activation(hT[:, g * HALF:(g + 1) * HALF], T_BANK[g][:], ACT.Identity,
                                     bias=lns[:, 1:2], scale=lns[:, 0:1]).then_inc(s["features"], 1)

            def upper(n):
                half, w = divmod(n % 4, 2)
                c = (n // 4) * S + half * HALF
                act.wait_ge(s["latent_product"], n + 1)
                nc.scalar.copy((cq, ck)[w][:, c:c + HALF], C_BANK[n % 4][:]).then_inc(s["latent_hi"], 1)

            def values_out(b):
                act.wait_ge(s["value_product"], b + 1)
                nc.scalar.copy(c_all[:, TB * b:TB * b + TB, :].rearrange("p a l -> p (a l)"), ps_m[0][:]).then_inc(s["values"], 1)

            def up_out(q, j):
                w, half = divmod(j, 2)
                act.wait_ge(s["x_product"], x_use("up", q, j) + 1)
                if j == 0:
                    ge(act, s["rotated"], NROPE * q)
                nc.scalar.copy(us[:, w, half * HALF:(half + 1) * HALF], up_bank(q, j)[:]).then_inc(s["x_free"], 1)

            def upper_rot(q, n):
                w, half = divmod(n, 2)
                if n == 0:
                    ge(act, qk_placed[0], 64 * q)
                    ge(act, qk_placed[1], 64 * q)
                act.wait_ge(s["rotated"], NROPE * q + ROPE.index((n, 2)) + 1)
                c = slice(half * HALF, (half + 1) * HALF)
                nc.scalar.copy(xh[:, w, c], us[:, w, c]).then_inc(s["rotated_hi"], 1)

            def expo(p, st, h):
                act.wait_ge(s["scores"], n_score(p, st, h))
                before = step_before(p, st, 4)
                if before:
                    bp, bst_ = before
                    if h == 0:
                        act.wait_ge(s["sums"], 16 * bp + bst_ + 1)
                    wait_adds(act, bp, bst_, (h,))
                nc.scalar.activation(probs[:, st % 4, h, :], ps_s[2 * (st % 2) + h][:], ACT.Exp,
                                     scale=SCALE).then_inc(s["probs"], 1)

            def o_out(p, half):
                act.wait_ge(s["sums"], 16 * p + 8 * half + 8)
                if not is_first(p):
                    act.wait_ge(s["x_product"], x_use("out", p - 1, half) + 1)
                nc.scalar.copy(ou[:, half, :], ps_o[:]).then_inc(s["sums_copied"], 1)

            def den_out(p, half):
                act.wait_ge(s["x_product"], x_use("den", p, half) + 1)
                ge(act, den_cols_in, 32 * (2 * p + half))
                nc.scalar.copy(den[:], ps_x[0:64, :]).then_inc(s["x_free"], 1)

            features(0)
            features(1)
            root(2)
            for n in range(4):
                upper(n)
            values_out(0)
            act.wait_ge(s["g_product"], 2)
            for j in range(4):
                up_out(0, j)
            root(3)
            features(2)
            features(3)
            for n in range(4):
                upper_rot(0, n)
            for n in range(4, 8):
                upper(n)
            values_out(1)
            for j in range(4):
                up_out(1, j)
            for n in range(4):
                upper_rot(1, n)

            def h2T_out(b):
                for g in range(2):
                    act.wait_ge(s["norm2_T"], 2 * b + g + 1)
                    nc.scalar.copy(h2T[:, g * HALF:(g + 1) * HALF], ps_m[g][:]).then_inc(s["norm2_features"], 1)

            def exp_logits(b):
                act.wait_ge(s["logits"], b + 1)
                nc.scalar.activation(rt[b][:, 1, :], rt[b][:, 0, :], ACT.Exp).then_inc(s["logit_exp"], 1)

            def pair(p, par):
                for st in range(NSTEP):
                    expo(p, st, 0)
                    expo(p, st, 1)
                    if last(p):
                        if st == 0:
                            h2T_out(0)
                        if st == 3:
                            exp_logits(0)
                    if st == 0 and not is_first(p):
                        o_out(p - 1, 1)
                    if st == 8:
                        o_out(p, 0)
                    if st in UP_STEPS and not last(p, 2):
                        up_out(p + 2, st - UP_STEPS[0])
                    if st == DEN1 and not is_first(p):
                        den_out(p - 1, 1)
                    if st == DEN0:
                        den_out(p, 0)
                    if st in ACT_ROPE and not last(p, 2):
                        upper_rot(p + 2, ACT_ROPE[st])

            pairs(act, pair)

            def hidden(i, k):
                act.wait_ge(s["hidden_product"], k + 1)
                ge(act, s["y_product"], k - 1)
                for c in range(4):
                    ins = nc.scalar.activation(hid[i % 2][:, c * P:(c + 1) * P], ps_s[i % 2][:, c * P:(c + 1) * P], ACT.Relu,
                                               bias=b1_sb[i][:, c:c + 1])
                ins.then_inc(s["hidden"], 1)

            def slots_out(i, k):
                act.wait_ge(s["slots_T"], k + 1)
                ge(act, s["hidden_product"], k - 1)
                nc.scalar.copy(xT[i % 2], ps_s[2][:, 0:P]).then_inc(s["slots_in"], 1)

            def y_out(i, k):
                act.wait_ge(s["y_product"], k + 1)
                ge(act, group_out[i // GS], 16 * (k // (2 * GS)))
                nc.scalar.copy(ys[:, i // GS, i % GS, :], ps_s[3][:, 0:D]).then_inc(s["y_copied"], 1)

            slots_out(0, 0)
            for k in range(NA * GS):
                if k + 1 < NA * GS:
                    slots_out((k + 1) % (2 * GS), k + 1)
                hidden(k % (2 * GS), k)
                if k:
                    y_out((k - 1) % (2 * GS), k - 1)
                if k == T_H2:
                    h2T_out(1)
                    exp_logits(1)
            for k in range(NA * GS, 6 * GS):
                hidden(k % (2 * GS), k)
                if k == NA * GS:
                    y_out((k - 1) % (2 * GS), k - 1)
            with act.Fori(3, NG // 2) as g2:
                for i in range(2 * GS):
                    hidden(i, g2 * (2 * GS) + i)

        @block.gpsimd
        def _(pool):
            V = nc.gpsimd
            V.memset(ident[:], 0.0).then_inc(s["pool_step"], 1)
            pool.wait_ge(s["pool_step"], 1)
            V.affine_select(out=ident[:], in_=ident[:], compare_op=ALU.not_equal, fill=1.0, base=0,
                            pattern=[[-1, P]], channel_multiplier=1).then_inc(s["tables"], 1)
            V.memset(ones_sq[:], 1.0)
            V.memset(half_neg[:], -0.5)
            V.memset(again[:], 1.0).then_inc(s["pool_step"], 1)
            V.memset(zero[:], 0.0).then_inc(s["pool_step"], 1)
            pool.wait_ge(s["pool_step"], 3)
            V.memset(again[:].rearrange("p (e t) -> p e t", e=E)[:, :, 0:1], 0.0)
            V.affine_select(out=tri[:], in_=ones_sq[:], compare_op=ALU.is_gt, fill=0.0, base=0,
                            pattern=[[1, P]], channel_multiplier=-1)
            V.iota(rev[:], [[-1, E]], base=E, channel_multiplier=0, allow_small_or_imprecise_dtypes=True)
            V.iota(thr[:], [[P, TB]], base=0, channel_multiplier=0, allow_small_or_imprecise_dtypes=True)
            V.iota(tix[:], [[1, NSL]], base=0, channel_multiplier=0,
                   allow_small_or_imprecise_dtypes=True).then_inc(s["tables"], 1)

            def split(q):
                pool.wait_ge(up_in, 16 * (q + 1))
                if not is_first(q):
                    pool.wait_ge(s["x_product"], x_use("up", q - 1, 3) + 1)
                V.tensor_tensor(wh[:], wu[:], ones_sq[:].unsqueeze(1).to_broadcast([P, 2, P]),
                                ALU.mult).then_inc(s["weights_split"], 1)
                pool.wait_ge(s["weights_split"], 2 * q + 1)
                V.tensor_tensor(wl[:], wu[:], wh[:].bitcast(F32), ALU.subtract).then_inc(s["weights_split"], 1)

            split(0)
            pool.wait_ge(s["norm1"], 1)
            pool.wait_ge(s["mod_scales"], 1)
            hb = h0[:, TB:NT, :]
            V.tensor_tensor(hb, hb, mod[:, 1, 1:2, :].to_broadcast([P, TB, D]), ALU.mult).then_inc(s["modulated"], 1)
            pool.wait_ge(s["modulated"], 1)
            V.tensor_tensor(hb, hb, mod[:, 1, 0:1, :].to_broadcast([P, TB, D]), ALU.add).then_inc(s["modulated"], 1)
            split(1)
            pool.wait_ge(s["g_copied"], 2)
            pool.wait_ge(s["gates"], 1)
            pool.wait_ge(s["value_product"], 2)
            for b in range(B):
                V.tensor_tensor(g_all[:, b, :, :], g_raw.rearrange("p (j d) -> p j d", d=D),
                                mod[:, b, 2:3, :].to_broadcast([P, HP, D]), ALU.mult).then_inc(s["g_gated"], 1)
            split(2)
            for piece in ROPE:
                rope(pool, 1, *piece)

            def add(p, st, h):
                half, kt = divmod(st, TB)
                pool.wait_ge(s["probs"], n_score(p, st, h))
                if kt == 1:
                    first = probs[:, (st - 1) % 4, h, :]
                    if not is_first(p):
                        pool.wait_ge(s["x_product"], x_use("den", p - 1, half) + 1)
                else:
                    first = acc[:, half, h, :]
                    pool.wait_ge(s["added"], n_add(p, st, h) - (1 if last(p) else 2))
                V.tensor_tensor(acc[:, half, h, :], first, probs[:, st % 4, h, :], ALU.add).then_inc(s["added"], 1)

            def inverse_root(b):
                v = sd[:, 0, b * TB:(b + 1) * TB]
                pool.wait_ge(s["var2_ready"], b + 1)
                V.tensor_tensor(v, v, half_neg[:], ALU.pow).then_inc(s["inv2_ready"], 1)

            def scatter(b):
                pool.wait_ge(zeros_out, 16 * B)
                pool.wait_ge(s["slots"], 2 * b + 1)
                pool.wait_ge(s["weighted"], b + 1)
                for k in range(b * TB, (b + 1) * TB):
                    nc.gpsimd.indirect_dma_start(out=xs_dram[b], out_offset=bass.IndirectOffsetOnAxis(ap=slot[:, k:k + 1], axis=0),
                                                 in_=xw[:, k, :], in_offset=None).then_inc(scattered, 16)

            pool.wait_ge(s["g_gated"], 2)

            def pair(p, par):
                for st in range(NSTEP):
                    if st % TB and not (last(p) and st > LAST_ADD):
                        add(p, st, 0)
                        if not last(p):
                            add(p, st, 1)
                    if last(p, 2) and not last(p) and st == 9:
                        inverse_root(0)
                    if st == TB and not last(p, 3):
                        split(p + 3)

            pairs(pool, pair)

            def add_b2(k):
                i = k % (2 * GS)
                pool.wait_ge(s["y_copied"], k + 1)
                y = ys[:, i // GS, i % GS, :]
                V.tensor_tensor(y, y, b2_sb[i], ALU.add).then_inc(s["y_biased"], 1)

            scatter(0)
            for k in range(NA * GS):
                add_b2(k)
                if k == 1:
                    inverse_root(1)
                if k == T_CN:
                    scatter(1)
            for b in range(B):
                groups = NG // B * (b + 1)
                for n in range(2):
                    pool.wait_ge(group_out[n], 16 * ((groups + 1 - n) // 2))
                for k in range(b * TB, (b + 1) * TB):
                    nc.gpsimd.indirect_dma_start(out=yg[:, k, :], out_offset=None, in_=ys_dram[b],
                                                 in_offset=bass.IndirectOffsetOnAxis(ap=slot[:, k:k + 1], axis=0)
                                                 ).then_inc(gathered[[k < n1 for _, n1 in PARTS].index(True)], 16)

        @block.vector
        def _(dve):
            seq = [0]
            V = nc.vector

            def then(ins):
                seq[0] += 1
                ins.then_inc(s["vector_step"], 1)
                dve.wait_ge(s["vector_step"], seq[0])

            V.memset(ones[:], 1.0)
            V.memset(k2[64:65, :, :, :].bitcast(F32), 1.0).then_inc(s["constants"], 1)

            def statistics(src, tiles):
                for k in tiles:
                    ins = V.bn_stats(bst[:, k, :], src[:, k, :])
                then(ins)
                for k in tiles:
                    ins = V.bn_aggr(mv[:, k, :], bst[:, k, :])
                then(ins)
                ts = slice(tiles[0], tiles[-1] + 1)
                V.tensor_scalar_add(sd[:, 0, ts], mv[:, ts, 1], EPS).then_inc(s["var_ready"], 1)

            def inverse(tiles, n):
                ts = slice(tiles[0], tiles[-1] + 1)
                dve.wait_ge(s["dev_ready"], n)
                then(V.reciprocal(sd[:, 0, ts], sd[:, 1, ts]))

            def normalise(dst, src, tiles):
                for k in tiles:
                    ins = V.tensor_scalar(dst[:, k, :], src[:, k, :], mv[:, k, 0:1], sd[:, 0, k:k + 1],
                                          ALU.subtract, ALU.mult)
                    if dst is hn:
                        ins.then_inc(s["tile_norm"], 1)
                return ins

            T0, T1 = range(0, TB), range(TB, NT)
            dve.wait_ge(s["cond_exp"], 1)
            dve.wait_ge(c_in, 16)
            then(V.tensor_scalar_add(c_e[:, 1, :], c_e[:, 0, :], 1.0))
            then(V.reciprocal(c_e[:, 2, :], c_e[:, 1, :]))
            then(V.tensor_tensor(c_e[:, 0, :], c_e[:, 2, :], c_col[:], ALU.mult))
            for b in range(B):
                ins = V.tensor_copy(c_rep[:, b, :], c_e[:, 0, b:b + 1].to_broadcast([P, P]))
            ins.then_inc(s["cond_wide"], 1)
            dve.wait_ge(x_in[0], 32)
            statistics(x_sb, T0)
            inverse(T0, 1)
            then(normalise(h0, x_sb, T0))
            dve.wait_ge(s["mod_copied"], 4)
            V.tensor_scalar_add(mod[:, :, 1:5:3, :], mod[:, :, 1:5:3, :], 1.0).then_inc(s["mod_scales"], 1)
            dve.wait_ge(s["mod_scales"], 1)
            hb = h0[:, 0:TB, :]
            then(V.tensor_tensor(hb, hb, mod[:, 0, 1:2, :].to_broadcast([P, TB, D]), ALU.mult))
            then(V.tensor_tensor(hb, hb, mod[:, 0, 0:1, :].to_broadcast([P, TB, D]), ALU.add))
            statistics(h0, T0)
            inverse(T0, 2)
            normalise(hn, h0, T0)
            def lower(n):
                half, w = divmod(n % 4, 2)
                c = slice((n // 4) * S + half * HALF, (n // 4) * S + (half + 1) * HALF)
                dst = (cq, ck)[w][64:128, c]
                dve.wait_ge(s["latent_hi"], n + 1)
                V.tensor_tensor(dst, C_BANK[n % 4][64:128, :], dst.bitcast(F32), ALU.subtract).then_inc(s["latent_lo"], 1)

            dve.wait_ge(x_in[1], 32)
            statistics(x_sb, T1)
            lower(0)
            inverse(T1, 3)
            normalise(h0, x_sb, T1).then_inc(s["norm1"], 1)
            for n in range(1, 4):
                lower(n)
            for b in range(B):
                gates = mod[:, b, 2:6:3, :]
                then(V.tensor_scalar(g_tmp[:, b, :, :], gates, 0.0, 2.0, ALU.is_ge, ALU.mult))
                then(V.tensor_scalar(g_abs[:, b, :, :], gates, -1.0, 0.25, ALU.mult, ALU.max))
                then(V.tensor_tensor(gates, gates, g_abs[:, b, :, :], ALU.max))
                ins = V.scalar_tensor_tensor(out=gates, in0=g_tmp[:, b, :, :], scalar=-1.0, in1=gates,
                                             op0=ALU.add, op1=ALU.mult)
            ins.then_inc(s["gates"], 1)

            dve.wait_ge(s["modulated"], 2)
            statistics(h0, T1)
            inverse(T1, 4)
            normalise(hn, h0, T1)
            def reduce_max(q, n):
                h, r = divmod(n, 16)
                qt, kh = divmod(r, 2)
                dve.wait_ge(s["max_product"], 32 * q + n + 1)
                if r == 0:
                    ge(dve, s["max_row"], 2 * q + h - 1)
                V.reduce_max(mx[:, h, kh, qt:qt + 1], max_bank(q, n)[:], AX.X).then_inc(s["max_reduced"], 1)

            def neg_max(q, h):
                dve.wait_ge(s["max_reduced"], 32 * q + 16 * (h + 1))
                ge(dve, row_placed[h], 16 * q)
                V.tensor_reduce(nm[:, h, :], mx[:, h, :, :].rearrange("p k t -> p t k"), AX.X, ALU.max,
                                negate=True).then_inc(s["max_row"], 1)

            def recip(p, half):
                dve.wait_ge(den_cols_in, 32 * (2 * p + half + 1))
                V.reciprocal(rc[:, half, :, :], denc[:, half, :, :]).then_inc(s["inverses"], 1)

            def divide(p, half):
                dve.wait_ge(inv_in, 32 * (2 * p + half + 1))
                dve.wait_ge(s["sums_copied"], 2 * p + half + 1)
                V.tensor_tensor(ou[:, half, :], ou[:, half, :], rr[:, half, :], ALU.mult).then_inc(s["divided"], 1)

            def out_add(p, half):
                dve.wait_ge(s["x_product"], x_use("out", p, half) + 1)
                xt = x_sb[:, bass.ds((p // HP) * TB + 4 * half, 4), :]
                V.tensor_tensor(xt, xt, ps_x[:].rearrange("p (t d) -> p t d", d=D), ALU.add).then_inc(s["x_free"], 1)

            dve.wait_ge(rot_in, 32)
            for piece in ROPE:
                rope(dve, 0, *piece)
            for n in range(4, 8):
                lower(n)
            dve.wait_ge(s["gates"], 1)
            for b in range(B):
                tb = slice(b * TB, (b + 1) * TB)
                dve.wait_ge(s["tile_norm"], TB * (b + 1))
                then(V.tensor_tensor(h0[:, tb, :], h0[:, tb, :], mod[:, b, 2:3, :].to_broadcast([P, TB, D]), ALU.mult))
                then(V.tensor_tensor(x_sb[:, tb, :], x_sb[:, tb, :], h0[:, tb, :], ALU.add))
            dve.wait_ge(s["values"], 2)
            for n in range(16):
                reduce_max(0, n)
            neg_max(0, 0)
            for n in range(16, 32):
                reduce_max(0, n)
            neg_max(0, 1)
            def add_sums(st, h):
                half, kt = divmod(st, TB)
                sums = s["added_last" if h else "added"]
                dve.wait_ge(s["probs"], n_score(NPAIR - 1, st, h))
                if kt == 1:
                    first = probs[:, (st - 1) % 4, h, :]
                    dve.wait_ge(s["x_product"], x_use("den", NPAIR - 2, half) + 1)
                else:
                    first = acc[:, half, h, :]
                    dve.wait_ge(sums, n_add(NPAIR - 1, st, h) - 1)
                V.tensor_tensor(acc[:, half, h, :], first, probs[:, st % 4, h, :], ALU.add).then_inc(sums, 1)

            def block_stats(tiles):
                for k in tiles:
                    ins = V.bn_stats(bst[:, k, :], x_sb[:, k, :])
                then(ins)

            def block_norm(b):
                tiles, ts = range(b * TB, (b + 1) * TB), slice(b * TB, (b + 1) * TB)
                for k in tiles:
                    ins = V.bn_aggr(mv[:, k, :], bst[:, k, :])
                then(ins)
                V.tensor_scalar_add(sd[:, 0, ts], mv[:, ts, 1], EPS).then_inc(s["var2_ready"], 1)

            def block_out(b):
                ts = slice(b * TB, (b + 1) * TB)
                wide = lambda m: mod[:, b, m:m + 1, :].to_broadcast([P, TB, D])
                dve.wait_ge(s["inv2_ready"], b + 1)
                for k in range(b * TB, (b + 1) * TB):
                    ins = V.tensor_scalar(h2[:, k, :], x_sb[:, k, :], mv[:, k, 0:1], sd[:, 0, k:k + 1],
                                          ALU.subtract, ALU.mult)
                then(ins)
                then(V.tensor_tensor(h2[:, ts, :], h2[:, ts, :], wide(4), ALU.mult))
                V.tensor_tensor(h2[:, ts, :], h2[:, ts, :], wide(3), ALU.add).then_inc(s["norm2"], 1)
                dve.wait_ge(s["norm2"], b + 1)

            tok = lambda a: a.unsqueeze(2).to_broadcast([P, TB, E])
            row = lambda a: a.unsqueeze(1).to_broadcast([P, TB, E])
            by_tok = lambda a: a.rearrange("p (t e) -> p t e", e=E)
            by_exp = lambda a: a.rearrange("p (e t) -> p e t", e=E)

            def judge(b):
                r = [by_tok(rt[b][:, n, :]) for n in range(8)]
                dve.wait_ge(s["logit_product"], b + 1)
                if b == 0:
                    dve.wait_ge(gatew_in, 32)
                    dve.wait_ge(s["tables"], 2)
                then(V.tensor_tensor(r[2], by_tok(ps_m[0][:, 0:TB * E]), row(gb_sb[:]), ALU.add))
                then(V.reduce_max(rs[:, 0, :], r[2], AX.X))
                V.tensor_tensor(r[0], r[2], tok(rs[:, 0, :]), ALU.subtract).then_inc(s["logits"], 1)

            def choose(b):
                r = [by_tok(rt[b][:, n, :]) for n in range(8)]
                dve.wait_ge(s["logit_exp"], b + 1)
                then(V.reduce_sum(rs[:, 1, :], r[1], AX.X))
                then(V.reciprocal(rs[:, 2, :], rs[:, 1, :]))
                then(V.tensor_tensor(r[3], r[1], tok(rs[:, 2, :]), ALU.mult))
                then(V.reduce_max(rs[:, 3, :], r[3], AX.X))
                then(V.tensor_tensor(r[4], r[3], tok(rs[:, 3, :]), ALU.is_equal))
                then(V.tensor_tensor(r[4], r[4], row(rev[:]), ALU.mult))
                then(V.reduce_max(rs[:, 4, :], r[4], AX.X))
                then(V.tensor_tensor(r[5], r[4], tok(rs[:, 4, :]), ALU.is_equal))
                then(V.scalar_tensor_tensor(out=r[6], in0=r[5], scalar=-2.0, in1=r[3], op0=ALU.mult, op1=ALU.add))
                then(V.reduce_max(rs[:, 5, :], r[6], AX.X))
                then(V.tensor_tensor(r[7], r[6], tok(rs[:, 5, :]), ALU.is_equal))
                then(V.tensor_tensor(r[7], r[7], row(rev[:]), ALU.mult))
                then(V.reduce_max(rs[:, 6, :], r[7], AX.X))
                then(V.tensor_tensor(rs[:, 7, :], rs[:, 6, :], rs[:, 4, :], ALU.is_lt))
                then(V.scalar_tensor_tensor(out=rs[:, 7, :], in0=rs[:, 5, :], scalar=0.0, in1=rs[:, 7, :],
                                            op0=ALU.is_gt, op1=ALU.mult))
                V.tensor_tensor(rs[:, 5, :], rs[:, 5, :], rs[:, 7, :], ALU.mult)
                V.tensor_tensor(rs[:, 6, :], rs[:, 6, :], rs[:, 7, :], ALU.mult)
                then(V.tensor_scalar(rs[:, 8, :], rs[:, 7, :], -1.0, 1.0, ALU.mult, ALU.add))
                V.tensor_tensor(rs[:, 9, :], rs[:, 3, :], rs[:, 8, :], ALU.mult)
                then(V.tensor_tensor(rs[:, 4, :], rs[:, 4, :], rs[:, 8, :], ALU.mult))
                V.tensor_tensor(rs[:, 10, :], rs[:, 9, :], rs[:, 5, :], ALU.add)
                then(V.tensor_tensor(rs[:, 11, :], rs[:, 4, :], rs[:, 6, :], ALU.add))
                one_hot, count = rt[b][:, 8, :], rt[b][:, 9, :]
                then(V.tensor_tensor(by_exp(one_hot), rev[:].unsqueeze(2).to_broadcast([P, E, TB]),
                                     rs[:, 11, :].unsqueeze(1).to_broadcast([P, E, TB]), ALU.is_equal))
                V.tensor_tensor_scan(count, again[:], one_hot, 0.0, ALU.mult, ALU.add).then_inc(s["counts"], 1)
                dve.wait_ge(s["counts"], b + 1)

            def scaled(b):
                for k in range(b * TB, (b + 1) * TB):
                    ins = V.tensor_scalar(xw[:, k, :], h2[:, k, :], rs[:, 10, k - b * TB:k - b * TB + 1], None, ALU.mult)
                ins.then_inc(s["weighted"], 1)

            def find_slots(b):
                one_hot, count, at = rt[b][:, 8, :], rt[b][:, 9, :], rt[b][:, 10, :]
                dve.wait_ge(s["counts_before"], b + 1)
                then(V.tensor_copy(cn[:, 0:2, :].rearrange("p a e -> p (a e)"), ps_m[1][:, 0:2 * E]))
                then(V.tensor_tensor(cmp3[:, :, 0:TB], cn[:, 1, :].unsqueeze(2).to_broadcast([P, E, TB]),
                                     thr[:].unsqueeze(1).to_broadcast([P, E, TB]), ALU.is_gt))
                then(V.reduce_sum(cn[:, 2, :], cmp3[:, :, 0:TB], AX.X))
                then(V.tensor_tensor_scan(cn[:, 3, :], ones_sq[:, 0:E], cn[:, 2, :], 0.0, ALU.mult, ALU.add))
                then(V.tensor_tensor(cn[:, 4, :], cn[:, 3, :], cn[:, 2, :], ALU.subtract))
                then(V.scalar_tensor_tensor(out=cn[:, 5, :], in0=cn[:, 4, :], scalar=float(P), in1=cn[:, 0, :],
                                            op0=ALU.mult, op1=ALU.add))
                then(V.tensor_tensor(by_exp(at), by_exp(count), cn[:, 5, :].unsqueeze(2).to_broadcast([P, E, TB]), ALU.add))
                then(V.tensor_tensor(at, at, one_hot, ALU.mult))
                then(V.reduce_sum(rs[:, 0, :], at.rearrange("p (e t) -> p t e", e=E), AX.X))
                V.tensor_scalar_add(slot[:, b * TB:(b + 1) * TB], rs[:, 0, :], -1.0).then_inc(s["slots"], 1)
                then(V.tensor_tensor(cmp3[:], cn[:, 3, :].unsqueeze(2).to_broadcast([P, E, NSL]),
                                     tix[:].unsqueeze(1).to_broadcast([P, E, NSL]), ALU.is_le))
                then(V.reduce_sum(tcount[:], cmp3[:].rearrange("p e t -> p t e"), AX.X))
                V.tensor_scalar(eid[:, b * NSL:(b + 1) * NSL], tcount[:], float(E - 1), None, ALU.min).then_inc(s["slots"], 1)
                dve.wait_ge(s["slots"], 2 * b + 2)

            def pair(p, par):
                rest = [] if last(p, 2) else list(ROPE)

                for st in range(NSTEP):
                    pieces = ROPE_STEPS.get(st, 0)
                    if last(p) and st % TB:
                        add_sums(st, 1)
                        if st > LAST_ADD:
                            add_sums(st, 0)
                    if last(p, 2) and not last(p):
                        if st == 7:
                            block_stats(T0)
                            block_norm(0)
                        if st == 14:
                            block_out(0)
                    if last(p):
                        if st == 3:
                            judge(0)
                        if st == 5:
                            choose(0)
                        if st == 7:
                            scaled(0)
                        if st == 9:
                            find_slots(0)
                    if not is_first(p):
                        if st == 1:
                            divide(p - 1, 0)
                        if st == 8:
                            recip(p - 1, 1)
                        if st == 11:
                            divide(p - 1, 1)
                    if not last(p):
                        for n in range(sum(MAXN[:st]), sum(MAXN[:st + 1])):
                            reduce_max(p + 1, n)
                            if n % 16 == 15:
                                neg_max(p + 1, n // 16)
                            if rest and pieces:
                                rope(dve, p + 2, *rest.pop(0))
                                pieces -= 1
                    for _ in range(pieces):
                        if rest:
                            rope(dve, p + 2, *rest.pop(0))
                    if not is_first(p):
                        if st == OUT0:
                            out_add(p - 1, 0)
                        if st == OUT1:
                            out_add(p - 1, 1)
                    if st == 13:
                        recip(p, 0)
                while rest:
                    rope(dve, p + 2, *rest.pop(0))

            pairs(dve, pair)
            p = NPAIR - 1
            divide(p, 0)
            dve.wait_ge(s["x_product"], x_use("den", p, 1) + 1)
            V.reciprocal(rr[:, 1, :], ps_x[:]).then_inc(s["x_free"], 1)
            dve.wait_ge(s["x_free"], x_use("den", p, 1) + 1)
            dve.wait_ge(s["sums"], 16 * NPAIR)
            V.tensor_tensor(ou[:, 1, :], ps_o[:], rr[:, 1, :], ALU.mult).then_inc(s["divided"], 1)
            for half in range(2):
                out_add(p, half)
                dve.wait_ge(s["x_free"], x_use("out", p, half) + 1)
                block_stats(T1[4 * half:4 * half + 4])
            block_norm(1)
            block_out(1)
            judge(1)
            choose(1)
            scaled(1)
            find_slots(1)

            def slots_out(i, k):
                dve.wait_ge(s["slots_T"], k + 1)
                dve.wait_ge(s["hidden_product"], k - 1)
                V.tensor_copy(xT[i % 2], ps_s[2][:, 0:P]).then_inc(s["slots_in"], 1)

            def y_out(i, k):
                dve.wait_ge(s["y_product"], k + 1)
                dve.wait_ge(group_out[i // GS], 16 * (k // (2 * GS)))
                V.tensor_tensor(ys[:, i // GS, i % GS, :], ps_s[3][:, 0:D], b2_sb[i], ALU.add).then_inc(s["y_copied"], 1)

            def tiles(k0, first, i0=0):
                slots_out(i0, k0 + i0)
                for i in range(i0, 2 * GS):
                    if i < 2 * GS - 1:
                        slots_out(i + 1, k0 + i + 1)
                    if i > i0 or not first:
                        y_out((i - 1) % (2 * GS), k0 + i - 1)

            tiles(4 * GS, True, GS)
            with dve.Fori(3, NG // 2) as g2:
                tiles(g2 * (2 * GS), False)
            y_out(2 * GS - 1, NG * GS - 1)

            for g, (n0, n1) in enumerate(PARTS):
                ts = slice(n0, n1)
                dve.wait_ge(gathered[g], 16 * (n1 - n0))
                then(V.tensor_tensor(yg[:, ts, :], yg[:, ts, :],
                                     mod[:, n0 // TB, 5:6, :].to_broadcast([P, n1 - n0, D]), ALU.mult))
                V.tensor_tensor(x_sb[:, ts, :], x_sb[:, ts, :], yg[:, ts, :], ALU.add).then_inc(s["done"], 1)

        @block.sync
        def _(sp):
            sp.dma_start(c_col[:], t["c_t"]).then_inc(c_in, 16)
            for g in range(4):
                sp.dma_start(x_sb[:, 4 * g:4 * g + 4, :],
                             t["x"][4 * g * P:4 * (g + 1) * P, :].rearrange("(t p) d -> p t d", p=P)).then_inc(x_in[g // 2], 16)
                if g == 1:
                    sp.dma_start(wmod_sb[:], t["wmod"]).then_inc(wmod_in, 16)
            sp.dma_start(wuv_sb, t["wuv"]).then_inc(vo_in, 16)
            sp.dma_start(wo_sb, t["wo"]).then_inc(vo_in, 16)
            sp.dma_start(lns[:], t["lns"]).then_inc(lns_in, 16)
            sp.dma_start(wd_sb[:], t["wd"]).then_inc(down_in, 16)

            def weights(q):
                if isinstance(q, int):
                    ge(sp, s["weights_split"], 2 * q)
                    sp.dma_start(wu[:], t["wqk"][q % HP]).then_inc(up_in, 16)
                    return
                ge_all(sp,
                       (s["weights_split"], 2 * q),
                       (s["constants"], 1))
                sp.dma_start(wu[:], t["wqk"][q % HP]).then_inc(up_in, 16)

            def values(q, par):
                ge_all(sp,
                       (s["sums"], 16 * (q - 1)),
                       (s["values"], 2))
                b = q // HP
                sp.dma_start(cv[:, par, :, :], c_all[:, bass.ds(b * TB, TB), :]).then_inc(cv_in, 16)

            def swap(q, w):
                gone = [(qlo_placed[h], 16 * q) for h in range(2)]
                if w == 1:
                    gone = [(qk_placed[h], 64 * q) for h in range(2)] + [(khi_placed[h], 16 * q) for h in range(2)]
                ge_all(sp,
                       (s["x_free"], x_use("up", q, 2 * w + 1) + 1),
                       *gone)
                for a in range(4):
                    c = a ^ 1
                    sp.dma_start(vs[32 * a:32 * a + 32, w, :], us[32 * c:32 * c + 32, w, :]).then_inc(swapped[w], 16)

            def place(q, par):
                ge_all(sp,
                       (s["rotated"], NROPE * q + ROPE.index((1, 3)) + 1),
                       (s["scores"], 32 * (q - 1)))
                for h in range(2):
                    r = slice(64 * h, 64 * h + 64)
                    q_hi, k_hi = [xh[r, w, :].bitcast(F32) for w in range(2)]
                    for n, (dst, src) in enumerate(((qq[0:64], q_hi), (qq[64:128], q_hi), (kk[0:64], k_hi), (kk[64:128], vs[r, 1, :]))):
                        if h == 0 and n == 2:
                            sp.wait_ge(s["rotated"], NROPE * (q + 1))
                        sp.dma_start(dst[:, par, h, :].bitcast(F32), src).then_inc(qk_placed[h], 16)
                    if h == 0:
                        for i in range(2):
                            sp.dma_start(q2[0:64, par, i, :].bitcast(F32), vs[64 * i:64 * i + 64, 0, :]).then_inc(qlo_placed[i], 16)

            def place_k(q, par):
                for h in range(2):
                    sp.dma_start(k2[0:64, par, h, :].bitcast(F32), xh[64 * h:64 * h + 64, 1, :].bitcast(F32)).then_inc(khi_placed[h], 16)

            def max_row(q, par, h):
                ge_all(sp,
                       (s["max_row"], 2 * q + h + 1),
                       (s["scores"], 32 * (q - 1)))
                sp.dma_start(q2[64:65, par, h, :].bitcast(F32), nm[:, h, :].bitcast(F32)).then_inc(row_placed[h], 16)

            def den_cols(p, half):
                sp.wait_ge(s["x_free"], x_use("den", p, half) + 1)
                for h in range(2):
                    sp.dma_start(denc[:, half, h, :], den[32 * h:32 * h + 1, :]).then_inc(den_cols_in, 16)

            def inv_rows(p, half):
                sp.wait_ge(s["inverses"], 2 * p + half + 1)
                sp.dma_start(rd_dram[half].rearrange("h (p f) -> p h f", f=4), rc[:, half, :, :]).then_inc(inv_out, 16)

            def inv_spread(p, half):
                sp.wait_ge(inv_out, 16 * (2 * p + half + 1))
                for h in range(2):
                    sp.dma_start(rr[64 * h:64 * h + 64, half, :],
                                 rd_dram[half, h:h + 1, :].to_broadcast([64, HALF])).then_inc(inv_in, 16)

            weights(0)
            weights(1)
            sp.dma_start(cos_sb, t["cos"]).then_inc(rot_in, 16)
            sp.dma_start(sin_sb, t["sin"]).then_inc(rot_in, 16)
            sp.dma_start(gw_sb[:], t["gate_w"]).then_inc(gatew_in, 16)
            sp.dma_start(gb_sb[:], t["gate_b"].to_broadcast([P, E])).then_inc(gatew_in, 16)
            sp.wait_ge(s["tables"], 2)
            for b in range(B):
                sp.dma_start(xs_dram[b].rearrange("(t p) d -> p t d", p=P),
                             zero[:].unsqueeze(1).to_broadcast([P, NSL, D])).then_inc(zeros_out, 16)
            swap(0, 0)
            swap(0, 1)
            place(0, 0)
            place_k(0, 0)
            weights(2)
            values(0, 0)
            swap(1, 0)
            swap(1, 1)
            for h in range(2):
                max_row(0, 0, h)

            def pair(p, par):
                if not last(p):
                    place(p + 1, 1 - par)
                if not last(p, 2):
                    swap(p + 2, 0)
                if not last(p):
                    place_k(p + 1, 1 - par)
                if not last(p, 2):
                    swap(p + 2, 1)
                if not last(p):
                    values(p + 1, 1 - par)
                if not last(p, 3):
                    weights(p + 3)
                if not is_first(p):
                    den_cols(p - 1, 1)
                if not last(p):
                    max_row(p + 1, 1 - par, 0)
                if not is_first(p):
                    inv_rows(p - 1, 1)
                    inv_spread(p - 1, 1)
                den_cols(p, 0)
                if not last(p):
                    max_row(p + 1, 1 - par, 1)
                inv_rows(p, 0)
                inv_spread(p, 0)

            pairs(sp, pair)

            def expert_data(g, par, i):
                k = g * GS + i
                by_pool = isinstance(g, int) and g - 2 < NA
                if isinstance(g, int):
                    if k == 2:
                        sp.wait_ge(s["sums"], 16 * NPAIR)
                        wait_adds(sp, NPAIR - 1, NSTEP - 1, (0, 1))
                    if k == 5:
                        sp.wait_ge(s["x_product"], x_use("out", NPAIR - 1, 1) + 1)
                ge_all(sp,
                       (s["y_biased" if by_pool else "y_copied"], k - 2 * GS + 1),
                       (s["slots"], 2))
                e = sp.value_load(eid[0:1, bass.ds(k, 1)], min_val=0, max_val=E - 1)
                sp.dma_start(wb[par * GS + i], t["experts"][e]).then_inc(expert_in[par * GS + i], 16)

            def rows(dram, g):
                b = 0 if isinstance(g, int) and g < NG // B else 1
                return dram[b][bass.ds((g - b * (NG // B)) * (GS * P), GS * P), :].rearrange("(t p) d -> p t d", p=P)

            def slots_in(g, par):
                ge_all(sp,
                       (s["slots_T"], GS * (g - 1)),
                       (scattered, 16 * TB * (g // (NG // B) + 1)),
                       (s["slots"], 2))
                sp.dma_start(xs[:, par, :, :], rows(xs_dram, g)).then_inc(group_in[par], 16)

            def store(g, par):
                if isinstance(g, int) and g < NA:
                    sp.wait_ge(s["y_biased"], GS * (g + 1))
                else:
                    ge_all(sp, (s["y_copied"], GS * (g + 1)), (s["slots"], 4))
                sp.dma_start(rows(ys_dram, g), ys[:, par, :, :]).then_inc(group_out[par], 16)

            def group(g, par, first=False):
                expert_data(g, par, 0)
                slots_in(g, par)
                expert_data(g, par, 1)
                expert_data(g, par, 2)
                if not first:
                    store(g - 2, par)

            sp.wait_ge(s["slots"], 2)
            for g in range(NG):
                if g == NG // B:
                    sp.wait_ge(s["slots"], 4)
                group(g, g % 2, g < 2)
            store(NG - 2, 0)
            store(NG - 1, 1)
            for g, (n0, n1) in enumerate(PARTS):
                sp.wait_ge(s["done"], g + 1)
                sp.dma_start(out[n0 * P:n1 * P, :].rearrange("(t p) d -> p t d", p=P),
                             x_sb[:, n0:n1, :]).then_inc(result_out, 16)
            sp.wait_ge(result_out, 16 * len(PARTS))


def tables():
    inv_freq = 1.0 / 10000.0 ** (np.arange(0, DH, 2, dtype=np.float32) / DH)
    freqs = np.outer(np.arange(S, dtype=np.float32), inv_freq)
    cos = np.concatenate([np.cos(freqs), np.cos(freqs)], -1)[:, ::2].T
    sin = np.concatenate([np.sin(freqs), np.sin(freqs)], -1)[:, ::2].T
    return (np.ascontiguousarray(np.concatenate([cos] * 4), dtype=np.float32),
            np.ascontiguousarray(np.concatenate([-sin, sin] * 2), dtype=np.float32))


def layout(i):
    def up(w):
        w = np.asarray(w).reshape(HP, 2, DH // 2, 2, LAT).transpose(0, 4, 1, 3, 2).reshape(HP, LAT, 2 * DH)
        return np.concatenate([w, w], 1)
    cos, sin = tables()
    f = lambda a: np.ascontiguousarray(np.asarray(a))
    return {
        "x": f(i["L0_attn_x"]).reshape(B * S, D),
        "c_t": f(np.asarray(i["L0_c"]).T),
        "wmod": f(i["L0_wmod"]),
        "wd": f(np.stack([np.concatenate([np.asarray(w)] * 2) for w in (i["L0_attn_w_down_q"], i["L0_attn_w_down_kv"])]
                         ).transpose(2, 0, 1)),
        "lns": f(np.stack([np.asarray(i["L0_attn_ln_scale"]), np.asarray(i["L0_attn_ln_bias"])], 1)),
        "wqk": f(np.stack([up(i["L0_attn_w_up_q"]), up(i["L0_attn_w_up_k"])], 2)),
        "cos": cos, "sin": sin,
        "wuv": f(np.asarray(i["L0_attn_w_up_v"]).reshape(H, DH, LAT).transpose(1, 0, 2)),
        "wo": f(np.asarray(i["L0_attn_w_out"]).T.reshape(H, DH, D).transpose(1, 0, 2)),
        "gate_w": f(i["L0_ffn_gate_w"]), "gate_b": f(i["L0_ffn_gate_b"]).reshape(1, E),
        "experts": f(np.concatenate([np.asarray(i["L0_ffn_w1"]),
                                     np.asarray(i["L0_ffn_w2"]).reshape(E, 4, P, D).transpose(0, 2, 1, 3).reshape(E, P, 4 * D),
                                     np.asarray(i["L0_ffn_b1"]).reshape(E, 4, P).transpose(0, 2, 1),
                                     np.broadcast_to(np.asarray(i["L0_ffn_b2"])[:, None, :], (E, P, D))], 2)),
    }


def kernel(**inputs):
    import concourse.bacc as bacc
    from concourse.bass_utils import run_bass_kernel_spmd

    nc = bacc.Bacc("TRN2", target_bir_lowering=False, num_devices=1)
    arrays = layout(inputs)
    aps = {n: nc.dram_tensor(f"in_{n}", a.shape, mybir.dt.from_np(a.dtype), kind="ExternalInput").ap()
           for n, a in arrays.items()}
    out = nc.dram_tensor("out_dram", [B * S, D], F32, kind="ExternalOutput").ap()
    build(nc, aps, out)
    r = run_bass_kernel_spmd(nc, [{f"in_{n}": a for n, a in arrays.items()}], core_ids=[0])
    return r.results[0]["out_dram"].reshape(B, S, D)
```
